# Optimizing a Trainium2 kernel written in Bass

```python
import numpy as np
import jax
import jax.numpy as jnp

def _softmax(x, axis=-1):
    return jax.nn.softmax(x, axis=axis)

def _gelu(x):
    return jax.nn.gelu(x, approximate=True)

def _silu(x):
    return jax.nn.silu(x)

def _sigmoid(x):
    return jax.nn.sigmoid(x)

def _layernorm(x, axis=-1, eps=1e-05):
    m = jnp.mean(x, axis=axis, keepdims=True)
    v = jnp.var(x, axis=axis, keepdims=True)
    return (x - m) / jnp.sqrt(v + eps)

def _scatter_add(tgt, idx, src, axis=0):
    return tgt.at[idx].add(src)

def _segment_sum(src, seg, n):
    return jax.ops.segment_sum(src, seg, n)
kernel_name = 'mk_metaformer_d4_conv_nchw256_r4_7f9c5d'

def setup_inputs(seed: int=0):
    np.random.seed(seed)
    _w = jnp.asarray

    def _rec_inputs():
        import jax
        import jax.numpy as jnp
        _gk = jax.random.key(seed)
        x = -0.000125 + 0.9999 * jax.random.normal(jax.random.fold_in(_gk, 1), (2, 64, 64, 64), jnp.float32)
        return x
    x = _rec_inputs()

    def _L0_conv_setup():
        import jax, jax.numpy as jnp
        import numpy as np
        B, N, D = (2, 64, 64)
        key = jax.random.key(seed)
        ks = jax.random.split(key, 9)
        s = 1.0 / np.sqrt(D)
        return {'pair_repr': jax.random.normal(ks[0], (B, N, N, D), dtype=jnp.float32), 'Wa': jax.random.uniform(ks[1], (D, D), jnp.float32, -s, s), 'ba': jax.random.uniform(ks[2], (D,), jnp.float32, -s, s), 'Wb': jax.random.uniform(ks[3], (D, D), jnp.float32, -s, s), 'bb': jax.random.uniform(ks[4], (D,), jnp.float32, -s, s), 'Wg': jax.random.uniform(ks[5], (D, D), jnp.float32, -s, s), 'bg': jax.random.uniform(ks[6], (D,), jnp.float32, -s, s), 'Wo': jax.random.uniform(ks[7], (D, D), jnp.float32, -s, s), 'bo': jax.random.uniform(ks[8], (D,), jnp.float32, -s, s)}
    _L0_conv_all = _L0_conv_setup()
    _L0_conv_in = {k: v for k, v in _L0_conv_all.items() if k in ('Wa', 'ba', 'Wb', 'bb', 'Wg', 'bg', 'Wo', 'bo')}
    del _L0_conv_all

    def _L0_ffn_setup():
        import jax, jax.numpy as jnp
        import numpy as np
        NUM_EXPERTS = 8
        TOP_K = 2
        B, S, D = (8, 2048, 64)

        def _moe(tokens, router_w, w1, b1, w2, b2):
            N = tokens.shape[0]
            E = router_w.shape[0]
            logits = tokens.astype(jnp.float32) @ router_w.astype(jnp.float32).T
            probs = jax.nn.softmax(logits, axis=-1)
            rw, re = jax.lax.top_k(probs, TOP_K)
            if TOP_K > 1:
                rw = rw / jnp.maximum(rw.sum(-1, keepdims=True), 1e-12)
            rw = rw.astype(tokens.dtype)
            combine = jnp.zeros((N, E), tokens.dtype).at[jnp.arange(N)[:, None], re].set(rw)
            out = tokens
            for e in range(E):
                h = jax.nn.gelu(tokens @ w1[e] + b1[e], approximate=False)
                y = h @ w2[e] + b2[e]
                out = out + combine[:, e:e + 1] * y
            return out
        key = jax.random.key(seed)
        ks = jax.random.split(key, 4)
        scale = 1.0 / np.sqrt(D).astype(np.float32)
        return {'input_embeddings': jax.random.normal(ks[0], (B, S, D), jnp.float32), 'router_w': jax.random.normal(ks[1], (NUM_EXPERTS, D), jnp.float32) * scale, 'w1': jax.random.normal(ks[2], (NUM_EXPERTS, D, D), jnp.float32) * scale, 'b1': jnp.zeros((NUM_EXPERTS, D), jnp.float32), 'w2': jax.random.normal(ks[3], (NUM_EXPERTS, D, D), jnp.float32) * scale, 'b2': jnp.zeros((NUM_EXPERTS, D), jnp.float32)}
    _L0_ffn_all = _L0_ffn_setup()
    _L0_ffn_in = {k: v for k, v in _L0_ffn_all.items() if k in ('router_w', 'w1', 'b1', 'w2', 'b2')}
    del _L0_ffn_all

    def _L1_conv_setup():
        import jax, jax.numpy as jnp
        import numpy as np
        K, S, P, BS = (3, 1, 1, 8)
        CIN, COUT = (64, 64)

        def _img2col(x, k, s, p):
            B, C, H, W = x.shape
            ho = (H + 2 * p - k) // s + 1
            wo = (W + 2 * p - k) // s + 1
            xp = jnp.pad(x, ((0, 0), (0, 0), (p, p), (p, p)))
            cols = [xp[:, :, i:i + s * ho:s, j:j + s * wo:s] for i in range(k) for j in range(k)]
            X = jnp.stack(cols, axis=1)
            return (X.reshape(B, k * k * C, ho * wo), ho, wo)
        key = jax.random.key(seed)
        k1, k2, k3 = jax.random.split(key, 3)
        x = jax.random.normal(k1, (8, CIN, 56, 56), dtype=jnp.float32)
        num_r = COUT // BS
        num_c = K * K * CIN // BS
        bound = float(np.sqrt(6.0 / (num_r + num_c)))
        w = jax.random.uniform(k2, (num_r, num_c, BS), dtype=jnp.float32, minval=-bound, maxval=bound)
        b = jax.random.normal(k3, (COUT,), dtype=jnp.float32) * 0.05
        return {'x': x, 'w': w, 'b': b}
    _L1_conv_all = _L1_conv_setup()
    _L1_conv_in = {k: v for k, v in _L1_conv_all.items() if k in ('w', 'b')}
    del _L1_conv_all

    def _L1_ffn_setup():
        import jax, jax.numpy as jnp
        import numpy as np
        B, N, D = (16, 1024, 64)
        NUM_EXPERTS, TOP_K, HEADS = (4, 2, 4)
        N_EDGES = 262144
        LN_EPS = 1e-05

        def _layernorm(x, g, b):
            mu = x.mean(-1, keepdims=True)
            var = ((x - mu) ** 2).mean(-1, keepdims=True)
            return (x - mu) * jax.lax.rsqrt(var + LN_EPS) * g + b

        def _forward(x, edge_index, W_gat, att_src, att_dst, b_gat, ln_gamma, ln_beta, W1, b1, W2, b2):
            Bc, Nc, Dc = x.shape
            M = Bc * Nc
            x_flat = x.reshape(M, Dc)
            h = (x_flat @ W_gat).reshape(M, HEADS, NUM_EXPERTS)
            loops = jnp.arange(M, dtype=edge_index.dtype)
            src = jnp.concatenate([edge_index[0], loops])
            dst = jnp.concatenate([edge_index[1], loops])
            a_src = (h * att_src).sum(-1)
            a_dst = (h * att_dst).sum(-1)
            e = jax.nn.leaky_relu(a_src[src] + a_dst[dst], negative_slope=0.2)
            e_max = jax.ops.segment_max(e, dst, num_segments=M)
            ee = jnp.exp(e - e_max[dst])
            denom = jax.ops.segment_sum(ee, dst, num_segments=M)
            alpha = ee / (denom[dst] + 1e-16)
            msg = h[src] * alpha[:, :, None]
            agg = jax.ops.segment_sum(msg, dst, num_segments=M).reshape(M, HEADS * NUM_EXPERTS) + b_gat
            scores = _layernorm(agg, ln_gamma, ln_beta).reshape(M, HEADS, NUM_EXPERTS).mean(1)
            scores = scores.reshape(Bc, Nc, NUM_EXPERTS)
            topk_s, topk_i = jax.lax.top_k(scores, TOP_K)
            w = jax.nn.softmax(topk_s, axis=-1)
            out = jnp.zeros_like(x)
            for ei in range(NUM_EXPERTS):
                g = jnp.where(topk_i == ei, w, 0.0).sum(-1)
                hh = jax.nn.gelu(x @ W1[ei] + b1[ei], approximate=False)
                out = out + g[..., None] * (hh @ W2[ei] + b2[ei])
            return out
        key = jax.random.key(seed)
        ks = jax.random.split(key, 8)
        s = 0.05
        return {'x': jax.random.normal(ks[0], (B, N, D), jnp.float32), 'W_gat': jax.random.normal(ks[1], (D, HEADS * NUM_EXPERTS), jnp.float32) * s, 'att_src': jax.random.normal(ks[2], (HEADS, NUM_EXPERTS), jnp.float32) * s, 'att_dst': jax.random.normal(ks[3], (HEADS, NUM_EXPERTS), jnp.float32) * s, 'b_gat': jnp.zeros((HEADS * NUM_EXPERTS,), jnp.float32), 'ln_gamma': jnp.ones((HEADS * NUM_EXPERTS,), jnp.float32), 'ln_beta': jnp.zeros((HEADS * NUM_EXPERTS,), jnp.float32), 'W1': jax.random.normal(ks[4], (NUM_EXPERTS, D, 2 * D), jnp.float32) * s, 'b1': jnp.zeros((NUM_EXPERTS, 2 * D), jnp.float32), 'W2': jax.random.normal(ks[5], (NUM_EXPERTS, 2 * D, D), jnp.float32) * s, 'b2': jnp.zeros((NUM_EXPERTS, D), jnp.float32), 'edge_index': jax.random.randint(ks[6], (2, N_EDGES), 0, B * N, jnp.int32)}
    _L1_ffn_all = _L1_ffn_setup()
    _L1_ffn_in = {k: v for k, v in _L1_ffn_all.items() if k in ('W_gat', 'att_src', 'att_dst', 'b_gat', 'ln_gamma', 'ln_beta', 'W1', 'b1', 'W2', 'b2', 'edge_index')}
    del _L1_ffn_all

    def _L2_conv_setup():
        import jax, jax.numpy as jnp
        import numpy as np
        from jax import lax
        EPS = 1e-05

        def _feature_map(t):
            t = jax.nn.relu(t) + EPS
            t = t * t
            n = jnp.sqrt(jnp.sum(t * t, axis=1, keepdims=True))
            return t / jnp.maximum(n, 1e-12)

        def _forward(x, qkv_w, qkv_b, dwc_w, dwc_b, norm_w, proj_w, proj_b):
            B, C, H, W = x.shape
            N = H * W
            d = norm_w.shape[0]
            qkv = jnp.einsum('bchw,oc->bohw', x, qkv_w) + qkv_b[None, :, None, None]
            qkv = qkv.reshape(B, 3 * d, N)
            q, k, v = jnp.split(qkv, 3, axis=1)
            q = _feature_map(q)
            k = _feature_map(k)
            scale = N ** (-0.5)
            kmean = jnp.mean(k, axis=2)
            z = jnp.einsum('bd,bdn->bn', kmean, q)[:, None, :] + EPS
            vkT = jnp.einsum('bin,bjn->bij', v * scale, k * scale)
            attn = jnp.einsum('bij,bjn->bin', vkT, q) / z
            rms = jnp.sqrt(jnp.mean(attn * attn, axis=1, keepdims=True) + EPS)
            attn = attn / rms * norm_w[None, :, None]
            attn = attn.reshape(B, d, H, W)
            v_img = v.reshape(B, d, H, W)
            dw = lax.conv_general_dilated(v_img, dwc_w, window_strides=(1, 1), padding='SAME', feature_group_count=d, dimension_numbers=('NCHW', 'OIHW', 'NCHW'))
            dw = dw + dwc_b[None, :, None, None]
            y = attn + dw
            return jnp.einsum('bdhw,cd->bchw', y, proj_w) + proj_b[None, :, None, None]
        key = jax.random.key(seed)
        ks = jax.random.split(key, 5)
        B, C, H, W = (16, 64, 16, 16)
        d, kk = (64, 5)
        x = jax.random.normal(ks[0], (B, C, H, W), jnp.float32)
        qkv_w = jax.random.normal(ks[1], (3 * d, C), jnp.float32) * 0.02
        qkv_b = jnp.zeros((3 * d,), jnp.float32)
        dwc_w = jax.random.normal(ks[2], (d, 1, kk, kk), jnp.float32) * 0.02
        dwc_b = jnp.zeros((d,), jnp.float32)
        norm_w = jnp.ones((d,), jnp.float32)
        proj_w = jax.random.normal(ks[3], (C, d), jnp.float32) * 0.02
        proj_b = jnp.zeros((C,), jnp.float32)
        return {'x': x, 'qkv_w': qkv_w, 'qkv_b': qkv_b, 'dwc_w': dwc_w, 'dwc_b': dwc_b, 'norm_w': norm_w, 'proj_w': proj_w, 'proj_b': proj_b}
    _L2_conv_all = _L2_conv_setup()
    _L2_conv_in = {k: v for k, v in _L2_conv_all.items() if k in ('qkv_w', 'qkv_b', 'dwc_w', 'dwc_b', 'norm_w', 'proj_w', 'proj_b')}
    del _L2_conv_all

    def _L2_ffn_setup():
        import jax, jax.numpy as jnp
        import numpy as np
        TOP_K = 2
        key = jax.random.key(seed)
        ks = jax.random.split(key, 4)
        B, L, D, H, E = (8, 1024, 64, 256, 8)
        s = 0.02
        return {'x': jax.random.normal(ks[0], (B, L, D), jnp.float32), 'Wg': jax.random.normal(ks[1], (D, E), jnp.float32) * s, 'bg': jnp.zeros((E,), jnp.float32), 'W1': jax.random.normal(ks[2], (E, D, H), jnp.float32) * s, 'b1': jnp.zeros((E, H), jnp.float32), 'W2': jax.random.normal(ks[3], (E, H, D), jnp.float32) * s, 'b2': jnp.zeros((E, D), jnp.float32)}
    _L2_ffn_all = _L2_ffn_setup()
    _L2_ffn_in = {k: v for k, v in _L2_ffn_all.items() if k in ('Wg', 'bg', 'W1', 'b1', 'W2', 'b2')}
    del _L2_ffn_all

    def _L3_conv_setup():
        import jax, jax.numpy as jnp
        import numpy as np
        DIM = 64
        K = 7
        G = 4
        CPG = DIM // G
        HID = DIM // 4
        PAD = K // 2
        key = jax.random.key(seed)
        ks = jax.random.split(key, 6)
        s = jnp.float32(0.05)
        return {'x': jax.random.normal(ks[0], (16, DIM, 16, 16), dtype=jnp.float32), 'dw_weight': jax.random.normal(ks[1], (DIM, 1, K, K), dtype=jnp.float32) * s, 'dk_w1': jax.random.normal(ks[2], (HID, DIM), dtype=jnp.float32) * s, 'dk_b1': jnp.zeros((HID,), jnp.float32), 'dk_w2': jax.random.normal(ks[3], (G * K * K, HID), dtype=jnp.float32) * s, 'dk_b2': jnp.zeros((G * K * K,), jnp.float32), 'cg_w1': jax.random.normal(ks[4], (HID, DIM), dtype=jnp.float32) * s, 'cg_b1': jnp.zeros((HID,), jnp.float32), 'cg_w2': jax.random.normal(ks[5], (DIM, HID), dtype=jnp.float32) * s, 'cg_b2': jnp.zeros((DIM,), jnp.float32)}
    _L3_conv_all = _L3_conv_setup()
    _L3_conv_in = {k: v for k, v in _L3_conv_all.items() if k in ('dw_weight', 'dk_w1', 'dk_b1', 'dk_w2', 'dk_b2', 'cg_w1', 'cg_b1', 'cg_w2', 'cg_b2')}
    del _L3_conv_all

    def _L3_ffn_setup():
        import jax, jax.numpy as jnp
        import numpy as np
        NUM_EXPERTS = 8
        TOP_K = 2
        B, S, D = (8, 2048, 64)

        def _moe(tokens, router_w, w1, b1, w2, b2):
            N = tokens.shape[0]
            E = router_w.shape[0]
            logits = tokens.astype(jnp.float32) @ router_w.astype(jnp.float32).T
            probs = jax.nn.softmax(logits, axis=-1)
            rw, re = jax.lax.top_k(probs, TOP_K)
            if TOP_K > 1:
                rw = rw / jnp.maximum(rw.sum(-1, keepdims=True), 1e-12)
            rw = rw.astype(tokens.dtype)
            combine = jnp.zeros((N, E), tokens.dtype).at[jnp.arange(N)[:, None], re].set(rw)
            out = tokens
            for e in range(E):
                h = jax.nn.gelu(tokens @ w1[e] + b1[e], approximate=False)
                y = h @ w2[e] + b2[e]
                out = out + combine[:, e:e + 1] * y
            return out
        key = jax.random.key(seed)
        ks = jax.random.split(key, 4)
        scale = 1.0 / np.sqrt(D).astype(np.float32)
        return {'input_embeddings': jax.random.normal(ks[0], (B, S, D), jnp.float32), 'router_w': jax.random.normal(ks[1], (NUM_EXPERTS, D), jnp.float32) * scale, 'w1': jax.random.normal(ks[2], (NUM_EXPERTS, D, D), jnp.float32) * scale, 'b1': jnp.zeros((NUM_EXPERTS, D), jnp.float32), 'w2': jax.random.normal(ks[3], (NUM_EXPERTS, D, D), jnp.float32) * scale, 'b2': jnp.zeros((NUM_EXPERTS, D), jnp.float32)}
    _L3_ffn_all = _L3_ffn_setup()
    _L3_ffn_in = {k: v for k, v in _L3_ffn_all.items() if k in ('router_w', 'w1', 'b1', 'w2', 'b2')}
    del _L3_ffn_all
    return {'x': x, 'L0_conv_Wa': _L0_conv_in['Wa'], 'L0_conv_ba': _L0_conv_in['ba'], 'L0_conv_Wb': _L0_conv_in['Wb'], 'L0_conv_bb': _L0_conv_in['bb'], 'L0_conv_Wg': _L0_conv_in['Wg'], 'L0_conv_bg': _L0_conv_in['bg'], 'L0_conv_Wo': _L0_conv_in['Wo'], 'L0_conv_bo': _L0_conv_in['bo'], 'L0_ffn_router_w': _L0_ffn_in['router_w'], 'L0_ffn_w1': _L0_ffn_in['w1'], 'L0_ffn_b1': _L0_ffn_in['b1'], 'L0_ffn_w2': _L0_ffn_in['w2'], 'L0_ffn_b2': _L0_ffn_in['b2'], 'L1_conv_w': _L1_conv_in['w'], 'L1_conv_b': _L1_conv_in['b'], 'L1_ffn_W_gat': _L1_ffn_in['W_gat'], 'L1_ffn_att_src': _L1_ffn_in['att_src'], 'L1_ffn_att_dst': _L1_ffn_in['att_dst'], 'L1_ffn_b_gat': _L1_ffn_in['b_gat'], 'L1_ffn_ln_gamma': _L1_ffn_in['ln_gamma'], 'L1_ffn_ln_beta': _L1_ffn_in['ln_beta'], 'L1_ffn_W1': _L1_ffn_in['W1'], 'L1_ffn_b1': _L1_ffn_in['b1'], 'L1_ffn_W2': _L1_ffn_in['W2'], 'L1_ffn_b2': _L1_ffn_in['b2'], 'L1_ffn_edge_index': _L1_ffn_in['edge_index'], 'L2_conv_qkv_w': _L2_conv_in['qkv_w'], 'L2_conv_qkv_b': _L2_conv_in['qkv_b'], 'L2_conv_dwc_w': _L2_conv_in['dwc_w'], 'L2_conv_dwc_b': _L2_conv_in['dwc_b'], 'L2_conv_norm_w': _L2_conv_in['norm_w'], 'L2_conv_proj_w': _L2_conv_in['proj_w'], 'L2_conv_proj_b': _L2_conv_in['proj_b'], 'L2_ffn_Wg': _L2_ffn_in['Wg'], 'L2_ffn_bg': _L2_ffn_in['bg'], 'L2_ffn_W1': _L2_ffn_in['W1'], 'L2_ffn_b1': _L2_ffn_in['b1'], 'L2_ffn_W2': _L2_ffn_in['W2'], 'L2_ffn_b2': _L2_ffn_in['b2'], 'L3_conv_dw_weight': _L3_conv_in['dw_weight'], 'L3_conv_dk_w1': _L3_conv_in['dk_w1'], 'L3_conv_dk_b1': _L3_conv_in['dk_b1'], 'L3_conv_dk_w2': _L3_conv_in['dk_w2'], 'L3_conv_dk_b2': _L3_conv_in['dk_b2'], 'L3_conv_cg_w1': _L3_conv_in['cg_w1'], 'L3_conv_cg_b1': _L3_conv_in['cg_b1'], 'L3_conv_cg_w2': _L3_conv_in['cg_w2'], 'L3_conv_cg_b2': _L3_conv_in['cg_b2'], 'L3_ffn_router_w': _L3_ffn_in['router_w'], 'L3_ffn_w1': _L3_ffn_in['w1'], 'L3_ffn_b1': _L3_ffn_in['b1'], 'L3_ffn_w2': _L3_ffn_in['w2'], 'L3_ffn_b2': _L3_ffn_in['b2']}

def reference(x, L0_conv_Wa, L0_conv_ba, L0_conv_Wb, L0_conv_bb, L0_conv_Wg, L0_conv_bg, L0_conv_Wo, L0_conv_bo, L0_ffn_router_w, L0_ffn_w1, L0_ffn_b1, L0_ffn_w2, L0_ffn_b2, L1_conv_w, L1_conv_b, L1_ffn_W_gat, L1_ffn_att_src, L1_ffn_att_dst, L1_ffn_b_gat, L1_ffn_ln_gamma, L1_ffn_ln_beta, L1_ffn_W1, L1_ffn_b1, L1_ffn_W2, L1_ffn_b2, L1_ffn_edge_index, L2_conv_qkv_w, L2_conv_qkv_b, L2_conv_dwc_w, L2_conv_dwc_b, L2_conv_norm_w, L2_conv_proj_w, L2_conv_proj_b, L2_ffn_Wg, L2_ffn_bg, L2_ffn_W1, L2_ffn_b1, L2_ffn_W2, L2_ffn_b2, L3_conv_dw_weight, L3_conv_dk_w1, L3_conv_dk_b1, L3_conv_dk_w2, L3_conv_dk_b2, L3_conv_cg_w1, L3_conv_cg_b1, L3_conv_cg_w2, L3_conv_cg_b2, L3_ffn_router_w, L3_ffn_w1, L3_ffn_b1, L3_ffn_w2, L3_ffn_b2):
    import jax
    import jax.numpy as jnp

    def _L0_conv_ref(pair_repr, Wa, ba, Wb, bb, Wg, bg, Wo, bo):
        import jax, jax.numpy as jnp
        import numpy as np
        B, N, D = (2, 64, 64)
        a = pair_repr @ Wa + ba
        b = pair_repr @ Wb + bb
        g = jax.nn.sigmoid(pair_repr @ Wg + bg)
        ab = jnp.einsum('bijk,bikl->bijl', a, b)
        return g * ab @ Wo + bo

    def _L0_ffn_ref(input_embeddings, router_w, w1, b1, w2, b2):
        import jax, jax.numpy as jnp
        import numpy as np
        NUM_EXPERTS = 8
        TOP_K = 2
        B, S, D = (8, 2048, 64)

        def _moe(tokens, router_w, w1, b1, w2, b2):
            N = tokens.shape[0]
            E = router_w.shape[0]
            logits = tokens.astype(jnp.float32) @ router_w.astype(jnp.float32).T
            probs = jax.nn.softmax(logits, axis=-1)
            rw, re = jax.lax.top_k(probs, TOP_K)
            if TOP_K > 1:
                rw = rw / jnp.maximum(rw.sum(-1, keepdims=True), 1e-12)
            rw = rw.astype(tokens.dtype)
            combine = jnp.zeros((N, E), tokens.dtype).at[jnp.arange(N)[:, None], re].set(rw)
            out = tokens
            for e in range(E):
                h = jax.nn.gelu(tokens @ w1[e] + b1[e], approximate=False)
                y = h @ w2[e] + b2[e]
                out = out + combine[:, e:e + 1] * y
            return out
        b, s, d = input_embeddings.shape
        tokens = input_embeddings.reshape(b * s, d)
        return _moe(tokens, router_w, w1, b1, w2, b2).reshape(b, s, d)

    def _L1_conv_ref(x, w, b):
        import jax, jax.numpy as jnp
        import numpy as np
        K, S, P, BS = (3, 1, 1, 8)
        CIN, COUT = (64, 64)

        def _img2col(x, k, s, p):
            B, C, H, W = x.shape
            ho = (H + 2 * p - k) // s + 1
            wo = (W + 2 * p - k) // s + 1
            xp = jnp.pad(x, ((0, 0), (0, 0), (p, p), (p, p)))
            cols = [xp[:, :, i:i + s * ho:s, j:j + s * wo:s] for i in range(k) for j in range(k)]
            X = jnp.stack(cols, axis=1)
            return (X.reshape(B, k * k * C, ho * wo), ho, wo)
        num_r, num_c, bs = w.shape
        X, ho, wo = _img2col(x, K, S, P)
        B, row, col = X.shape
        Xr = X.transpose(0, 2, 1).reshape(B * col, num_c, bs)
        xf = jnp.fft.rfft(Xr, axis=-1)
        wf = jnp.fft.rfft(w, axis=-1)
        res = jnp.einsum('mki,pki->mpi', xf, wf)
        z = jnp.fft.irfft(res, n=bs, axis=-1)
        out = z.reshape(B, col, num_r * bs).transpose(0, 2, 1)
        return out.reshape(B, num_r * bs, ho, wo) + b[None, :, None, None]

    def _L1_ffn_ref(x, W_gat, att_src, att_dst, b_gat, ln_gamma, ln_beta, W1, b1, W2, b2, edge_index):
        import jax, jax.numpy as jnp
        import numpy as np
        B, N, D = (16, 1024, 64)
        NUM_EXPERTS, TOP_K, HEADS = (4, 2, 4)
        N_EDGES = 262144
        LN_EPS = 1e-05

        def _layernorm(x, g, b):
            mu = x.mean(-1, keepdims=True)
            var = ((x - mu) ** 2).mean(-1, keepdims=True)
            return (x - mu) * jax.lax.rsqrt(var + LN_EPS) * g + b

        def _forward(x, edge_index, W_gat, att_src, att_dst, b_gat, ln_gamma, ln_beta, W1, b1, W2, b2):
            Bc, Nc, Dc = x.shape
            M = Bc * Nc
            x_flat = x.reshape(M, Dc)
            h = (x_flat @ W_gat).reshape(M, HEADS, NUM_EXPERTS)
            loops = jnp.arange(M, dtype=edge_index.dtype)
            src = jnp.concatenate([edge_index[0], loops])
            dst = jnp.concatenate([edge_index[1], loops])
            a_src = (h * att_src).sum(-1)
            a_dst = (h * att_dst).sum(-1)
            e = jax.nn.leaky_relu(a_src[src] + a_dst[dst], negative_slope=0.2)
            e_max = jax.ops.segment_max(e, dst, num_segments=M)
            ee = jnp.exp(e - e_max[dst])
            denom = jax.ops.segment_sum(ee, dst, num_segments=M)
            alpha = ee / (denom[dst] + 1e-16)
            msg = h[src] * alpha[:, :, None]
            agg = jax.ops.segment_sum(msg, dst, num_segments=M).reshape(M, HEADS * NUM_EXPERTS) + b_gat
            scores = _layernorm(agg, ln_gamma, ln_beta).reshape(M, HEADS, NUM_EXPERTS).mean(1)
            scores = scores.reshape(Bc, Nc, NUM_EXPERTS)
            topk_s, topk_i = jax.lax.top_k(scores, TOP_K)
            w = jax.nn.softmax(topk_s, axis=-1)
            out = jnp.zeros_like(x)
            for ei in range(NUM_EXPERTS):
                g = jnp.where(topk_i == ei, w, 0.0).sum(-1)
                hh = jax.nn.gelu(x @ W1[ei] + b1[ei], approximate=False)
                out = out + g[..., None] * (hh @ W2[ei] + b2[ei])
            return out
        return _forward(x, edge_index, W_gat, att_src, att_dst, b_gat, ln_gamma, ln_beta, W1, b1, W2, b2)

    def _L2_conv_ref(x, qkv_w, qkv_b, dwc_w, dwc_b, norm_w, proj_w, proj_b):
        import jax, jax.numpy as jnp
        import numpy as np
        from jax import lax
        EPS = 1e-05

        def _feature_map(t):
            t = jax.nn.relu(t) + EPS
            t = t * t
            n = jnp.sqrt(jnp.sum(t * t, axis=1, keepdims=True))
            return t / jnp.maximum(n, 1e-12)

        def _forward(x, qkv_w, qkv_b, dwc_w, dwc_b, norm_w, proj_w, proj_b):
            B, C, H, W = x.shape
            N = H * W
            d = norm_w.shape[0]
            qkv = jnp.einsum('bchw,oc->bohw', x, qkv_w) + qkv_b[None, :, None, None]
            qkv = qkv.reshape(B, 3 * d, N)
            q, k, v = jnp.split(qkv, 3, axis=1)
            q = _feature_map(q)
            k = _feature_map(k)
            scale = N ** (-0.5)
            kmean = jnp.mean(k, axis=2)
            z = jnp.einsum('bd,bdn->bn', kmean, q)[:, None, :] + EPS
            vkT = jnp.einsum('bin,bjn->bij', v * scale, k * scale)
            attn = jnp.einsum('bij,bjn->bin', vkT, q) / z
            rms = jnp.sqrt(jnp.mean(attn * attn, axis=1, keepdims=True) + EPS)
            attn = attn / rms * norm_w[None, :, None]
            attn = attn.reshape(B, d, H, W)
            v_img = v.reshape(B, d, H, W)
            dw = lax.conv_general_dilated(v_img, dwc_w, window_strides=(1, 1), padding='SAME', feature_group_count=d, dimension_numbers=('NCHW', 'OIHW', 'NCHW'))
            dw = dw + dwc_b[None, :, None, None]
            y = attn + dw
            return jnp.einsum('bdhw,cd->bchw', y, proj_w) + proj_b[None, :, None, None]
        return _forward(x, qkv_w, qkv_b, dwc_w, dwc_b, norm_w, proj_w, proj_b)

    def _L2_ffn_ref(x, Wg, bg, W1, b1, W2, b2):
        import jax, jax.numpy as jnp
        import numpy as np
        TOP_K = 2
        B, L, D = x.shape
        E = W1.shape[0]
        xf = x.reshape(-1, D)
        gate_logits = xf @ Wg + bg
        top_w, top_i = jax.lax.top_k(gate_logits, TOP_K)
        top_w = jax.nn.softmax(top_w, axis=-1)
        w_dense = jnp.sum(jax.nn.one_hot(top_i, E, dtype=xf.dtype) * top_w[..., None], axis=1)
        out = jnp.zeros_like(xf)
        for e in range(E):
            h = jax.nn.gelu(xf @ W1[e] + b1[e], approximate=False)
            out = out + w_dense[:, e:e + 1] * (h @ W2[e] + b2[e])
        return out.reshape(B, L, D)

    def _L3_conv_ref(x, dw_weight, dk_w1, dk_b1, dk_w2, dk_b2, cg_w1, cg_b1, cg_w2, cg_b2):
        import jax, jax.numpy as jnp
        import numpy as np
        DIM = 64
        K = 7
        G = 4
        CPG = DIM // G
        HID = DIM // 4
        PAD = K // 2
        B, C, H, W = x.shape
        pooled = x.mean(axis=(2, 3))
        h = jax.nn.gelu(pooled @ dk_w1.T + dk_b1, approximate=False)
        dyn = (h @ dk_w2.T + dk_b2).reshape(B, G, 1, K, K)
        base = dw_weight.reshape(1, G, CPG, K, K)
        fused = (base + dyn).reshape(B * C, 1, K, K)
        out = jax.lax.conv_general_dilated(x.reshape(1, B * C, H, W), fused, window_strides=(1, 1), padding=[(PAD, PAD), (PAD, PAD)], feature_group_count=B * C, dimension_numbers=('NCHW', 'OIHW', 'NCHW')).reshape(B, C, H, W)
        g = jax.nn.gelu(pooled @ cg_w1.T + cg_b1, approximate=False)
        gate = jax.nn.sigmoid(g @ cg_w2.T + cg_b2)
        return out * gate[:, :, None, None]

    def _L3_ffn_ref(input_embeddings, router_w, w1, b1, w2, b2):
        import jax, jax.numpy as jnp
        import numpy as np
        NUM_EXPERTS = 8
        TOP_K = 2
        B, S, D = (8, 2048, 64)

        def _moe(tokens, router_w, w1, b1, w2, b2):
            N = tokens.shape[0]
            E = router_w.shape[0]
            logits = tokens.astype(jnp.float32) @ router_w.astype(jnp.float32).T
            probs = jax.nn.softmax(logits, axis=-1)
            rw, re = jax.lax.top_k(probs, TOP_K)
            if TOP_K > 1:
                rw = rw / jnp.maximum(rw.sum(-1, keepdims=True), 1e-12)
            rw = rw.astype(tokens.dtype)
            combine = jnp.zeros((N, E), tokens.dtype).at[jnp.arange(N)[:, None], re].set(rw)
            out = tokens
            for e in range(E):
                h = jax.nn.gelu(tokens @ w1[e] + b1[e], approximate=False)
                y = h @ w2[e] + b2[e]
                out = out + combine[:, e:e + 1] * y
            return out
        b, s, d = input_embeddings.shape
        tokens = input_embeddings.reshape(b * s, d)
        return _moe(tokens, router_w, w1, b1, w2, b2).reshape(b, s, d)

    def _gn(v, G=32, eps=1e-05):
        B_, C_, H_, W_ = v.shape
        g = v.reshape(B_, G, C_ // G, H_, W_)
        m = jnp.mean(g, axis=(2, 3, 4), keepdims=True)
        s = jnp.var(g, axis=(2, 3, 4), keepdims=True)
        return ((g - m) / jnp.sqrt(s + eps)).reshape(v.shape)

    def _ln_c(v, eps=1e-06):
        m = jnp.mean(v, axis=1, keepdims=True)
        s = jnp.var(v, axis=1, keepdims=True)
        return (v - m) / jnp.sqrt(s + eps)

    def _ln_t(v, eps=1e-05):
        m = jnp.mean(v, axis=-1, keepdims=True)
        s = jnp.var(v, axis=-1, keepdims=True)
        return (v - m) / jnp.sqrt(s + eps)

    def _to_tokens(v):
        B_, C_, H_, W_ = v.shape
        return v.reshape(B_, C_, H_ * W_).transpose(0, 2, 1)

    def _from_tokens(t, like):
        B_, C_, H_, W_ = like.shape
        return t.transpose(0, 2, 1).reshape(B_, C_, H_, W_)
    x = x + _L0_conv_ref(_ln_c(x), L0_conv_Wa, L0_conv_ba, L0_conv_Wb, L0_conv_bb, L0_conv_Wg, L0_conv_bg, L0_conv_Wo, L0_conv_bo)
    t = _to_tokens(x)
    t = t + _L0_ffn_ref(_ln_t(t), L0_ffn_router_w, L0_ffn_w1, L0_ffn_b1, L0_ffn_w2, L0_ffn_b2)
    x = _from_tokens(t, x)
    x = x + _L1_conv_ref(_ln_c(x), L1_conv_w, L1_conv_b)
    t = _to_tokens(x)
    t = t + _L1_ffn_ref(_ln_t(t), L1_ffn_W_gat, L1_ffn_att_src, L1_ffn_att_dst, L1_ffn_b_gat, L1_ffn_ln_gamma, L1_ffn_ln_beta, L1_ffn_W1, L1_ffn_b1, L1_ffn_W2, L1_ffn_b2, L1_ffn_edge_index)
    x = _from_tokens(t, x)
    x = x + _L2_conv_ref(_ln_c(x), L2_conv_qkv_w, L2_conv_qkv_b, L2_conv_dwc_w, L2_conv_dwc_b, L2_conv_norm_w, L2_conv_proj_w, L2_conv_proj_b)
    t = _to_tokens(x)
    t = t + _L2_ffn_ref(_ln_t(t), L2_ffn_Wg, L2_ffn_bg, L2_ffn_W1, L2_ffn_b1, L2_ffn_W2, L2_ffn_b2)
    x = _from_tokens(t, x)
    x = x + _L3_conv_ref(_ln_c(x), L3_conv_dw_weight, L3_conv_dk_w1, L3_conv_dk_b1, L3_conv_dk_w2, L3_conv_dk_b2, L3_conv_cg_w1, L3_conv_cg_b1, L3_conv_cg_w2, L3_conv_cg_b2)
    t = _to_tokens(x)
    t = t + _L3_ffn_ref(_ln_t(t), L3_ffn_router_w, L3_ffn_w1, L3_ffn_b1, L3_ffn_w2, L3_ffn_b2)
    x = _from_tokens(t, x)
    return x

_drawn_inputs = setup_inputs


def setup_inputs(seed=0):
    import zlib

    import numpy as np

    out = dict(_drawn_inputs(seed))
    spreads = {'L0_ffn_b1': (0.0, 0.333),
     'L0_ffn_b2': (0.0, 0.1),
     'L1_ffn_b_gat': (0.0, 0.466),
     'L1_ffn_ln_gamma': (1.0, 0.6),
     'L1_ffn_ln_beta': (0.0, 0.8),
     'L1_ffn_b1': (0.0, 0.8),
     'L1_ffn_b2': (0.0, 0.4),
     'L2_conv_qkv_b': (0.0, 0.1),
     'L2_conv_dwc_b': (0.0, 0.8),
     'L2_conv_norm_w': (1.0, 0.6),
     'L2_conv_proj_b': (0.0, 0.318),
     'L2_ffn_bg': (0.0, 0.497),
     'L2_ffn_b1': (0.0, 0.8),
     'L2_ffn_b2': (0.0, 0.419),
     'L3_conv_dk_b1': (0.0, 0.762),
     'L3_conv_dk_b2': (0.0, 0.1),
     'L3_conv_cg_b1': (0.0, 0.8),
     'L3_conv_cg_b2': (0.0, 0.8),
     'L3_ffn_b1': (0.0, 0.8),
     'L3_ffn_b2': (0.0, 0.589)}
    factors = {'L0_conv_bo': 4.554,
     'L1_conv_b': 4.323,
     'L1_ffn_W_gat': 4.016,
     'L1_ffn_att_src': 8.0,
     'L1_ffn_att_dst': 8.0,
     'L2_conv_qkv_w': 8.0,
     'L2_conv_dwc_w': 8.0,
     'L2_ffn_Wg': 3.786,
     'L2_ffn_W1': 8.0,
     'L2_ffn_W2': 8.0,
     'L3_conv_dk_w1': 8.0,
     'L3_conv_dk_w2': 6.266,
     'L3_conv_cg_w1': 8.0,
     'L3_conv_cg_w2': 8.0}
    for name, (base, spread) in spreads.items():
        noise = np.random.default_rng([zlib.crc32(name.encode()), seed]).standard_normal(out[name].shape)
        drawn = base * np.exp(spread * noise) if base else spread * noise
        out[name] = jnp.asarray(drawn.astype(out[name].dtype))
    for name, factor in factors.items():
        out[name] = (out[name] * factor).astype(out[name].dtype)
    return out
```

```python
from contextlib import ExitStack

import concourse.bass as bass
from concourse import mybir

F32 = mybir.dt.float32
I32 = mybir.dt.int32
BF16 = mybir.dt.bfloat16
ALU = mybir.AluOpType
ACT = mybir.ActivationFunctionType
AX = mybir.AxisListType.X

P = 128
B, C, IMG = 2, 64, 64
TOK = B * IMG * IMG
NT = TOK // P
TPB = NT // B
NEG = -1.0e30
EDGES = 262144
EPP = EDGES // P
GROUP = 32
NG = EPP // GROUP
SUB = 8
NSUB = EPP // SUB
WIN = 64
NW = EPP // WIN
HEADS, GE = 4, 4
ROW = HEADS * GE + HEADS
ACC = ROW + HEADS


def program(nc, d, out, scratch, stages):
    with ExitStack() as ctx:
        def sb(name, shape, dt=F32, c=ctx):
            return c.enter_context(nc.sbuf_tensor(name, shape, dt))

        def sem(name):
            return ctx.enter_context(nc.semaphore(name))

        bank = [ctx.enter_context(nc.psum_tensor(f"bank{i}", [P, 512], F32)) for i in range(8)]

        x_tok = sb("x_tok", [P, NT, C])
        n_tok = sb("n_tok", [P, NT, C])
        n_chan = sb("n_chan", [C, TOK])
        ident = sb("ident", [P, P])
        ident2 = sb("ident2", [P, C])
        ones_f = sb("ones_f", [P, P])
        ones_b = sb("ones_b", [P, P], BF16)
        gates = sb("gates", [P, NT, 8])
        order8 = sb("order8", [P, 8])
        order4 = sb("order4", [P, 4])
        mean = sb("mean", [P, NT])
        var = sb("var", [P, NT])
        seg_base = sb("seg_base", [P, NT])
        seg_size = sb("seg_size", [P, NT])
        gsel = sb("gsel", [P, 4])

        W = {}
        wsize = 4700
        wmem = [sb("weights_even", [P, wsize]), sb("weights_odd", [P, wsize])]
        wpos = [0, 0]

        def wt(stage, name, shape, dt=F32):
            n = 1
            for s in shape[1:]:
                n *= s
            words = n if dt is F32 else (n + 1) // 2
            r = stage % 2
            at = wpos[r]
            wpos[r] += words
            assert wpos[r] <= wsize, (stage, name, wpos[r])
            ap = wmem[r][0:shape[0], at:at + words]
            if dt is not F32:
                ap = ap.bitcast(dt)
            if len(shape) == 3:
                ap = ap.rearrange("p (a b) -> p a b", b=shape[2])
            if len(shape) == 4:
                ap = ap.rearrange("p (a b c) -> p a b c", b=shape[2], c=shape[3])
            W[stage, name] = ap
            return ap

        def bcast_row(ap, n=P):
            return ap.rearrange("(o n) -> o n", o=1).broadcast_to([n, ap.shape[0]])

        loads = {}

        def load(stage, dst, src):
            loads.setdefault(stage, []).append((dst, src))

        FFN = {1: (8, 64, "L0_ffn"), 3: (4, 128, "L1_ffn"), 5: (8, 256, "L2_ffn"), 7: (8, 64, "L3_ffn")}
        for s in range(8):
            wpos[s % 2] = 0
            if s == 0:
                for n in ("Wa", "Wb", "Wg", "Wo"):
                    load(s, wt(s, n, [C, C]), d["L0_conv_" + n])
                for n in ("ba", "bg"):
                    load(s, wt(s, n, [C, 1]), d["L0_conv_" + n].rearrange("(p o) -> p o", o=1))
                bo = wt(s, "bo", [P, 1])
                for h in range(2):
                    load(s, bo[h * C:(h + 1) * C], d["L0_conv_bo"].rearrange("(p o) -> p o", o=1))
                load(s, wt(s, "bb", [C, C]), bcast_row(d["L0_conv_bb"], C))
            if s in FFN:
                E, HD, nm = FFN[s]
                NH = E * HD // P
                w1 = wt(s, "w1", [C, E, HD])
                load(s, w1, d[nm + "_w1"].rearrange("e c h -> c e h"))
                load(s, wt(s, "b1", [P, NH]), d[nm + "_b1"])
                if HD == 64:
                    load(s, wt(s, "w2", [P, NH, P]), d[nm + "_w2"].rearrange("k h c -> h k c"))
                else:
                    w2 = wt(s, "w2", [P, NH, C])
                    load(s, w2, d[nm + "_w2"].rearrange("e (a h) c -> h (e a) c", h=P))
                load(s, wt(s, "b2", [P, E * C]), d[nm + "_b2"])
                wt(s, "b2_parts", [P, 4, E * C], BF16)
                if s != 3:
                    load(s, wt(s, "router", [C, E]), d[nm + "_router"])
                if s == 5:
                    load(s, wt(s, "bg", [P, E]), bcast_row(d["L2_ffn_bg"]))
                if s == 3:
                    load(s, wt(s, "w_gat", [C, 16]), d["L1_ffn_W_gat"])
                    for n in ("att_src", "att_dst", "b_gat", "ln_gamma", "ln_beta"):
                        load(s, wt(s, n, [P, 16]), bcast_row(d["L1_ffn_" + n]))
            if s == 2:
                load(s, wt(s, "conv", [P, 6, C]), d["L1_conv_wk"])
                load(s, wt(s, "b", [P, C]), bcast_row(d["L1_conv_b"]))
            if s == 4:
                load(s, wt(s, "qkv", [C, 192]), d["L2_qkv_wT"])
                load(s, wt(s, "qkv_b", [P, 192]), bcast_row(d["L2_conv_qkv_b"]))
                load(s, wt(s, "norm_w", [P, C]), bcast_row(d["L2_conv_norm_w"]))
                load(s, wt(s, "proj_b", [P, C]), bcast_row(d["L2_conv_proj_b"]))
                pj = wt(s, "proj", [P, C])
                dw = wt(s, "dwc", [P, 15])
                load(s, dw, d["L2_dwc_taps"])
                for h in range(2):
                    load(s, pj[h * C:(h + 1) * C], d["L2_proj_wT"])
                load(s, wt(s, "dwc_b", [C, 1]), d["L2_conv_dwc_b"].rearrange("(p o) -> p o", o=1))
                wt(s, "conv", [P, 15, C])
            if s == 6:
                load(s, wt(s, "dw", [P, 28]), d["L3_dw_taps"])
                load(s, wt(s, "dk_w1", [C, 16]), d["L3_dk_w1T"])
                load(s, wt(s, "dk_w2", [16, 4 * 56]), d["L3_dk_w2T"])
                load(s, wt(s, "cg_w1", [C, 16]), d["L3_cg_w1T"])
                load(s, wt(s, "cg_w2", [16, C]), d["L3_cg_w2T"])
                for n in ("dk_b1", "cg_b1"):
                    load(s, wt(s, n, [16, 1]), d["L3_conv_" + n].rearrange("(p o) -> p o", o=1))
                load(s, wt(s, "dk_b2", [P, 4 * 56]), bcast_row(d["L3_dk_b2p"]))
                cb = wt(s, "cg_b2", [P, 1])
                for h in range(2):
                    load(s, cb[h * C:(h + 1) * C], d["L3_conv_cg_b2"].rearrange("(p o) -> p o", o=1))

        def region():
            return ExitStack()

        packed = sb("packed", [P, EPP], I32)
        pos_all = sb("pos_all", [P, EPP], I32)
        packed_ring = sb("packed_ring", [P, 2, GROUP], I32)
        pos_ring = sb("pos_ring", [P, 2, GROUP], I32)
        with region() as r:
            edge_i = sb("edge_i", [P, 2, EPP], I32, r)
            bits_i = sb("bits_i", [P, 2, EPP], I32, r)
            low_high = sb("low_high", [P, NG, 2, GROUP], BF16, r)
            ring = sb("ring", [P, 2, 2, GROUP], BF16, r)
            ring_low = sb("ring_low", [P, 2, GROUP], F32, r)
            onehot_lo = sb("onehot_lo", [P, 2, P, SUB], BF16, r)
            onehot_hi = sb("onehot_hi", [P, 2, NT, SUB], BF16, r)
            lo_on_part = sb("lo_on_part", [P, 2, SUB, P], F32, r)
            same_before = sb("same_before", [P, 2, SUB, P], BF16, r)
            lo_rows = sb("lo_rows", [GROUP, 2, P], BF16, r)
            sel = sb("sel", [GROUP, GROUP, P], BF16, r)
            tri = sb("tri", [P, P], BF16, r)
            tri_f = sb("tri_f", [P, P], F32, r)
            iota = sb("iota", [P, P, SUB], BF16, r)
            iota_p = sb("iota_p", [P, 1], F32, r)
            hist = sb("hist", [P, 2, NT], F32, r)
            cums = sb("cums", [P, NT], F32, r)
            junk = sb("junk", [P, 4, NT], F32, r)
            rank = sb("rank", [P, 2, GROUP], F32, r)
            dropped = sb("dropped", [P, GROUP], F32, r)
        with region() as r:
            hsq = sb("hsq", [P, NT, C], F32, r)
        with region() as r:
            a_k = sb("a_k", [C, TOK], F32, r)
            g_l = sb("g_l", [C, TOK], F32, r)
            b_h = sb("b_h", [C, C, C], F32, r)
        with region() as r:
            hid = sb("hid", [P, 2, 16, 512], F32, r)
            prod = sb("prod", [P, 2, 512], F32, r)
            y_sum = sb("y_sum", [P, 2, 4, C], F32, r)
            gt = [sb(f"gt{i}", [P, NT * 8], F32, r) for i in range(6)]
            gs = [sb(f"gs{i}", [P, NT], F32, r) for i in range(4)]
            b2_rest = sb("b2_rest", [P, 512], F32, r)
        with region() as r:
            image = sb("image", [P, 4 * 70 * IMG], F32, r)
            diag = sb("diag", [P, B, 28, C], F32, r)
            pooled = sb("pooled", [C, B], F32, r)
            hid16 = sb("hid16", [16, 2, B], F32, r)
            hid_rep = sb("hid_rep", [16, B, P], F32, r)
            fused = sb("fused", [P, B, 28], F32, r)
            dyn = packed[:, 0:B * 4 * 28].bitcast(F32).rearrange("p (b n) -> p b n", b=B)
            gate3 = packed[:, B * 4 * 28:B * 4 * 28 + B].bitcast(F32)
        with region() as r:
            sb("image_l2", [P, 3 * 68 * IMG], F32, r)
            v_tok = sb("v_tok", [P, NT, C + 1], F32, r)
            k_tok = sb("k_tok", [P, NT, C], F32, r)
            kv = sb("kv", [C, B, C + 1], F32, r)
            zrec = sb("zrec", [P, NT], F32, r)
            ssq = sb("ssq", [P, 2, NT], F32, r)
            att_c = pos_all[0:C, 0:1024].bitcast(F32).rearrange("p (s n) -> p s n", s=2)
        with region() as r:
            src_i = sb("src_i", [P, EPP + 2 * WIN], I32, r)
            same = pos_all[:, :].bitcast(F32)
            a_dst_e = sb("a_dst_e", [P, EPP, HEADS], F32, r)
            idx_ring = sb("idx_ring", [P, 2, WIN], I32, r)
            rows = sb("rows", [P, 2, WIN, ROW], F32, r)
            h_tok = sb("h_tok", [P, NT, ROW], F32, r)
            a_dst = sb("a_dst", [P, NT, HEADS], F32, r)
            has = sb("has", [P, NT], F32, r)
            start_f = sb("start_f", [P, NT], F32, r)
            start_i = sb("start_i", [P, NT], I32, r)
            end_i = sb("end_i", [P, NT], I32, r)
            part_i = sb("part_i", [P, NT], I32, r)
            part_f = sb("part_f", [P, NT], F32, r)
            cont = sb("cont", [P, NT], F32, r)
            first_i = sb("first_i", [P, 1], I32, r)
            first_f = sb("first_f", [P, 1], F32, r)
            prev_edge = sb("prev_edge", [P, 2], I32, r)
            prev_dst = sb("prev_dst", [P, 2], F32, r)
            sb("gap", [P, 1], F32, r)
            join = sb("join", [P, 2], F32, r)
            last = sb("last", [P, 3, ROW], F32, r)
            last_t = sb("last_t", [ROW, 8, P + 1], F32, r)
            carry = sb("carry", [P, ACC], F32, r)
            with region() as q:
                sorted_e = sb("sorted_e", [P, EPP], I32, q)
                dst_f = sb("dst_f", [P, EPP], F32, q)
                dst_i = packed[:, :]
            with region() as q:
                z = sb("z", [P, WIN, HEADS], F32, q)
                e4 = sb("e4", [P, HEADS, WIN], F32, q)
                restart = sb("restart", [P, WIN], F32, q)
                runmax = sb("runmax", [P, 2, HEADS, WIN + 1], F32, q)
                expo = sb("expo", [P, 2, HEADS, WIN], F32, q)
                scale = sb("scale", [P, 2, 2, HEADS, WIN], F32, q)
                msg = packed[:, 0:HEADS * GE * WIN].bitcast(F32).rearrange("p (h e w) -> p h e w", h=HEADS, e=GE)
                sums = sb("sums", [P, 2, WIN, ACC], F32, q)
        with region() as r:
            sb("keep_clear", [P, EPP + 2 * WIN], F32, r)
            tok_end = sb("tok_end", [P, NT, ACC], F32, r)
            tok_carry = sb("tok_carry", [P, NT, ACC], F32, r)
            m_all = sb("m_all", [P, NT, HEADS], F32, r)
            e_self = sb("e_self", [P, NT, HEADS], F32, r)
            wgt = sb("wgt", [P, 3, NT, HEADS], F32, r)
            agg = sb("agg", [P, NT, ROW], F32, r)
            tmp = sb("tmp", [P, NT, ROW], F32, r)
            sc1 = sb("sc1", [P, NT], F32, r)
            sc2 = sb("sc2", [P, NT], F32, r)

        sems = {}

        def S(name):
            if name not in sems:
                sems[name] = sem(name)
            return sems[name]

        s_sc = [sem("s_scattered0"), sem("s_scattered1")]
        s_gath = [sem("s_gathered0"), sem("s_gathered1")]
        s_yout = [sem("s_sums_out0"), sem("s_sums_out1")]
        H = bank[0][:, 0:NT]
        sorted_d, start_d, row_d, adst_d, sums_d, carry_d = (scratch[n] for n in ("sorted", "start", "row", "adst", "sums", "carry"))
        n_w = n_chan[:, :].rearrange("w (t p c) -> w t p c", p=2, c=C)
        MIXERS = (0, 2, 4, 6)
        last_stage = max(stages)

        def steps(st, name):
            if name in ("normed", "centred", "squared", "var", "std"):
                return 4
            if name in ("chan", "chan_t"):
                return 16 if st else 0
            if name in ("conv", "conv_used", "img0", "img1"):
                return 8 if st in (2, 4, 6) else 0
            if name == "img_zero":
                return int(st in (2, 4, 6))
            if st not in FFN:
                return 0
            if name in ("up", "hid"):
                return 16 * FFN[st][0] * FFN[st][1] // P
            if name in ("down", "gated"):
                return NT
            if name == "router":
                return int(st != 3)
            return int(name in ("b2", "gate_in", "gate_exp"))

        def at(st, name):
            return sum(steps(e, name) for e in stages if e < st)

        def done(st):
            return S("stage_done"), stages.index(st) + 1

        def ln_vector(v, link, st):
            eps = 1e-6 if st in MIXERS else 1e-5
            Q = 16
            for q in range(4):
                x, m = x_tok[:, q * Q:(q + 1) * Q, :], mean[:, q * Q:(q + 1) * Q]
                link(v.tensor_reduce(m, x, AX, ALU.add))
                link(v.tensor_scalar(m, m, 1.0 / C, None, ALU.mult))
                link(v.tensor_tensor(n_tok[:, q * Q:(q + 1) * Q, :], x, m.unsqueeze(2).broadcast_to([P, Q, C]), ALU.subtract))
                v.sem_inc(S("centred"), 1)
            for q in range(4):
                m = var[:, q * Q:(q + 1) * Q]
                v.wait_ge(S("squared"), at(st, "squared") + q + 1)
                link(v.tensor_reduce(m, hsq[:, q * Q:(q + 1) * Q, :], AX, ALU.add))
                link(v.tensor_scalar(m, m, 1.0 / C, eps, ALU.mult, ALU.add))
                v.sem_inc(S("var"), 1)
            for q in range(4):
                m = var[:, q * Q:(q + 1) * Q]
                n = n_tok[:, q * Q:(q + 1) * Q, :]
                v.wait_ge(S("std"), at(st, "std") + q + 1)
                link(v.reciprocal(m, m))
                v.tensor_tensor(n, n, m.unsqueeze(2).broadcast_to([P, Q, C]), ALU.mult).then_inc(S("normed"), 1)

        def ln_scalar(a, st):
            Q = 16
            for q in range(4):
                a.wait_ge(S("centred"), at(st, "centred") + q + 1)
                nc.scalar.activation(hsq[:, q * Q:(q + 1) * Q, :], n_tok[:, q * Q:(q + 1) * Q, :], ACT.Square).then_inc(S("squared"), 1)
            for q in range(4):
                a.wait_ge(S("var"), at(st, "var") + q + 1)
                m = var[:, q * Q:(q + 1) * Q]
                nc.scalar.activation(m, m, ACT.Sqrt).then_inc(S("std"), 1)

        def channels_tensor(pe, st, src=None, kind="chan"):
            src = n_tok if src is None else src
            for g in range(NT // 4):
                if g % 4 == 0 and kind == "chan":
                    pe.wait_ge(S("normed"), at(st, "normed") + g // 4 + 1)
                if g >= 2:
                    pe.wait_ge(S(kind), at(st, kind) + g - 1)
                for t in range(4):
                    m = nc.tensor.transpose(bank[6 + g % 2][0:C, t * P:(t + 1) * P], src[:, 4 * g + t, :], ident[:, :])
                m.then_inc(S(kind + "_t"), 1)

        def channels_scalar(a, st, kind="chan", bias=None):
            for g in range(NT // 4):
                a.wait_ge(S(kind + "_t"), at(st, kind + "_t") + g + 1)
                dst, src = n_chan[:, g * 512:(g + 1) * 512], bank[6 + g % 2][0:C, :]
                m = nc.scalar.copy(dst, src) if bias is None else nc.scalar.activation(dst, src, ACT.Identity, bias=bias)
                m.then_inc(S(kind), 1)

        def ffn_tensor(pe, st):
            E, HD, _ = FFN[st]
            NH = E * HD // P
            cols = E * C
            w1 = W[st, "w1"].rearrange("p e h -> p (e h)")
            pe.wait_ge(S(f"s{st}_weights"), 16 * len(loads[st]))
            if st != 3:
                for t in range(NT):
                    if t % 4 == 0:
                        pe.wait_ge(S("chan"), at(st, "chan") + t // 4 + 1)
                    m = nc.tensor.matmul(bank[5][:, t * E:(t + 1) * E], n_chan[:, t * P:(t + 1) * P], W[st, "router"], start=True, stop=True)
                m.then_inc(S("router"), 1)

            def up(n):
                pe.wait_ge(S("chan"), at(st, "chan") + n + 1)
                for k in range(NH):
                    i = n * NH + k
                    if i >= 3:
                        pe.wait_ge(S("hid"), at(st, "hid") + i - 2)
                    nc.tensor.matmul(bank[i % 3][:, :], w1[:, k * P:(k + 1) * P], n_chan[:, n * 512:(n + 1) * 512],
                                     start=True, stop=True).then_inc(S("up"), 1)

            def down(n):
                pe.wait_ge(S("hid"), at(st, "hid") + (n + 1) * NH)
                for t in range(4):
                    T = 4 * n + t
                    y = bank[3 + T % 2]
                    if T >= 2:
                        pe.wait_ge(S("gated"), at(st, "gated") + T - 1)
                    nc.tensor.matmul(y[:, 0:cols], ones_b[:, :], W[st, "b2_parts"][:, 3, :], start=True, stop=False, skip_group_check=True)
                    for k in range(NH):
                        lhs = hid[:, n % 2, k, t * P:(t + 1) * P]
                        if HD == 64:
                            o = y[:, k * P:(k + 1) * P]
                        else:
                            e = k * P // HD
                            o = y[:, e * C:(e + 1) * C]
                        m = nc.tensor.matmul(o, lhs, W[st, "w2"][:, k, :], start=False, stop=(k == NH - 1), skip_group_check=True)
                    m.then_inc(S("down"), 1)

            pe.wait_ge(S("b2"), at(st, "b2") + 1)
            for n in range(17):
                if n < 16:
                    up(n)
                if n >= 1:
                    down(n - 1)

        def ffn_scalar(a, st):
            E, HD, _ = FFN[st]
            NH = E * HD // P
            a.wait_ge(S(f"s{st}_weights"), 16 * len(loads[st]))
            gate_scalar(a, st)
            for n in range(16):
                if n >= 2:
                    a.wait_ge(S("down"), at(st, "down") + 4 * (n - 1))
                for k in range(NH):
                    i = n * NH + k
                    a.wait_ge(S("up"), at(st, "up") + i + 1)
                    nc.scalar.activation(hid[:, n % 2, k, :], bank[i % 3][:, :], ACT.Gelu,
                                         bias=W[st, "b1"][:, k:k + 1]).then_inc(S("hid"), 1)

        def top2(v, link, E, values, order, mask, m1, m2, eq, rest):
            def bc(m):
                return m.unsqueeze(2).broadcast_to([P, NT, E])
            cur = values
            for i, m in enumerate((m1, m2)):
                link(v.tensor_reduce(m, cur, AX, ALU.max))
                link(v.tensor_tensor(eq, cur, bc(m), ALU.is_equal))
                link(v.tensor_tensor(eq, eq, order, ALU.mult))
                link(v.tensor_reduce(gs[3][:, :], eq, AX, ALU.max))
                if i == 0:
                    link(v.tensor_tensor(mask, eq, bc(gs[3][:, :]), ALU.is_equal))
                    link(v.scalar_tensor_tensor(rest, mask, 2 * NEG, cur, ALU.mult, ALU.add))
                    cur = rest
                else:
                    link(v.tensor_tensor(eq, eq, bc(gs[3][:, :]), ALU.is_equal))
                    link(v.tensor_tensor(mask, mask, eq, ALU.add))

        def gate_vector(v, link, st):
            E = FFN[st][0]
            n = NT * E
            val, ex, eq, rest, mask = (g[:, 0:n].rearrange("p (t e) -> p t e", e=E) for g in gt[:5])
            G = gates[:, :, 0:E]
            order = (order8 if E == 8 else order4)[:, :].unsqueeze(1).broadcast_to([P, NT, E])

            def bc(m):
                return m.unsqueeze(2).broadcast_to([P, NT, E])
            m1, m2, m3 = gs[0][:, :], gs[1][:, :], gs[2][:, :]
            logits = bank[5][:, 0:n].rearrange("p (t e) -> p t e", e=E)
            if st in (1, 7):
                v.wait_ge(S("router"), at(st, "router") + 1)
                link(v.tensor_reduce(m1, logits, AX, ALU.max))
                link(v.tensor_tensor(ex, logits, bc(m1), ALU.subtract))
                v.sem_inc(S("gate_in"), 1)
                v.wait_ge(S("gate_exp"), at(st, "gate_exp") + 1)
                link(v.tensor_reduce(m1, ex, AX, ALU.add))
                link(v.reciprocal(m1, m1))
                link(v.tensor_tensor(val, ex, bc(m1), ALU.mult))
                top2(v, link, E, val, order, mask, m1, m2, eq, rest)
                link(v.tensor_tensor(m3, m1, m2, ALU.add))
                link(v.tensor_scalar(m3, m3, 1e-12, None, ALU.max))
                link(v.reciprocal(m3, m3))
                link(v.tensor_tensor(val, val, mask, ALU.mult))
                link(v.tensor_tensor(G, val, bc(m3), ALU.mult))
                return
            if st == 5:
                v.wait_ge(S("router"), at(st, "router") + 1)
                link(v.tensor_tensor(val, logits, W[st, "bg"].unsqueeze(1).broadcast_to([P, NT, E]), ALU.add))
            top2(v, link, E, val, order, mask, m1, m2, eq, rest)
            link(v.tensor_tensor(ex, val, bc(m1), ALU.subtract))
            v.sem_inc(S("gate_in"), 1)
            v.wait_ge(S("gate_exp"), at(st, "gate_exp") + 1)
            link(v.tensor_tensor(ex, ex, mask, ALU.mult))
            link(v.tensor_reduce(m3, ex, AX, ALU.add))
            link(v.reciprocal(m3, m3))
            link(v.tensor_tensor(G, ex, bc(m3), ALU.mult))

        def gate_scalar(a, st):
            E = FFN[st][0]
            ex = gt[1][:, 0:NT * E]
            a.wait_ge(S("gate_in"), at(st, "gate_in") + 1)
            nc.scalar.activation(ex, ex, ACT.Exp).then_inc(S("gate_exp"), 1)

        def ffn_b2(v, link, st):
            b2, parts = W[st, "b2"], W[st, "b2_parts"]
            n = b2.shape[1]
            rest = b2_rest[:, 0:n]
            v.wait_ge(S(f"s{st}_weights"), 16 * len(loads[st]))
            link(v.tensor_copy(parts[:, 0, :], b2))
            link(v.tensor_tensor(rest, b2, parts[:, 0, :], ALU.subtract))
            link(v.tensor_copy(parts[:, 1, :], rest))
            link(v.tensor_tensor(rest, rest, parts[:, 1, :], ALU.subtract))
            link(v.tensor_copy(parts[:, 2, :], rest))
            link(v.memset(parts[:, 3, :], 0.0))
            for i in range(3):
                link(v.tensor_copy(parts[32 * i:32 * i + 32, 3, :], parts[32 * i:32 * i + 32, i, :]))
            v.sem_inc(S("b2"), 1)

        def ffn_vector(v, link, st):
            E, HD, _ = FFN[st]
            cols = E * C
            ffn_b2(v, link, st)
            gate_vector(v, link, st)
            if st in (1, 7):
                link(v.tensor_tensor(x_tok[:, :, :], x_tok[:, :, :], n_tok[:, :, :], ALU.add))
            for T in range(NT):
                v.wait_ge(S("down"), at(st, "down") + T + 1)
                p = prod[:, T % 2, 0:cols]
                v.tensor_tensor(p.rearrange("p (e c) -> p e c", c=C), bank[3 + T % 2][:, 0:cols].rearrange("p (e c) -> p e c", c=C),
                                gates[:, T, 0:E].unsqueeze(2).broadcast_to([P, E, C]), ALU.mult).then_inc(S("gated"), 1)
                v.wait_ge(S("gated"), at(st, "gated") + T + 1)
                link(v.tensor_reduce(y_sum[:, (T // 4) % 2, T % 4, :], p.rearrange("p (e c) -> p c e", c=C), AX, ALU.add))
                if T % 4 == 3:
                    x = x_tok[:, T - 3:T + 1, :]
                    link(v.tensor_tensor(x, x, y_sum[:, (T // 4) % 2, :, :], ALU.add))
            v.sem_inc(done(st)[0], 1)

        def conv_shape(st):
            p = {2: 1, 4: 2, 6: 3}[st]
            return p, 2 * p + 1, IMG + 2 * p, p + 1

        def img(st):
            p, k, side, pairs = conv_shape(st)
            return image[:, 0:pairs * side * IMG].rearrange("p (d r w) -> p d r w", d=pairs, w=IMG)

        def shifts(eng, copy, st, half, kind, images=(0, 1), parts=(0, 1, 2, 3)):
            p, k, side, pairs = conv_shape(st)
            eng.wait_ge(S("img_zero"), at(st, "img_zero") + 1)
            src = n_chan[:, :].rearrange("c (b r w) -> c b r w", b=B, w=IMG)
            for b in images:
                for g in parts:
                    eng.wait_ge(S(kind), at(st, kind) + 8 * b + 2 * g + 2)
                    if b:
                        eng.wait_ge(S("conv"), at(st, "conv") + min(4, (16 * g + 15 + p) // 16 + 1))
                    for dx in range(half, k, 2):
                        lo, hi = max(0, p - dx), min(IMG, IMG + p - dx)
                        m = copy(img(st)[half * C:(half + 1) * C, dx // 2, p + 16 * g:p + 16 * g + 16, lo:hi],
                                 src[:, b, 16 * g:16 * g + 16, lo + dx - p:hi + dx - p])
                    m.then_inc(S(f"img{half}"), 1)

        def image_zero(v, link, st):
            p, k, side, pairs = conv_shape(st)
            im = img(st)
            link(v.memset(im[:, :, 0:p, :], 0.0))
            link(v.memset(im[:, :, p + IMG:side, :], 0.0))
            link(v.memset(im[:, :, :, 0:p], 0.0))
            link(v.memset(im[:, :, :, IMG - p:IMG], 0.0))
            v.sem_inc(S("img_zero"), 1)

        def conv_tensor(pe, st, weights):
            p, k, side, pairs = conv_shape(st)
            for g in range(NT // 8):
                y = bank[g % 2]
                if g >= 2:
                    pe.wait_ge(S("conv_used"), at(st, "conv_used") + g - 1)
                for t in range(8):
                    T = 8 * g + t
                    b, h2 = T // TPB, T % TPB
                    need = b * 4 + min(3, (2 * h2 + 1 + p) // 16) + 1
                    for half in range(2):
                        pe.wait_ge(S(f"img{half}"), at(st, f"img{half}") + need)
                    n = 0
                    for pair in range(pairs):
                        K = P if 2 * pair + 1 < k else C
                        for dy in range(k):
                            r = 2 * h2 + dy
                            m = nc.tensor.matmul(y[:, t * C:(t + 1) * C], img(st)[0:K, pair, r:r + 2, :].rearrange("p r w -> p (r w)"),
                                                 weights(b, n)[0:K], start=(n == 0), stop=(n == pairs * k - 1))
                            n += 1
                m.then_inc(S("conv"), 1)

        def conv_vector(v, link, st, kind="chan"):
            p = conv_shape(st)[0]
            shifts(v, v.tensor_copy, st, 0, kind, images=(0,))
            for g in range(NT // 8):
                if g >= 1 and g <= 4:
                    shifts(v, v.tensor_copy, st, 0, kind, images=(1,), parts=(g - 1,))
                v.wait_ge(S("conv"), at(st, "conv") + g + 1)
                x = x_tok[:, 8 * g:8 * g + 8, :]
                v.tensor_tensor(x, x, bank[g % 2][:, :].rearrange("p (t c) -> p t c", c=C), ALU.add).then_inc(S("conv_used"), 1)
            v.wait_ge(S("conv_used"), at(st, "conv_used") + NT // 8)
            v.sem_inc(done(st)[0], 1)

        def bias_vector(v, link, bias):
            link(v.tensor_tensor(x_tok[:, :, :], x_tok[:, :, :], bias.unsqueeze(1).broadcast_to([P, NT, C]), ALU.add))

        def l0_tensor(pe):
            pe.wait_ge(S("s0_weights"), 16 * len(loads[0]))
            pe.wait_ge(S("s0_rows"), 32)
            rows_w = n_chan
            for j in range(16):
                if j >= 2:
                    pe.wait_ge(S("s0_a"), j - 1)
                    pe.wait_ge(S("s0_g"), j - 1)
                nc.tensor.matmul(bank[j % 2][0:C, :], W[0, "Wa"], rows_w[:, j * 512:(j + 1) * 512], start=True, stop=True).then_inc(S("s0_a_t"), 1)
                nc.tensor.matmul(bank[2 + j % 2][0:C, :], W[0, "Wg"], rows_w[:, j * 512:(j + 1) * 512], start=True, stop=True).then_inc(S("s0_g_t"), 1)
            ak = a_k[:, :].rearrange("k (b h c) -> k b h c", b=B, c=C)
            for b in range(B):
                for g in range(8 * b, 8 * b + 8):
                    c0 = (g % 8) * 8
                    if g >= 2:
                        pe.wait_ge(S("s0_b"), g - 1)
                    for i in range(8):
                        lhs = n_w[:, b * TPB:(b + 1) * TPB, :, c0 + i].rearrange("w t p -> w (t p)")
                        m = nc.tensor.matmul(bank[4 + g % 2][0:C, i * C:(i + 1) * C], lhs, W[0, "Wb"], start=True, stop=True)
                    m.then_inc(S("s0_b_t"), 1)
                pe.wait_ge(S("s0_a"), 16)
                for g in range(8 * b, 8 * b + 8):
                    c0 = (g % 8) * 8
                    pe.wait_ge(S("s0_b"), g + 1)
                    if g >= 2:
                        pe.wait_ge(S("s0_gab"), g - 1)
                    for i in range(8):
                        m = nc.tensor.matmul(bank[6 + g % 2][0:C, i * C:(i + 1) * C], b_h[:, c0 + i, :], ak[:, b, :, c0 + i], start=True, stop=True)
                    m.then_inc(S("s0_ab_t"), 1)
            gl = g_l[:, :].rearrange("l (t p c) -> l t p c", p=2, c=C)
            for m8 in range(8):
                pe.wait_ge(S("s0_gab"), 8 if m8 < 4 else 16)
                if m8 >= 2:
                    pe.wait_ge(S("s0_out"), m8 - 1)
                for par in range(2):
                    m = nc.tensor.matmul(bank[m8 % 2][par * C:(par + 1) * C, :], W[0, "Wo"], gl[:, m8 * 8:(m8 + 1) * 8, par, :], start=True, stop=True)
                m.then_inc(S("s0_out_t"), 1)

        def l0_scalar(a):
            a.wait_ge(S("s0_weights"), 16 * len(loads[0]))
            for j in range(16):
                a.wait_ge(S("s0_g_t"), j + 1)
                nc.scalar.activation(g_l[:, j * 512:(j + 1) * 512], bank[2 + j % 2][0:C, :], ACT.Sigmoid, bias=W[0, "bg"]).then_inc(S("s0_g"), 1)

        def l0_vector(v, link):
            v.wait_ge(S("s0_weights"), 16 * len(loads[0]))
            for j in range(16):
                v.wait_ge(S("s0_a_t"), j + 1)
                v.tensor_scalar(a_k[:, j * 512:(j + 1) * 512], bank[j % 2][0:C, :], W[0, "ba"], None, ALU.add).then_inc(S("s0_a"), 1)
            gl = g_l[:, :].rearrange("l (b h c) -> l b h c", b=B, c=C)
            for b in range(B):
                for g in range(8 * b, 8 * b + 8):
                    c0 = (g % 8) * 8
                    v.wait_ge(S("s0_b_t"), g + 1)
                    if b:
                        v.wait_ge(S("s0_ab_t"), g - 7)
                    v.tensor_tensor(b_h[:, c0:c0 + 8, :], bank[4 + g % 2][0:C, :].rearrange("p (i l) -> p i l", l=C),
                                    W[0, "bb"].unsqueeze(1).broadcast_to([C, 8, C]), ALU.add).then_inc(S("s0_b"), 1)
                v.wait_ge(S("s0_g"), 16)
                for g in range(8 * b, 8 * b + 8):
                    c0 = (g % 8) * 8
                    v.wait_ge(S("s0_ab_t"), g + 1)
                    dst = gl[:, b, :, c0:c0 + 8]
                    v.tensor_tensor(dst, dst, bank[6 + g % 2][0:C, :].rearrange("l (c j) -> l j c", j=C), ALU.mult).then_inc(S("s0_gab"), 1)
            for m8 in range(8):
                v.wait_ge(S("s0_out_t"), m8 + 1)
                x = x_tok[:, m8 * 8:(m8 + 1) * 8, :]
                v.scalar_tensor_tensor(x, bank[m8 % 2][:, :].rearrange("p (t c) -> p t c", c=C), W[0, "bo"], x, ALU.add, ALU.add).then_inc(S("s0_out"), 1)
            v.wait_ge(S("s0_out"), 8)
            v.sem_inc(done(0)[0], 1)

        def l2_tensor(pe):
            channels_tensor(pe, 4)
            pe.wait_ge(S("s4_weights"), 16 * len(loads[4]))
            for g in range(NT // 2):
                pe.wait_ge(S("chan"), at(4, "chan") + g // 2 + 1)
                if g >= 2:
                    pe.wait_ge(S("s4_qkv"), g - 1)
                for t in range(2):
                    T = 2 * g + t
                    m = nc.tensor.matmul(bank[g % 2][:, t * 192:(t + 1) * 192], n_chan[:, T * P:(T + 1) * P], W[4, "qkv"], start=True, stop=True)
                m.then_inc(S("s4_qkv_t"), 1)
            pe.wait_ge(S("s4_k"), 2)
            for b in range(B):
                for t in range(TPB):
                    T = b * TPB + t
                    m = nc.tensor.matmul(bank[2][0:C, b * 128:b * 128 + C + 1], k_tok[:, T, :], v_tok[:, T, :], start=(t == 0), stop=(t == TPB - 1))
            m.then_inc(S("s4_kv_t"), 1)
            pe.wait_ge(S("s4_q"), 2)
            channels_tensor(pe, 4, kind="qchan")
            pe.wait_ge(S("s4_kv"), 1)
            for g in range(NT // 4):
                pe.wait_ge(S("qchan"), g + 1)
                if g >= 2:
                    pe.wait_ge(S("s4_att"), g - 1)
                for t in range(4):
                    T = 4 * g + t
                    m = nc.tensor.matmul(bank[g % 2][:, t * 128:t * 128 + C + 1], n_chan[:, T * P:(T + 1) * P], kv[:, T // TPB, :], start=True, stop=True)
                m.then_inc(S("s4_att_t"), 1)
            pe.wait_ge(S("s4_att_done"), 1)
            channels_tensor(pe, 4, src=k_tok, kind="attchan")
            for g in range(NT // 8):
                pe.wait_ge(S("attchan"), 2 * g + 2)
                if g >= 2:
                    pe.wait_ge(S("s4_proj"), g - 1)
                for t in range(8):
                    T = 8 * g + t
                    m = nc.tensor.matmul(bank[3 + g % 2][:, t * C:(t + 1) * C], n_chan[:, T * P:(T + 1) * P], W[4, "proj"][0:C], start=True, stop=True)
                m.then_inc(S("s4_proj_t"), 1)
            channels_tensor(pe, 4, src=v_tok[:, :, 0:C], kind="vchan")
            pe.wait_ge(S("s4_conv_w"), 1)
            conv_tensor(pe, 4, lambda b, n: W[4, "conv"][:, n, :])

        def l2_scalar(a):
            channels_scalar(a, 4)
            sq = image[:, 0:4096].rearrange("p (t c) -> p t c", c=C)
            for kind, x in (("k", k_tok), ("q", n_tok)):
                for b in range(B):
                    t = x[:, b * TPB:(b + 1) * TPB, :]
                    u = sq[:, b * TPB:(b + 1) * TPB, :]
                    a.wait_ge(S(f"s4_{kind}_relu"), b + 1)
                    nc.scalar.activation(t, t, ACT.Square).then_inc(S("s4_sq_a"), 1)
                    a.wait_ge(S("s4_sq_a"), (0 if kind == "k" else 2) + b + 1)
                    nc.scalar.activation(u, t, ACT.Square).then_inc(S(f"s4_{kind}_sq"), 1)
                    a.wait_ge(S(f"s4_{kind}_ssq"), b + 1)
                    w = ssq[:, 0, b * TPB:(b + 1) * TPB]
                    nc.scalar.activation(w, w, ACT.Sqrt).then_inc(S(f"s4_{kind}_norm"), 1)
            channels_scalar(a, 4, "qchan")
            a.wait_ge(S("s4_att"), 16)
            nc.scalar.activation(n_tok[:, :, :], k_tok[:, :, :], ACT.Square).then_inc(S("s4_att_sq"), 1)
            a.wait_ge(S("s4_att_ms"), 1)
            nc.scalar.activation(ssq[:, 1, :], ssq[:, 1, :], ACT.Sqrt).then_inc(S("s4_att_rms"), 1)
            a.wait_ge(S("s4_weights"), 16 * len(loads[4]))
            channels_scalar(a, 4, "attchan", W[4, "dwc_b"])
            a.wait_ge(S("s4_proj_t"), 8)
            channels_scalar(a, 4, "vchan")
            shifts(a, nc.scalar.copy, 4, 1, "vchan")

        def l2_vector(v, link):
            bias = W[4, "qkv_b"].unsqueeze(1).broadcast_to([P, 2, 192])
            v.wait_ge(S("s4_weights"), 16 * len(loads[4]))
            link(v.memset(v_tok[:, :, C:C + 1], 1.0))
            link(v.tensor_tensor(W[4, "conv"], W[4, "proj"].unsqueeze(1).broadcast_to([P, 15, C]),
                                 W[4, "dwc"].unsqueeze(2).broadcast_to([P, 15, C]), ALU.mult))
            v.sem_inc(S("s4_conv_w"), 1)
            for g in range(NT // 2):
                v.wait_ge(S("s4_qkv_t"), g + 1)
                src = bank[g % 2][:, 0:384].rearrange("p (t c) -> p t c", c=192)
                for i, x in enumerate((n_tok, k_tok, v_tok)):
                    m = v.tensor_tensor(x[:, 2 * g:2 * g + 2, 0:C], src[:, :, i * C:(i + 1) * C], bias[:, :, i * C:(i + 1) * C], ALU.add)
                m.then_inc(S("s4_qkv"), 1)
            v.wait_ge(S("s4_qkv"), NT // 2)
            sq = image[:, 0:4096].rearrange("p (t c) -> p t c", c=C)
            for kind, x in (("k", k_tok), ("q", n_tok)):
                for b in range(B):
                    t = x[:, b * TPB:(b + 1) * TPB, :]
                    v.tensor_scalar(t, t, 0.0, 1e-5, ALU.max, ALU.add).then_inc(S(f"s4_{kind}_relu"), 1)
            for kind, x in (("k", k_tok), ("q", n_tok)):
                for b in range(B):
                    t = x[:, b * TPB:(b + 1) * TPB, :]
                    w = ssq[:, 0, b * TPB:(b + 1) * TPB]
                    v.wait_ge(S(f"s4_{kind}_sq"), b + 1)
                    link(v.tensor_reduce(w, sq[:, b * TPB:(b + 1) * TPB, :], AX, ALU.add))
                    v.sem_inc(S(f"s4_{kind}_ssq"), 1)
                    v.wait_ge(S(f"s4_{kind}_norm"), b + 1)
                    link(v.tensor_scalar(w, w, 1e-12, None, ALU.max))
                    link(v.reciprocal(w, w))
                    link(v.tensor_tensor(t, t, w.unsqueeze(2).broadcast_to([P, TPB, C]), ALU.mult))
                    v.sem_inc(S(f"s4_{kind}"), 1)
            v.wait_ge(S("s4_kv_t"), 1)
            link(v.tensor_scalar(kv[:, :, :], bank[2][0:C, 0:256].rearrange("p (b c) -> p b c", b=B)[:, :, 0:C + 1], 1.0 / (IMG * IMG), None, ALU.mult))
            v.sem_inc(S("s4_kv"), 1)
            image_zero(v, link, 4)
            for g in range(NT // 4):
                v.wait_ge(S("s4_att_t"), g + 1)
                src = bank[g % 2][:, :].rearrange("p (t c) -> p t c", c=128)
                w = zrec[:, 4 * g:4 * g + 4]
                link(v.tensor_scalar(w, src[:, :, C], 1e-5, None, ALU.add))
                link(v.reciprocal(w, w))
                v.tensor_tensor(k_tok[:, 4 * g:4 * g + 4, :], src[:, :, 0:C], w.unsqueeze(2).broadcast_to([P, 4, C]), ALU.mult).then_inc(S("s4_att"), 1)
            w = ssq[:, 1, :]
            v.wait_ge(S("s4_att_sq"), 1)
            link(v.tensor_reduce(w, n_tok[:, :, :], AX, ALU.add))
            link(v.tensor_scalar(w, w, 1.0 / C, 1e-5, ALU.mult, ALU.add))
            v.sem_inc(S("s4_att_ms"), 1)
            v.wait_ge(S("s4_att_rms"), 1)
            link(v.reciprocal(w, w))
            link(v.tensor_tensor(k_tok[:, :, :], k_tok[:, :, :], w.unsqueeze(2).broadcast_to([P, NT, C]), ALU.mult))
            link(v.tensor_tensor(k_tok[:, :, :], k_tok[:, :, :], W[4, "norm_w"].unsqueeze(1).broadcast_to([P, NT, C]), ALU.mult))
            v.sem_inc(S("s4_att_done"), 1)
            bias_vector(v, link, W[4, "proj_b"])
            for g in range(NT // 8):
                v.wait_ge(S("s4_proj_t"), g + 1)
                x = x_tok[:, 8 * g:8 * g + 8, :]
                v.tensor_tensor(x, x, bank[3 + g % 2][:, :].rearrange("p (t c) -> p t c", c=C), ALU.add).then_inc(S("s4_proj"), 1)
            v.wait_ge(S("s4_proj"), 8)
            conv_vector(v, link, 4, "vchan")

        def l3_tensor(pe):
            pe.wait_ge(S("normed"), at(6, "normed") + 4)
            for b in range(B):
                for t in range(TPB):
                    m = nc.tensor.matmul(bank[2][0:C, b:b + 1], n_tok[:, b * TPB + t, :], ones_f[:, 0:1], start=(t == 0), stop=(t == TPB - 1))
            m.then_inc(S("s6_pool_t"), 1)
            pe.wait_ge(S("s6_weights"), 16 * len(loads[6]))
            pe.wait_ge(S("s6_pool"), 1)
            nc.tensor.matmul(bank[3][0:16, 0:B], W[6, "dk_w1"], pooled[:, :], start=True, stop=True)
            nc.tensor.matmul(bank[3][0:16, B:2 * B], W[6, "cg_w1"], pooled[:, :], start=True, stop=True).then_inc(S("s6_hid_t"), 1)
            pe.wait_ge(S("s6_hidden"), 2)
            for h in range(2):
                m = nc.tensor.matmul(bank[4][h * C:(h + 1) * C, 0:B], W[6, "cg_w2"], hid16[:, 1, :], start=True, stop=True)
            m.then_inc(S("s6_gate_t"), 1)
            pe.wait_ge(S("s6_rep"), 1)
            for b in range(B):
                m = nc.tensor.matmul(bank[5][:, b * 224:(b + 1) * 224], hid_rep[:, b, :], W[6, "dk_w2"], start=True, stop=True)
            m.then_inc(S("s6_dyn_t"), 1)
            channels_tensor(pe, 6)
            pe.wait_ge(S("s6_diag"), 1)
            conv_tensor(pe, 6, lambda b, n: diag[:, b, n, :])

        def l3_scalar(a):
            a.wait_ge(S("s6_weights"), 16 * len(loads[6]))
            a.wait_ge(S("s6_hid_t"), 1)
            for i, n in enumerate(("dk_b1", "cg_b1")):
                nc.scalar.activation(hid16[:, i, :], bank[3][0:16, i * B:(i + 1) * B], ACT.Gelu, bias=W[6, n]).then_inc(S("s6_hidden"), 1)
            a.wait_ge(S("s6_gate_t"), 1)
            nc.scalar.activation(gate3[:, :], bank[4][:, 0:B], ACT.Sigmoid, bias=W[6, "cg_b2"]).then_inc(S("s6_gate"), 1)
            channels_scalar(a, 6)
            shifts(a, nc.scalar.copy, 6, 1, "chan")

        def l3_vector(v, link):
            v.wait_ge(S("s6_pool_t"), 1)
            link(v.tensor_scalar(pooled[:, :], bank[2][0:C, 0:B], 1.0 / (IMG * IMG), None, ALU.mult))
            v.sem_inc(S("s6_pool"), 1)
            image_zero(v, link, 6)
            v.wait_ge(S("s6_hidden"), 2)
            link(v.tensor_copy(hid_rep[:, :, :], hid16[:, 0, :].unsqueeze(2).broadcast_to([16, B, P])))
            v.sem_inc(S("s6_rep"), 1)
            v.wait_ge(S("s6_weights"), 16 * len(loads[6]))
            v.wait_ge(S("s6_dyn_t"), 1)
            v.wait_ge(S("s6_gate"), 1)
            for h in range(2):
                p = slice(h * C, (h + 1) * C)
                src = bank[5][p, 0:448].rearrange("p (b g h n) -> p b g h n", b=B, g=4, h=2)
                b2 = W[6, "dk_b2"][p].rearrange("p (g h n) -> p g h n", g=4, h=2)
                for b in range(B):
                    f = fused[p, b, :]
                    d4 = dyn[p, b, :].rearrange("p (g n) -> p g n", g=4)
                    link(v.tensor_tensor(d4, src[:, b, :, h, :], b2[:, :, h, :], ALU.add))
                    for g in range(4):
                        link(v.scalar_tensor_tensor(f, d4[:, g, :], gsel[p, g:g + 1], W[6, "dw"][p] if g == 0 else f, ALU.mult, ALU.add))
                    link(v.tensor_scalar(f, f, gate3[p, b:b + 1], None, ALU.mult))
            for b in range(B):
                link(v.tensor_tensor(diag[:, b, :, :], ident2[:, :].unsqueeze(1).broadcast_to([P, 28, C]),
                                     fused[:, b, :].unsqueeze(2).broadcast_to([P, 28, C]), ALU.mult))
            v.sem_inc(S("s6_diag"), 1)
            conv_vector(v, link, 6)

        def graph_tensor(pe):
            pe.wait_ge(S("s3_weights"), 16 * len(loads[3]))
            for T in range(NT):
                pe.wait_ge(S("chan"), at(3, "chan") + T // 4 + 1)
                m = nc.tensor.matmul(bank[T // 32][:, (T % 32) * 16:(T % 32) * 16 + 16], n_chan[:, T * P:(T + 1) * P], W[3, "w_gat"], start=True, stop=True)
            m.then_inc(S("s3_h_t"), 1)
            pe.wait_ge(S("s3_last"), 1)
            for i in range(3):
                m = nc.tensor.transpose(bank[2][0:ROW, i * P:(i + 1) * P], last[:, i, :], ident[:, :])
            m.then_inc(S("s3_last_t"), 1)
            pe.wait_ge(S("s3_across"), 1)
            nc.tensor.transpose(bank[3][:, 0:ROW], last_t[0:ROW, 4, 1:P + 1], ident[0:ROW, 0:ROW])
            nc.tensor.transpose(bank[3][:, 32:32 + ROW], last_t[0:ROW, 0, 1:P + 1], ident[0:ROW, 0:ROW]).then_inc(S("s3_carry_t"), 1)

        def graph_scalar(a):
            def window(i, b):
                a.wait_ge(S("s3_expo"), 2 * i + b + 1)
                nc.scalar.activation(scale[:, b, :, :, :], expo[:, :, :, :], ACT.Exp).then_inc(S("s3_scale"), 1)
            with a.Fori(0, NW // 2) as i:
                for b in range(2):
                    window(i, b)
            a.wait_ge(S("s3_across_in"), 1)
            nc.scalar.activation(last_t[0:ROW, 2, 1:P + 1], last_t[0:ROW, 1, 1:P + 1], ACT.Exp).then_inc(S("s3_across_exp"), 1)
            nc.scalar.activation(last_t[0:ROW, 3, 1:P + 1], last_t[0:ROW, 5, 1:P + 1], ACT.Exp).then_inc(S("s3_across_exp"), 1)
            a.wait_ge(S("s3_merge_in"), 1)
            nc.scalar.activation(wgt[:, :, :, :], wgt[:, :, :, :], ACT.Exp).then_inc(S("s3_merge_exp"), 1)
            a.wait_ge(S("s3_score_var"), 1)
            nc.scalar.activation(sc2[:, :], sc2[:, :], ACT.Sqrt).then_inc(S("s3_score_std"), 1)

        def graph_vector(v, link):
            H16 = HEADS * GE

            def rep(ap, n):
                return ap.unsqueeze(1).broadcast_to([P, NT, n])
            v.wait_ge(S("s3_weights"), 16 * len(loads[3]))
            v.wait_ge(S("s3_h_t"), 1)
            for i in range(2):
                link(v.tensor_copy(h_tok[:, 32 * i:32 * i + 32, 0:H16], bank[i][:, :].rearrange("p (t f) -> p t f", f=H16)))
            prod16 = src_i[:, 0:NT * H16].bitcast(F32).rearrange("p (t f) -> p t f", f=H16)
            for att, dst in (("att_src", h_tok[:, :, H16:ROW]), ("att_dst", a_dst[:, :, :])):
                link(v.tensor_tensor(prod16, h_tok[:, :, 0:H16], rep(W[3, att], H16), ALU.mult))
                link(v.tensor_reduce(dst, prod16.rearrange("p t (h g) -> p t h g", g=GE), AX, ALU.add))
            link(v.tensor_scalar(has[:, :], seg_size[:, :], 0.0, None, ALU.is_gt))
            link(v.tensor_scalar(start_f[:, :], has[:, :], -1.0, -1.0e9, ALU.add, ALU.mult))
            link(v.tensor_tensor(start_f[:, :], start_f[:, :], seg_base[:, :], ALU.add))
            link(v.tensor_copy(start_i[:, :], start_f[:, :]))
            link(v.tensor_tensor(start_f[:, :], seg_base[:, :], seg_size[:, :], ALU.add))
            link(v.tensor_scalar(start_f[:, :], start_f[:, :], -1.0, 0.0, ALU.add, ALU.max))
            link(v.tensor_copy(end_i[:, :], start_f[:, :]))
            link(v.tensor_scalar(part_i[:, :], end_i[:, :], 11, None, ALU.logical_shift_right))
            link(v.tensor_copy(part_f[:, :], part_i[:, :]))
            link(v.tensor_scalar(cont[:, :], part_f[:, :], float(EPP), None, ALU.mult))
            link(v.tensor_tensor(cont[:, :], seg_base[:, :], cont[:, :], ALU.is_lt))
            link(v.tensor_tensor(cont[:, :], cont[:, :], has[:, :], ALU.mult))
            link(v.tensor_scalar(part_f[:, :], part_f[:, :], -1.0, 0.0, ALU.add, ALU.max))
            link(v.tensor_copy(part_i[:, :], part_f[:, :]))
            v.sem_inc(S("s3_tok"), 1)
            link(v.memset(prev_edge[:, :], 32767 << 13))
            v.sem_inc(S("s3_prev0"), 1)
            v.wait_ge(S("s3_sorted"), 32)
            link(v.memset(src_i[:, EPP:EPP + 2 * WIN], 0))
            link(v.tensor_scalar(src_i[:, 0:EPP], sorted_e[:, :], TOK - 1, None, ALU.bitwise_and))
            link(v.tensor_scalar(dst_i[:, :], sorted_e[:, :], 13, None, ALU.logical_shift_right))
            link(v.tensor_copy(dst_f[:, :], dst_i[:, :]))
            link(v.tensor_scalar(prev_edge[:, :], prev_edge[:, :], 13, None, ALU.logical_shift_right))
            link(v.tensor_copy(prev_dst[:, 0:1], prev_edge[:, 1:2]))
            link(v.tensor_tensor(same[:, 1:EPP], dst_f[:, 1:EPP], dst_f[:, 0:EPP - 1], ALU.is_equal))
            link(v.tensor_scalar(first_f[:, :], dst_f[:, 0:1], float(TOK - 1), None, ALU.min))
            link(v.tensor_copy(first_i[:, :], first_f[:, :]))
            link(v.tensor_tensor(join[:, 0:1], dst_f[:, 0:1], prev_dst[:, 0:1], ALU.is_equal))
            link(v.tensor_reduce(join[:, 1:2], same[:, 1:EPP], AX, ALU.min))
            link(v.memset(same[:, 0:1], 0.0))
            v.sem_inc(S("s3_idx_all"), 1)
            for b in range(2):
                link(v.tensor_copy(idx_ring[:, b, :], src_i[:, b * WIN:(b + 1) * WIN]))
                v.sem_inc(S("s3_idx"), 1)
            v.wait_ge(S("s3_adst"), 16)
            for h in range(HEADS):
                link(v.tensor_tensor_scan(a_dst_e[:, :, h], same[:, :], a_dst_e[:, :, h], 0.0, ALU.mult, ALU.add))
            link(v.memset(runmax[:, 1, :, WIN:WIN + 1], NEG))
            link(v.memset(sums[:, 1, WIN - 1, :], 0.0))

            STEPS = 34

            def window(i, b, first=False):
                g = 2 * i + b
                k = [0]

                def step(ins):
                    k[0] += 1
                    ins.then_inc(S("s3_window"), 1)
                    v.wait_ge(S("s3_window"), g * STEPS + k[0])
                prev = 1 - b
                v.wait_ge(s_gath[b], (i + 1) * (16 * WIN))
                at = bass.ds(g * WIN, WIN)
                step(v.tensor_tensor(z[:, :, :], rows[:, b, :, H16:ROW], a_dst_e[:, at, :], ALU.add))
                zt = z[:, :, :].rearrange("p c h -> p h c")
                step(v.scalar_tensor_tensor(e4[:, :, :], zt, 0.2, zt, ALU.mult, ALU.max))
                step(v.tensor_scalar(restart[:, :], same[:, at], -1.0, -NEG, ALU.add, ALU.mult))
                step(v.tensor_copy(runmax[:, b, :, 0:1], runmax[:, prev, :, WIN:WIN + 1]))
                for h in range(HEADS):
                    step(v.tensor_tensor_scan(runmax[:, b, h, 1:WIN + 1], restart[:, :], e4[:, h, :], runmax[:, prev, h, WIN:WIN + 1], ALU.add, ALU.max))
                step(v.tensor_tensor(expo[:, 0, :, :], runmax[:, b, :, 0:WIN], restart[:, :].unsqueeze(1).broadcast_to([P, HEADS, WIN]), ALU.add))
                step(v.tensor_tensor(expo[:, 0, :, :], expo[:, 0, :, :], runmax[:, b, :, 1:WIN + 1], ALU.subtract))
                step(v.tensor_tensor(expo[:, 1, :, :], e4[:, :, :], runmax[:, b, :, 1:WIN + 1], ALU.subtract))
                v.sem_inc(S("s3_expo"), 1)
                v.wait_ge(S("s3_scale"), g + 1)
                step(v.tensor_tensor(msg[:, :, :, :], rows[:, b, :, 0:H16].rearrange("p c (h t) -> p h t c", t=GE),
                                     scale[:, b, 1, :, :].unsqueeze(2).broadcast_to([P, HEADS, GE, WIN]), ALU.mult))
                if not first:
                    v.wait_ge(s_yout[b], i * 16)
                for f in range(ROW):
                    h = f // GE if f < H16 else f - H16
                    val = msg[:, h, f % GE, :] if f < H16 else scale[:, b, 1, h, :]
                    step(v.tensor_tensor_scan(sums[:, b, :, f], scale[:, b, 0, h, :], val, sums[:, prev, WIN - 1, f:f + 1], ALU.mult, ALU.add))
                step(v.tensor_copy(sums[:, b, :, ROW:ACC].rearrange("p c h -> p h c"), runmax[:, b, :, 1:WIN + 1]))
                step(v.tensor_copy(idx_ring[:, b, :], src_i[:, bass.ds((g + 2) * WIN, WIN)]))
                v.sem_inc(S("s3_sums"), 1)
                v.sem_inc(S("s3_idx"), 1)
                assert k[0] == STEPS, k[0]

            for b in range(2):
                window(0, b, True)
            with v.Fori(1, NW // 2) as i:
                for b in range(2):
                    window(i, b)

            end = sums[:, 1, WIN - 1, :]
            link(v.tensor_copy(last[:, 0, :], end[:, 0:ROW]))
            link(v.tensor_copy(last[:, 1, 0:H16].rearrange("p (h t) -> p h t", t=GE), end[:, ROW:ACC].unsqueeze(2).broadcast_to([P, HEADS, GE])))
            link(v.tensor_copy(last[:, 1, H16:ROW], end[:, ROW:ACC]))
            link(v.tensor_tensor(join[:, 0:1], join[:, 0:1], join[:, 1:2], ALU.mult))
            link(v.tensor_scalar(join[:, 0:1], join[:, 0:1], -1.0, -NEG, ALU.add, ALU.mult))
            link(v.tensor_copy(last[:, 2, :], join[:, 0:1].broadcast_to([P, ROW])))
            v.sem_inc(S("s3_last"), 1)
            v.wait_ge(S("s3_last_t"), 1)
            R = last_t[0:ROW, :, :]
            src = bank[2][0:ROW, :]
            one = slice(1, P + 1)
            link(v.tensor_copy(R[:, 6, one], src[:, 2 * P:3 * P]))
            link(v.tensor_copy(R[:, 7, one], src[:, P:2 * P]))
            link(v.memset(R[:, 0, 0:1], NEG))
            link(v.tensor_tensor_scan(R[:, 0, one], R[:, 6, one], R[:, 7, one], NEG, ALU.add, ALU.max))
            link(v.tensor_tensor(R[:, 1, one], R[:, 0, 0:P], R[:, 6, one], ALU.add))
            link(v.tensor_tensor(R[:, 1, one], R[:, 1, one], R[:, 0, one], ALU.subtract))
            link(v.tensor_tensor(R[:, 5, one], R[:, 7, one], R[:, 0, one], ALU.subtract))
            v.sem_inc(S("s3_across_in"), 1)
            v.wait_ge(S("s3_across_exp"), 2)
            link(v.tensor_tensor(R[:, 3, one], R[:, 3, one], src[:, 0:P], ALU.mult))
            link(v.tensor_tensor_scan(R[:, 4, one], R[:, 2, one], R[:, 3, one], 0.0, ALU.mult, ALU.add))
            v.sem_inc(S("s3_across"), 1)
            v.wait_ge(S("s3_carry_t"), 1)
            link(v.tensor_copy(carry[:, 0:ROW], bank[3][:, 0:ROW]))
            link(v.tensor_copy(carry[:, ROW:ACC], bank[3][:, 32 + H16:32 + ROW]))
            v.sem_inc(S("s3_carry"), 1)

            link(v.tensor_tensor(e_self[:, :, :], h_tok[:, :, H16:ROW], a_dst[:, :, :], ALU.add))
            link(v.scalar_tensor_tensor(e_self[:, :, :], e_self[:, :, :], 0.2, e_self[:, :, :], ALU.mult, ALU.max))
            link(v.tensor_scalar(has[:, :], has[:, :], -1.0, -NEG, ALU.add, ALU.mult))
            link(v.tensor_scalar(cont[:, :], cont[:, :], -1.0, -NEG, ALU.add, ALU.mult))
            v.wait_ge(S("s3_tok_end"), 16 * NT)
            v.wait_ge(S("s3_tok_carry"), 16 * NT)

            def bc4(ap):
                return ap.unsqueeze(2).broadcast_to([P, NT, HEADS])
            link(v.tensor_tensor(wgt[:, 0, :, :], tok_end[:, :, ROW:ACC], bc4(has[:, :]), ALU.add))
            link(v.tensor_tensor(wgt[:, 1, :, :], tok_carry[:, :, ROW:ACC], bc4(cont[:, :]), ALU.add))
            link(v.tensor_tensor(m_all[:, :, :], wgt[:, 0, :, :], wgt[:, 1, :, :], ALU.max))
            link(v.tensor_tensor(m_all[:, :, :], m_all[:, :, :], e_self[:, :, :], ALU.max))
            link(v.tensor_tensor(wgt[:, 0, :, :], wgt[:, 0, :, :], m_all[:, :, :], ALU.subtract))
            link(v.tensor_tensor(wgt[:, 1, :, :], wgt[:, 1, :, :], m_all[:, :, :], ALU.subtract))
            link(v.tensor_tensor(wgt[:, 2, :, :], e_self[:, :, :], m_all[:, :, :], ALU.subtract))
            v.sem_inc(S("s3_merge_in"), 1)
            v.wait_ge(S("s3_merge_exp"), 1)

            def weigh(out, src, w, ones_too=True):
                link(v.tensor_tensor(out[:, :, 0:H16].rearrange("p t (h g) -> p t h g", g=GE), src[:, :, 0:H16].rearrange("p t (h g) -> p t h g", g=GE),
                                     w.unsqueeze(3).broadcast_to([P, NT, HEADS, GE]), ALU.mult))
                if ones_too:
                    link(v.tensor_tensor(out[:, :, H16:ROW], src[:, :, H16:ROW], w, ALU.mult))
                else:
                    link(v.tensor_copy(out[:, :, H16:ROW], w))
            weigh(agg, tok_end, wgt[:, 0, :, :])
            weigh(tmp, tok_carry, wgt[:, 1, :, :])
            link(v.tensor_tensor(agg[:, :, :], agg[:, :, :], tmp[:, :, :], ALU.add))
            weigh(tmp, h_tok, wgt[:, 2, :, :], False)
            link(v.tensor_tensor(agg[:, :, :], agg[:, :, :], tmp[:, :, :], ALU.add))
            den = agg[:, :, H16:ROW]
            link(v.tensor_scalar(den, den, 1e-16, None, ALU.add))
            link(v.reciprocal(den, den))
            A = agg[:, :, 0:H16]
            A4 = A.rearrange("p t (h g) -> p t h g", g=GE)
            link(v.tensor_tensor(A4, A4, den.unsqueeze(3).broadcast_to([P, NT, HEADS, GE]), ALU.mult))
            link(v.tensor_tensor(A, A, rep(W[3, "b_gat"], H16), ALU.add))
            link(v.tensor_reduce(sc1[:, :], A, AX, ALU.add))
            link(v.tensor_scalar(sc1[:, :], sc1[:, :], 1.0 / H16, None, ALU.mult))
            link(v.tensor_tensor(A, A, sc1[:, :].unsqueeze(2).broadcast_to([P, NT, H16]), ALU.subtract))
            T16 = tmp[:, :, 0:H16]
            link(v.tensor_tensor(T16, A, A, ALU.mult))
            link(v.tensor_reduce(sc2[:, :], T16, AX, ALU.add))
            link(v.tensor_scalar(sc2[:, :], sc2[:, :], 1.0 / H16, 1e-5, ALU.mult, ALU.add))
            v.sem_inc(S("s3_score_var"), 1)
            v.wait_ge(S("s3_score_std"), 1)
            link(v.reciprocal(sc2[:, :], sc2[:, :]))
            link(v.tensor_tensor(A, A, sc2[:, :].unsqueeze(2).broadcast_to([P, NT, H16]), ALU.mult))
            link(v.tensor_tensor(A, A, rep(W[3, "ln_gamma"], H16), ALU.mult))
            link(v.tensor_tensor(A, A, rep(W[3, "ln_beta"], H16), ALU.add))
            link(v.tensor_reduce(gates[:, :, 4:8], A.rearrange("p t (h g) -> p t g h", g=GE), AX, ALU.add))
            val = gt[0][:, 0:NT * 4].rearrange("p (t e) -> p t e", e=4)
            link(v.tensor_scalar(val, gates[:, :, 4:8], 1.0 / HEADS, None, ALU.mult))

        def graph_sync(sp):
            rows_v = row_d.rearrange("(t p) f -> p t f", p=P)
            sp.wait_ge(S("s3_tok"), 1)
            sp.dma_start(rows_v, h_tok[:, :, :]).then_inc(S("s3_tables"), 16)
            sp.dma_start(adst_d.rearrange("(t p) f -> p t f", p=P), a_dst[:, :, :]).then_inc(S("s3_tables"), 16)
            for b in range(2):
                sp.wait_ge(s_sc[b], 8 * EPP)
            lists = sorted_d.rearrange("(p j) t -> p (j t)", p=P)
            sp.dma_start(sorted_e[:, :], lists).then_inc(S("s3_sorted"), 16)
            sp.wait_ge(S("s3_prev0"), 1)
            sp.dma_start(prev_edge[1:P, :], lists[0:P - 1, EPP - 2:EPP]).then_inc(S("s3_sorted"), 16)
            sp.wait_ge(S("s3_starts"), 16 * NT)
            sp.dma_start(a_dst_e[:, :, :].rearrange("p j h -> p (j h)"), start_d.rearrange("(p j) h -> p (j h)", p=P)).then_inc(S("s3_starts_in"), 16)
            out_v = sums_d.rearrange("(p j) f -> p j f", p=P)

            with sp.Fori(0, NW // 2) as i:
                for b in range(2):
                    sp.wait_ge(S("s3_sums"), 2 * i + b + 1)
                    sp.dma_start(out_v[:, bass.ds((2 * i + b) * WIN, WIN), :], sums[:, b, :, :]).then_inc(s_yout[b], 16)
            sp.wait_ge(S("s3_carry"), 1)
            sp.dma_start(carry_d, carry[:, :]).then_inc(S("s3_carry_out"), 16)

        def graph_pool(g):
            def at(ap):
                return bass.IndirectOffsetOnAxis(ap=ap, axis=0)
            g.wait_ge(S("s3_tok"), 1)
            for T in range(NT):
                g.indirect_dma_start(out=start_d[:, :], out_offset=at(start_i[:, T:T + 1]), in_=a_dst[:, T, :], in_offset=None,
                                     bounds_check=EDGES - 1, oob_is_err=False).then_inc(S("s3_starts"), 16)
            g.wait_ge(S("s3_tables"), 32)
            g.wait_ge(S("s3_idx_all"), 1)
            g.wait_ge(S("s3_starts_in"), 16)
            g.indirect_dma_start(out=a_dst_e[:, 0, :], out_offset=None, in_=adst_d[:, :], in_offset=at(first_i[:, 0:1])).then_inc(S("s3_adst"), 16)
            with g.Fori(0, NW // 2) as i:
                for b in range(2):
                    g.wait_ge(S("s3_idx"), 2 * i + b + 1)
                    g.sem_inc(S("s3_pool_go"), 1)
                    for c in range(WIN):
                        g.indirect_dma_start(out=rows[:, b, c, :], out_offset=None, in_=row_d[:, :], in_offset=at(idx_ring[:, b, c:c + 1])).then_inc(s_gath[b], 16)
            for b in range(2):
                g.wait_ge(s_yout[b], 16 * (NW // 2))
            for T in range(NT):
                g.indirect_dma_start(out=tok_end[:, T, :], out_offset=None, in_=sums_d[:, :], in_offset=at(end_i[:, T:T + 1])).then_inc(S("s3_tok_end"), 16)
            g.wait_ge(S("s3_carry_out"), 16)
            for T in range(NT):
                g.indirect_dma_start(out=tok_carry[:, T, :], out_offset=None, in_=carry_d[:, :], in_offset=at(part_i[:, T:T + 1])).then_inc(S("s3_tok_carry"), 16)

        NQ = GROUP // SUB

        def sort_sync(sp):
            sp.dma_start(edge_i[:, :, :], d["L1_ffn_edge_index"].rearrange("t (p j) -> p t j", p=P)).then_inc(S("sort_edges"), 16)
            sp.wait_ge(S("sort_fill"), 1)
            sp.dma_start(sorted_d.rearrange("(p j) t -> p (j t)", p=P), n_tok[:, 0:NT // 2, :].bitcast(I32).rearrange("p t c -> p (t c)")).then_inc(S("sort_filled"), 16)
            sv = start_d.rearrange("(h p j) f -> h p (j f)", p=P, h=2)
            for h in range(2):
                sp.dma_start(sv[h], x_tok[:, :, :].rearrange("p t c -> p (t c)")).then_inc(S("sort_zeroed"), 16)

        def sort_pool(g):
            g.iota(iota[:, :, :], pattern=[[1, P], [0, SUB]], base=0, channel_multiplier=0, allow_small_or_imprecise_dtypes=True).then_inc(S("c_made"), 1)
            g.iota(iota_p[:, :], pattern=[[0, 1]], base=0, channel_multiplier=1, allow_small_or_imprecise_dtypes=True).then_inc(S("c_made"), 1)
            g.iota(order8[:, :], pattern=[[-1, 8]], base=8, channel_multiplier=0, allow_small_or_imprecise_dtypes=True).then_inc(S("c_made"), 1)
            g.iota(order4[:, :], pattern=[[-1, 4]], base=4, channel_multiplier=0, allow_small_or_imprecise_dtypes=True).then_inc(S("c_made"), 1)
            for t, x in ((ident, 0.0), (ident2, 0.0), (tri, 1.0), (tri_f, 1.0), (ones_f, 1.0), (ones_b, 1.0), (gsel, 1.0)):
                g.memset(t[:, :], x).then_inc(S("c_made"), 1)
            g.memset(sel[:, :, :], 1.0).then_inc(S("c_made"), 1)
            g.wait_ge(S("c_made"), 12)

            def pick(t, op, fill, base, pattern, cm):
                return g.affine_select(out=t, in_=t, compare_op=op, fill=fill, base=base, pattern=pattern, channel_multiplier=cm)
            pick(ident[:, :], ALU.not_equal, 1.0, 0, [[-1, P]], 1).then_inc(S("c_ready"), 1)
            pick(tri[:, :], ALU.is_gt, 0.0, 0, [[1, P]], -1).then_inc(S("c_ready"), 1)
            pick(tri_f[:, :], ALU.is_gt, 0.0, 0, [[1, P]], -1).then_inc(S("c_ready"), 1)
            pick(sel[:, :, :], ALU.is_equal, 0.0, 0, [[1, GROUP], [0, P]], -1).then_inc(S("c_ready"), 1)
            for h in range(2):
                p = slice(h * C, (h + 1) * C)
                pick(ident2[p, :], ALU.not_equal, 1.0, 0, [[-1, C]], 1).then_inc(S("c_ready"), 1)
                pick(gsel[p, :], ALU.is_ge, 0.0, 0, [[-16, 4]], 1).then_inc(S("c_gsel"), 1)
                g.wait_ge(S("c_gsel"), h + 1)
                pick(gsel[p, :], ALU.is_ge, 0.0, 15, [[16, 4]], -1).then_inc(S("c_ready"), 1)
            g.wait_ge(S("sort_filled"), 16)

            def scatter_pair(i, first):
                for b in range(2):
                    at_group = bass.ds((i * 2 + b) * GROUP, GROUP)
                    g.wait_ge(S("sort_pos"), i * 2 + b + 1)
                    g.sem_inc(S("sort_pool_go"), 1)
                    if not first:
                        g.wait_ge(s_sc[b], i * (16 * GROUP))
                        g.sem_inc(S("sort_pool_go"), 1)
                    g.tensor_copy(pos_ring[:, b, :], pos_all[:, at_group]).then_inc(S("sort_rings"), 1)
                    g.tensor_copy(packed_ring[:, b, :], packed[:, at_group]).then_inc(S("sort_rings"), 1)
                    g.wait_ge(S("sort_rings"), (i * 2 + b) * 2 + 2)
                    g.sem_inc(S("sort_pool_go"), 1)
                    for c in range(GROUP):
                        g.indirect_dma_start(out=sorted_d[:, :], out_offset=bass.IndirectOffsetOnAxis(ap=pos_ring[:, b, c:c + 1], axis=0),
                                             in_=packed_ring[:, b, c:c + 1], in_offset=None, bounds_check=EDGES - 1, oob_is_err=False).then_inc(s_sc[b], 16)

            scatter_pair(0, True)
            with g.Fori(1, NG // 2) as i:
                scatter_pair(i, False)

        def sort_scalar(a):
            a.wait_ge(S("sort_base_in"), 1)
            nc.scalar.copy(hist[:, 0, :], H).then_inc(S("sort_hist"), 1)
            with a.Fori(0, EPP // 2) as i:
                for b in range(2):
                    c = i * 2 + b
                    a.wait_ge(S("sort_counted"), c + 1)
                    a.wait_ge(S("sort_ranked_t"), c + 1)
                    nc.scalar.copy(hist[:, (b + 1) % 2, :], H).then_inc(S("sort_hist"), 1)

        def sort_tensor(pe):
            pe.wait_ge(S("c_made"), 12)
            pe.wait_ge(S("sort_fill"), 1)
            nc.tensor.matmul(H, ones_f[:, :], x_tok[:, 0, :], start=True, stop=False, skip_group_check=True)
            with pe.Fori(0, NSUB // 2) as i:
                for b in range(2):
                    pe.wait_ge(S("sort_one1"), i * 2 + b + 1)
                    for c in range(SUB):
                        m = nc.tensor.matmul(H, onehot_lo[:, b, :, c], onehot_hi[:, b, :, c], start=False, stop=False, skip_group_check=True)
                    m.then_inc(S("sort_total_t"), 1)
            pe.wait_ge(S("c_ready"), 8)
            pe.wait_ge(S("sort_total"), 1)
            nc.tensor.matmul(bank[1][:, 0:NT], tri_f[:, :], seg_size[:, :], start=True, stop=True)
            nc.tensor.matmul(bank[1][:, NT:2 * NT], ones_f[:, :], seg_size[:, :], start=True, stop=True).then_inc(S("sort_cums_t"), 1)
            pe.wait_ge(S("sort_base"), 1)
            nc.tensor.matmul(H, ident[:, :], seg_base[:, :], start=True, stop=False, skip_group_check=True).then_inc(S("sort_base_in"), 1)

            def rows_of(gi, b):
                pe.wait_ge(S("sort_ring"), gi + 1)
                nc.tensor.transpose(bank[1][0:GROUP, 0:P], ring_low[:, b, :], ident[:, :]).then_inc(S("sort_rows_t"), 1)
                pe.wait_ge(S("sort_rows"), gi + 1)

            def spread(sub, b, q):
                pe.wait_ge(S("sort_one"), sub)
                for k in range(SUB):
                    m = nc.tensor.matmul(bank[2 + k // 4][:, (k % 4) * P:(k % 4 + 1) * P], sel[:, q * SUB + k, :], lo_rows[:, b, :], start=True, stop=True)
                m.then_inc(S("sort_bc_t"), 1)

            def ranks(sub, q):
                sbuf = q % 2
                pe.wait_ge(S("sort_one"), sub + 1)
                for k in range(SUB):
                    ch = sub * SUB + k
                    R = bank[4 + k % 4][:, 0:NT]
                    pe.wait_ge(S("sort_rank"), ch + 1)
                    nc.tensor.matmul(R, same_before[:, sbuf, k, :], onehot_hi[:, sbuf, :, k], start=True, stop=False)
                    pe.wait_ge(S("sort_hist"), ch + 1)
                    nc.tensor.matmul(H, onehot_lo[:, sbuf, :, k], onehot_hi[:, sbuf, :, k], start=False, stop=False, skip_group_check=True).then_inc(S("sort_counted"), 1)
                    nc.tensor.matmul(R, lo_on_part[:, sbuf, k, :], hist[:, k % 2, :], start=False, stop=True).then_inc(S("sort_ranked_t"), 1)

            def rank_pair(i, more):
                for b in range(2):
                    gi = i * 2 + b
                    for q in range(NQ):
                        sub = gi * NQ + q
                        if q < NQ - 1:
                            spread(sub + 1, b, q + 1)
                        elif b == 0 or more:
                            rows_of(gi + 1, 1 - b)
                            spread(sub + 1, 1 - b, 0)
                        ranks(sub, q)

            pe.sem_inc(S("sort_ranked_t"), 1)
            rows_of(0, 0)
            spread(0, 0, 0)
            with pe.Fori(0, NG // 2 - 1) as i:
                rank_pair(i, True)
            rank_pair(NG // 2 - 1, False)

        def sort_vector(v, link):
            link(v.memset(n_tok[:, 0:NT // 2, :].bitcast(I32), (2 * TOK) << 13))
            link(v.memset(x_tok[:, :, :], 0.0))
            v.sem_inc(S("sort_fill"), 1)
            v.wait_ge(S("c_made"), 12)
            v.wait_ge(S("sort_edges"), 16)
            link(v.tensor_scalar(bits_i[:, 0, :], edge_i[:, 1, :], P - 1, None, ALU.bitwise_and))
            link(v.tensor_scalar(bits_i[:, 1, :], edge_i[:, 1, :], 7, None, ALU.logical_shift_right))

            def groups(ap):
                return ap.rearrange("p (g c) -> p g c", c=GROUP)
            link(v.tensor_copy(low_high[:, :, 0, :], groups(bits_i[:, 0, :])))
            link(v.tensor_copy(low_high[:, :, 1, :], groups(bits_i[:, 1, :])))
            link(v.tensor_scalar(edge_i[:, 0, :], edge_i[:, 0, :], float(TOK - 1), None, ALU.min))
            link(v.tensor_scalar(bits_i[:, 0, :], edge_i[:, 1, :], 13, None, ALU.logical_shift_left))
            link(v.tensor_tensor(packed[:, :], bits_i[:, 0, :], edge_i[:, 0, :], ALU.bitwise_or))

            def onehots(sbuf, rb, q):
                at_sub = slice(q * SUB, (q + 1) * SUB)
                v.tensor_tensor(onehot_lo[:, sbuf, :, :], iota[:, :, :], ring[:, rb, 0, at_sub].unsqueeze(1).broadcast_to([P, P, SUB]), ALU.is_equal)
                return v.tensor_tensor(onehot_hi[:, sbuf, :, :], iota[:, 0:NT, :], ring[:, rb, 1, at_sub].unsqueeze(1).broadcast_to([P, NT, SUB]), ALU.is_equal)
            v.sem_inc(S("sort_total_t"), 2)
            v.sem_inc(S("sort_rank"), 4)
            with v.Fori(0, NG // 2) as i:
                for b in range(2):
                    gi = i * 2 + b
                    v.tensor_copy(ring[:, b, :, :], low_high[:, bass.ds(gi, 1), :, :].rearrange("p o k c -> p (o k) c")).then_inc(S("sort_ring1"), 1)
                    v.wait_ge(S("sort_ring1"), gi + 1)
                    for q in range(NQ):
                        v.wait_ge(S("sort_total_t"), gi * NQ + q + 1)
                        onehots(q % 2, b, q).then_inc(S("sort_one1"), 1)
            v.wait_ge(S("sort_total_t"), NSUB + 2)
            link(v.tensor_copy(seg_size[:, :], H))
            v.sem_inc(S("sort_total"), 1)
            v.wait_ge(S("sort_cums_t"), 1)
            link(v.tensor_tensor_scan(cums[:, :], ones_f[:, 0:NT], bank[1][:, NT:2 * NT], 0.0, ALU.mult, ALU.add))
            link(v.tensor_tensor(cums[:, :], cums[:, :], bank[1][:, NT:2 * NT], ALU.subtract))
            link(v.tensor_tensor(seg_base[:, :], cums[:, :], bank[1][:, 0:NT], ALU.add))
            v.sem_inc(S("sort_base"), 1)
            v.wait_ge(S("c_ready"), 8)

            def ring_of(gi, b):
                v.tensor_copy(ring[:, b, :, :], low_high[:, bass.ds(gi, 1), :, :].rearrange("p o k c -> p (o k) c")).then_inc(S("sort_ring_b"), 1)
                v.wait_ge(S("sort_ring_b"), gi + 1)
                v.tensor_copy(ring_low[:, b, :], ring[:, b, 0, :]).then_inc(S("sort_ring"), 1)
                v.wait_ge(S("sort_rows_t"), gi + 1)
                v.tensor_copy(lo_rows[:, b, :], bank[1][0:GROUP, 0:P]).then_inc(S("sort_rows"), 1)

            def make(sub, b, q):
                sbuf = q % 2
                onehots(sbuf, b, q)
                v.wait_ge(S("sort_bc_t"), sub + 1)
                for k in range(SUB):
                    low = bank[2 + k // 4][:, (k % 4) * P:(k % 4 + 1) * P]
                    j = q * SUB + k
                    v.scalar_tensor_tensor(same_before[:, sbuf, k, :], low, ring_low[:, b, j:j + 1], tri[:, :], ALU.is_equal, ALU.mult)
                for t in range(2):
                    m = v.tensor_scalar(lo_on_part[:, sbuf, 4 * t:4 * t + 4, :], bank[2 + t][:, :].rearrange("p (a b) -> p a b", b=P), iota_p[:, 0:1], None, ALU.is_equal)
                m.then_inc(S("sort_one"), 1)

            def read_ranks(sub, b, q):
                for k in range(SUB):
                    j = q * SUB + k
                    v.wait_ge(S("sort_ranked_t"), sub * SUB + k + 2)
                    v.tensor_tensor_reduce(junk[:, k % 4, :], bank[4 + k % 4][:, 0:NT], onehot_hi[:, q % 2, :, k], 1.0, 0.0,
                                           ALU.mult, ALU.add, rank[:, b, j:j + 1]).then_inc(S("sort_rank"), 1)

            def rank_pair(i, more):
                for b in range(2):
                    gi = i * 2 + b
                    for q in range(NQ):
                        sub = gi * NQ + q
                        v.wait_ge(S("sort_rank"), sub * SUB + 4)
                        if q < NQ - 1:
                            make(sub + 1, b, q + 1)
                        elif b == 0 or more:
                            ring_of(gi + 1, 1 - b)
                            make(sub + 1, 1 - b, 0)
                        read_ranks(sub, b, q)
                    v.tensor_scalar(dropped[:, :], ring[:, b, 1, :], float(NT), 1.0e9, ALU.is_ge, ALU.mult).then_inc(S("sort_step"), 1)
                    v.wait_ge(S("sort_step"), gi + 1)
                    v.wait_ge(S("sort_rank"), (gi + 1) * GROUP + 4)
                    v.tensor_tensor(pos_all[:, bass.ds(gi * GROUP, GROUP)], rank[:, b, :], dropped[:, :], ALU.add).then_inc(S("sort_pos"), 1)

            ring_of(0, 0)
            make(0, 0, 0)
            with v.Fori(0, NG // 2 - 1) as i:
                rank_pair(i, True)
            rank_pair(NG // 2 - 1, False)

        def x_tensor(pe):
            pe.wait_ge(S("x_in"), 16)
            pe.wait_ge(S("sort_rank"), EPP + 4)
            pe.wait_ge(S("c_ready"), 8)
            for g in range(8):
                if g >= 2:
                    pe.wait_ge(S("x_copied"), g - 1)
                for t in range(8):
                    T = 8 * g + t
                    m = nc.tensor.transpose(bank[6 + g % 2][:, t * C:(t + 1) * C], n_chan[:, T * P:(T + 1) * P], ident[0:C, 0:C])
                m.then_inc(S("x_t"), 1)

        def x_vector(v):
            v.wait_ge(S("sort_zeroed"), 32)
            for g in range(8):
                v.wait_ge(S("x_t"), g + 1)
                v.tensor_copy(x_tok[:, 8 * g:8 * g + 8, :], bank[6 + g % 2][:, :].rearrange("p (t c) -> p t c", c=C)).then_inc(S("x_copied"), 1)
            v.wait_ge(S("x_copied"), 8)

        SORT = 3 in stages
        block = ctx.enter_context(nc.Block())

        @block.sync
        def _(sp):
            def weights(st):
                if st not in stages:
                    return
                if st - 2 in stages:
                    sp.wait_ge(*done(st - 2))
                for dst, src in loads[st]:
                    sp.dma_start(dst, src).then_inc(S(f"s{st}_weights"), 16)

            sp.dma_start(n_chan[:, :].rearrange("c (b n) -> c b n", b=B), d["x"].rearrange("b c h w -> c b (h w)")).then_inc(S("x_in"), 16)
            sort_sync(sp)
            weights(0)
            weights(1)
            if 0 in stages:
                sp.wait_ge(S("normed"), at(0, "normed") + 4)
                sp.wait_ge(S("x_copied"), 8)
                for par in range(2):
                    sp.dma_start(n_w[:, :, par, :], n_tok[par * C:(par + 1) * C, :, :]).then_inc(S("s0_rows"), 16)
            weights(2)
            weights(3)
            weights(4)
            if 3 in stages:
                graph_sync(sp)
            for st in (5, 6, 7):
                weights(st)
            for b in range(B):
                sp.wait_ge(S("out"), 8 * (b + 1))
                sp.dma_start(out.rearrange("b c h w -> c b (h w)")[:, b], n_chan[:, b * TOK // 2:(b + 1) * TOK // 2]).then_inc(S("stored"), 16)
            sp.wait_ge(S("stored"), 32)
            sp.wait_ge(S("sort_zeroed"), 32)

        @block.gpsimd
        def _(g):
            sort_pool(g)
            if 3 in stages:
                graph_pool(g)
            for b in range(2):
                g.wait_ge(s_sc[b], 8 * EPP)

        @block.tensor
        def _(pe):
            sort_tensor(pe)
            x_tensor(pe)
            for st in stages:
                if st == 0:
                    l0_tensor(pe)
                if st in FFN:
                    channels_tensor(pe, st)
                    if st == 3:
                        graph_tensor(pe)
                    ffn_tensor(pe, st)
                if st == 2:
                    channels_tensor(pe, 2)
                    pe.wait_ge(S("s2_weights"), 16 * len(loads[2]))
                    conv_tensor(pe, 2, lambda b, n: W[2, "conv"][:, n, :])
                if st == 4:
                    l2_tensor(pe)
                if st == 6:
                    l3_tensor(pe)
            pe.wait_ge(*done(last_stage))
            channels_tensor(pe, 9, src=x_tok, kind="out")

        @block.scalar
        def _(a):
            sort_scalar(a)
            for st in stages:
                ln_scalar(a, st)
                if st == 0:
                    l0_scalar(a)
                if st in FFN:
                    channels_scalar(a, st)
                    if st == 3:
                        graph_scalar(a)
                    ffn_scalar(a, st)
                if st == 2:
                    channels_scalar(a, 2)
                    shifts(a, nc.scalar.copy, 2, 1, "chan")
                if st == 4:
                    l2_scalar(a)
                if st == 6:
                    l3_scalar(a)
            channels_scalar(a, 9, "out")

        @block.vector
        def _(v):
            chain = [0]

            def link(ins):
                chain[0] += 1
                ins.then_inc(S("vector_chain"), 1)
                v.wait_ge(S("vector_chain"), chain[0])

            sort_vector(v, link)
            x_vector(v)
            for st in stages:
                ln_vector(v, link, st)
                if st == 0:
                    l0_vector(v, link)
                if st in FFN:
                    if st == 3:
                        graph_vector(v, link)
                    ffn_vector(v, link, st)
                if st == 2:
                    v.wait_ge(S("normed"), at(2, "normed") + 4)
                    image_zero(v, link, 2)
                    v.wait_ge(S("s2_weights"), 16 * len(loads[2]))
                    bias_vector(v, link, W[2, "b"])
                    conv_vector(v, link, 2)
                if st == 4:
                    l2_vector(v, link)
                if st == 6:
                    l3_vector(v, link)


def layouts(inputs):
    import numpy as np
    c = np.ascontiguousarray
    d = {}
    for n, a in inputs.items():
        d[n] = np.asarray(a)
    for n in ("L0_ffn", "L1_ffn", "L2_ffn", "L3_ffn"):
        b1, b2, w2 = (d[f"{n}_{x}"] if f"{n}_{x}" in d else d[f"{n}_{x.upper()}"] for x in ("b1", "b2", "w2"))
        if n + "_W1" in d:
            d[n + "_w1"] = d.pop(n + "_W1")
            w2 = d.pop(n + "_W2")
        d[n + "_b1"] = c(b1.reshape(-1, P).T)
        rows = np.zeros((P, b2.size), b2.dtype)
        for r in range(3):
            rows[32 * r] = b2.reshape(-1)
        d[n + "_b2"] = rows
        if w2.shape[1] == 64:
            pairs = np.zeros((w2.shape[0] // 2, P, P), w2.dtype)
            for e in range(2):
                pairs[:, e * 64:(e + 1) * 64, e * 64:(e + 1) * 64] = w2[e::2]
            w2 = pairs
        d[n + "_w2"] = c(w2)
    for n in ("L0_ffn", "L3_ffn"):
        d[n + "_router"] = c(d.pop(n + "_router_w").T)
    d["L2_ffn_router"] = c(d.pop("L2_ffn_Wg"))
    for n in ("att_src", "att_dst"):
        d["L1_ffn_" + n] = c(d["L1_ffn_" + n].reshape(-1))

    def column_pairs(taps):
        k = taps.shape[0]
        both = np.zeros((2, taps.shape[2], (k + 1) // 2, k) + taps.shape[3:], taps.dtype)
        for x in range(k):
            both[x % 2, :, x // 2] = np.moveaxis(taps[:, x], 1, 0)
        return c(both.reshape((2 * taps.shape[2], -1) + taps.shape[3:]))
    w = d.pop("L1_conv_w").reshape(8, 3, 3, 8, 8)
    full = np.zeros((3, 3, 8, 8, 8, 8), w.dtype)
    for n in range(8):
        for m in range(8):
            full[:, :, :, n, :, m] = w[..., (m - n) % 8].transpose(1, 2, 3, 0)
    d["L1_conv_wk"] = column_pairs(full.reshape(3, 3, 64, 64))
    d["L2_qkv_wT"] = c(d.pop("L2_conv_qkv_w").T)
    d["L2_proj_wT"] = c(d.pop("L2_conv_proj_w").T)
    d["L2_dwc_taps"] = column_pairs(d.pop("L2_conv_dwc_w")[:, 0].transpose(1, 2, 0))
    d["L3_dw_taps"] = column_pairs(d.pop("L3_conv_dw_weight")[:, 0].transpose(1, 2, 0))
    d["L3_dk_w1T"] = c(d.pop("L3_conv_dk_w1").T)
    d["L3_cg_w1T"] = c(d.pop("L3_conv_cg_w1").T)
    d["L3_cg_w2T"] = c(d.pop("L3_conv_cg_w2").T)

    def dyn_pairs(a):
        a = a.reshape(4, 7, 7, -1)
        both = np.zeros((4, 2, 4, 7, a.shape[-1]), a.dtype)
        for r in range(7):
            both[:, r % 2, r // 2] = a[:, :, r]
        return c(both.reshape(4 * 56, -1).T)
    d["L3_dk_w2T"] = dyn_pairs(d.pop("L3_conv_dk_w2"))
    d["L3_dk_b2p"] = dyn_pairs(d.pop("L3_conv_dk_b2"))[0]
    return {n: c(a) for n, a in d.items()}


STAGES = (0, 1, 2, 3, 4, 5, 6, 7)


def kernel(**inputs):
    import numpy as np
    import concourse.bacc as bacc
    from concourse.bass_utils import run_bass_kernel_spmd

    nc = bacc.Bacc("TRN2", target_bir_lowering=False, num_devices=1)
    arrays = {"in_" + n: a for n, a in layouts(inputs).items()}
    d = {n[3:]: nc.dram_tensor(n, a.shape, mybir.dt.from_np(a.dtype), kind="ExternalInput").ap() for n, a in arrays.items()}
    out = nc.dram_tensor("out", (B, C, IMG, IMG), F32, kind="ExternalOutput").ap()
    scratch = {n: nc.dram_tensor("scratch_" + n, s, F32, kind="Internal").ap() for n, s in (
        ("start", (EDGES, HEADS)), ("row", (TOK, ROW)), ("adst", (TOK, HEADS)),
        ("sums", (EDGES, ACC)), ("carry", (P, ACC)))}
    scratch["sorted"] = nc.dram_tensor("scratch_sorted", (EDGES, 1), I32, kind="Internal").ap()
    program(nc, d, out, scratch, STAGES)
    r = run_bass_kernel_spmd(nc, [arrays], core_ids=[0])
    return r.results[0]["out"]
```

```python
from contextlib import ExitStack

import concourse.bass as bass
from concourse import mybir

F32 = mybir.dt.float32
I32 = mybir.dt.int32
BF16 = mybir.dt.bfloat16
ALU = mybir.AluOpType
ACT = mybir.ActivationFunctionType
AX = mybir.AxisListType.X

P = 128
B, C, IMG = 2, 64, 64
TOK = B * IMG * IMG
NT = TOK // P
TPB = NT // B
NEG = -1.0e30
EDGES = 262144
EPP = EDGES // P
GROUP = 32
NG = EPP // GROUP
SUB = 8
NSUB = EPP // SUB
WIN = 64
NW = EPP // WIN
HEADS, GE = 4, 4
TAPS = 32
ROW = HEADS * GE + HEADS
ACC = ROW + HEADS


def program(nc, d, out, scratch, stages):
    with ExitStack() as ctx:
        def sb(name, shape, dt=F32, c=ctx):
            return c.enter_context(nc.sbuf_tensor(name, shape, dt))

        def sem(name):
            return ctx.enter_context(nc.semaphore(name))

        bank = [ctx.enter_context(nc.psum_tensor(f"bank{i}", [P, 512], F32)) for i in range(8)]

        x_tok = sb("x_tok", [P, NT, C])
        n_tok = sb("n_tok", [P, NT, C])
        n_chan = sb("n_chan", [C, TOK])
        ident = sb("ident", [P, P])
        ident2 = sb("ident2", [P, C])
        ones_f = sb("ones_f", [P, P])
        ones_b = sb("ones_b", [P, P], BF16)
        gates = sb("gates", [P, NT, 8])
        order8 = sb("order8", [P, 8])
        order4 = sb("order4", [P, 4])
        mean = sb("mean", [P, NT])
        var = sb("var", [P, NT])
        seg_base = sb("seg_base", [P, NT])
        seg_size = sb("seg_size", [P, NT])
        gsel = sb("gsel", [P, 4])
        span = sb("span", [P, 4])
        pairs_i = sb("pairs_i", [P, 2], I32)

        W = {}
        wsize = 4700
        wmem = [sb("weights_even", [P, wsize]), sb("weights_odd", [P, wsize])]
        wpos = [0, 0]

        def wt(stage, name, shape, dt=F32):
            n = 1
            for s in shape[1:]:
                n *= s
            words = n if dt is F32 else (n + 1) // 2
            r = stage % 2
            at = wpos[r]
            wpos[r] += words
            assert wpos[r] <= wsize, (stage, name, wpos[r])
            ap = wmem[r][0:shape[0], at:at + words]
            if dt is not F32:
                ap = ap.bitcast(dt)
            if len(shape) == 3:
                ap = ap.rearrange("p (a b) -> p a b", b=shape[2])
            if len(shape) == 4:
                ap = ap.rearrange("p (a b c) -> p a b c", b=shape[2], c=shape[3])
            W[stage, name] = ap
            return ap

        def bcast_row(ap, n=P):
            return ap.rearrange("(o n) -> o n", o=1).broadcast_to([n, ap.shape[0]])

        loads = {}

        def load(stage, dst, src):
            loads.setdefault(stage, []).append((dst, src))

        FFN = {1: (8, 64, "L0_ffn"), 3: (4, 128, "L1_ffn"), 5: (8, 256, "L2_ffn"), 7: (8, 64, "L3_ffn")}
        for s in range(8):
            wpos[s % 2] = 0
            if s == 0:
                for n in ("Wa", "Wb", "Wg", "Wo"):
                    load(s, wt(s, n, [C, C]), d["L0_conv_" + n])
                for n in ("ba", "bg"):
                    load(s, wt(s, n, [C, 1]), d["L0_conv_" + n].rearrange("(p o) -> p o", o=1))
                bo = wt(s, "bo", [P, 1])
                for h in range(2):
                    load(s, bo[h * C:(h + 1) * C], d["L0_conv_bo"].rearrange("(p o) -> p o", o=1))
                load(s, wt(s, "bb", [C, C]), bcast_row(d["L0_conv_bb"], C))
            if s in FFN:
                E, HD, nm = FFN[s]
                NH = E * HD // P
                w1 = wt(s, "w1", [C, E, HD])
                load(s, w1, d[nm + "_w1"].rearrange("e c h -> c e h"))
                load(s, wt(s, "b1", [P, NH]), d[nm + "_b1"])
                if HD == 64:
                    load(s, wt(s, "w2", [P, NH, P]), d[nm + "_w2"].rearrange("k h c -> h k c"))
                else:
                    w2 = wt(s, "w2", [P, NH, C])
                    load(s, w2, d[nm + "_w2"].rearrange("e (a h) c -> h (e a) c", h=P))
                load(s, wt(s, "b2", [P, E * C]), d[nm + "_b2"])
                wt(s, "b2_parts", [P, 4, E * C], BF16)
                if s != 3:
                    load(s, wt(s, "router", [C, E]), d[nm + "_router"])
                if s == 5:
                    load(s, wt(s, "bg", [P, E]), bcast_row(d["L2_ffn_bg"]))
                if s == 3:
                    load(s, wt(s, "w_gat", [C, 16]), d["L1_ffn_W_gat"])
                    for n in ("att_src", "att_dst", "b_gat", "ln_gamma", "ln_beta"):
                        load(s, wt(s, n, [P, 16]), bcast_row(d["L1_ffn_" + n]))
            if s == 2:
                load(s, wt(s, "conv", [P, 4, 2 * C]), d["L1_conv_wk"])
                load(s, wt(s, "b", [P, C]), bcast_row(d["L1_conv_b"]))
            if s == 4:
                load(s, wt(s, "qkv", [C, 192]), d["L2_qkv_wT"])
                load(s, wt(s, "qkv_b", [P, 192]), bcast_row(d["L2_conv_qkv_b"]))
                load(s, wt(s, "norm_w", [P, C]), bcast_row(d["L2_conv_norm_w"]))
                load(s, wt(s, "proj_b", [P, C]), bcast_row(d["L2_conv_proj_b"]))
                pj = wt(s, "proj", [P, C])
                dw = wt(s, "dwc", [P, 9 * 2])
                load(s, dw, d["L2_dwc_taps"])
                for h in range(2):
                    load(s, pj[h * C:(h + 1) * C], d["L2_proj_wT"])
                load(s, wt(s, "dwc_b", [C, 1]), d["L2_conv_dwc_b"].rearrange("(p o) -> p o", o=1))
                wt(s, "conv", [P, 9 * 2, C])
            if s == 6:
                load(s, wt(s, "dw", [P, TAPS]), d["L3_dw_taps"])
                load(s, wt(s, "dk_w1", [C, 16]), d["L3_dk_w1T"])
                load(s, wt(s, "dk_w2", [16, 8 * TAPS]), d["L3_dk_w2T"])
                load(s, wt(s, "cg_w1", [C, 16]), d["L3_cg_w1T"])
                load(s, wt(s, "cg_w2", [16, C]), d["L3_cg_w2T"])
                for n in ("dk_b1", "cg_b1"):
                    load(s, wt(s, n, [16, 1]), d["L3_conv_" + n].rearrange("(p o) -> p o", o=1))
                load(s, wt(s, "dk_b2", [P, 8 * TAPS]), bcast_row(d["L3_dk_b2p"]))
                cb = wt(s, "cg_b2", [P, 1])
                for h in range(2):
                    load(s, cb[h * C:(h + 1) * C], d["L3_conv_cg_b2"].rearrange("(p o) -> p o", o=1))

        def region():
            return ExitStack()

        packed = sb("packed", [P, EPP], I32)
        pos_all = sb("pos_all", [P, EPP], I32)
        packed_ring = sb("packed_ring", [P, 2, GROUP], I32)
        pos_ring = sb("pos_ring", [P, 2, GROUP], I32)
        with region() as r:
            edge_i = sb("edge_i", [P, 2, EPP], I32, r)
            bits_i = sb("bits_i", [P, 2, EPP], I32, r)
            low_high = sb("low_high", [P, NG, 2, GROUP], BF16, r)
            ring = sb("ring", [P, 2, 2, GROUP], BF16, r)
            ring_low = sb("ring_low", [P, 2, GROUP], F32, r)
            onehot_lo = sb("onehot_lo", [P, 2, P, SUB], BF16, r)
            onehot_hi = sb("onehot_hi", [P, 2, NT, SUB], BF16, r)
            lo_on_part = sb("lo_on_part", [P, 2, SUB, P], F32, r)
            same_before = sb("same_before", [P, 2, SUB, P], BF16, r)
            lo_rows = sb("lo_rows", [GROUP, 2, P], BF16, r)
            sel = sb("sel", [GROUP, GROUP, P], BF16, r)
            tri = sb("tri", [P, P], BF16, r)
            tri_f = sb("tri_f", [P, P], F32, r)
            iota = sb("iota", [P, P, SUB], BF16, r)
            iota_p = sb("iota_p", [P, 1], F32, r)
            hist = sb("hist", [P, 2, NT], F32, r)
            cums = sb("cums", [P, NT], F32, r)
            junk = sb("junk", [P, 4, NT], F32, r)
            rank = sb("rank", [P, 2, GROUP], F32, r)
            dropped = sb("dropped", [P, GROUP], F32, r)
            limits = sb("limits", [P, NW // 2], F32, r)
            split = sb("split", [P, 4, GROUP], F32, r)
            split_i = sb("split_i", [P, GROUP], I32, r)
        with region() as r:
            hsq = sb("hsq", [P, NT, C], F32, r)
        with region() as r:
            a_k = sb("a_k", [C, TOK], F32, r)
            g_l = sb("g_l", [C, TOK], F32, r)
            b_h = sb("b_h", [C, C, C], F32, r)
        with region() as r:
            hid = sb("hid", [P, 2, 16, 512], F32, r)
            prod = sb("prod", [P, 2, 512], F32, r)
            y_sum = sb("y_sum", [P, 2, 4, C], F32, r)
            gt = [sb(f"gt{i}", [P, NT * 8], F32, r) for i in range(6)]
            gs = [sb(f"gs{i}", [P, NT], F32, r) for i in range(4)]
            b2_rest = sb("b2_rest", [P, 512], F32, r)
        with region() as r:
            image = sb("image", [P, B * 70 * 70], F32, r)
            diag = sb("diag", [P, B, TAPS, C], F32, r)
            pooled = sb("pooled", [C, B], F32, r)
            hid16 = sb("hid16", [16, 2, B], F32, r)
            hid_rep = sb("hid_rep", [16, B, P], F32, r)
            fused = sb("fused", [P, B, TAPS], F32, r)
            dyn = packed[:, 0:B * 4 * TAPS].bitcast(F32).rearrange("p (b n) -> p b n", b=B)
            gate3 = packed[:, B * 4 * TAPS:B * 4 * TAPS + B].bitcast(F32)
        with region() as r:
            sb("image_l2", [P, B * 68 * 68], F32, r)
            v_tok = sb("v_tok", [P, NT, C + 1], F32, r)
            k_tok = sb("k_tok", [P, NT, C], F32, r)
            kv = sb("kv", [C, B, C + 1], F32, r)
            zrec = sb("zrec", [P, NT], F32, r)
            ssq = sb("ssq", [P, 2, NT], F32, r)
        with region() as r:
            src_i = sb("src_i", [P, EPP + 2 * WIN], I32, r)
            same = pos_all[:, :].bitcast(F32)
            a_dst_e = sb("a_dst_e", [P, EPP, HEADS], F32, r)
            idx_ring = sb("idx_ring", [P, 2, WIN], I32, r)
            rows = sb("rows", [P, 2, WIN, ROW], F32, r)
            h_tok = sb("h_tok", [P, NT, ROW], F32, r)
            a_dst = sb("a_dst", [P, NT, HEADS], F32, r)
            has = sb("has", [P, NT], F32, r)
            start_f = sb("start_f", [P, NT], F32, r)
            start_i = sb("start_i", [P, NT], I32, r)
            end_i = sb("end_i", [P, NT], I32, r)
            part_i = sb("part_i", [P, NT], I32, r)
            part_f = sb("part_f", [P, NT], F32, r)
            cont = sb("cont", [P, NT], F32, r)
            first_i = sb("first_i", [P, 1], I32, r)
            first_f = sb("first_f", [P, 1], F32, r)
            last_dst = sb("last_dst", [P, 2], F32, r)
            prev_dst = sb("prev_dst", [P, 2], F32, r)
            tok_split = sb("tok_split", [P, 3, NT], F32, r)
            tok_part = sb("tok_part", [P, NT], F32, r)
            sb("gap", [P, 1], F32, r)
            join = sb("join", [P, 2], F32, r)
            last = sb("last", [P, 3, ROW], F32, r)
            last_t = sb("last_t", [ROW, 8, P + 1], F32, r)
            carry = sb("carry", [P, ACC], F32, r)
            with region() as q:
                sorted_e = sb("sorted_e", [P, EPP], I32, q)
                dst_f = sb("dst_f", [P, EPP], F32, q)
                dst_i = packed[:, :]
            with region() as q:
                z = packed[:, HEADS * GE * WIN:HEADS * GE * WIN + WIN * HEADS].bitcast(F32).rearrange("p (w h) -> p w h", w=WIN)
                e4 = sb("e4", [P, HEADS, WIN], F32, q)
                restart = sb("restart", [P, WIN], F32, q)
                runmax = sb("runmax", [P, 2, HEADS, WIN + 1], F32, q)
                expo = sb("expo", [P, 2, HEADS, WIN], F32, q)
                scale = sb("scale", [P, 2, 2, HEADS, WIN], F32, q)
                msg = packed[:, 0:HEADS * GE * WIN].bitcast(F32).rearrange("p (h e w) -> p h e w", h=HEADS, e=GE)
                sums = sb("sums", [P, 2, WIN, ACC], F32, q)
        with region() as r:
            sb("keep_clear", [P, EPP + 2 * WIN], F32, r)
            tok_end = sb("tok_end", [P, NT, ACC], F32, r)
            tok_carry = sb("tok_carry", [P, NT, ACC], F32, r)
            m_all = sb("m_all", [P, NT, HEADS], F32, r)
            e_self = sb("e_self", [P, NT, HEADS], F32, r)
            wgt = sb("wgt", [P, 3, NT, HEADS], F32, r)
            agg = sb("agg", [P, NT, ROW], F32, r)
            tmp = sb("tmp", [P, NT, ROW], F32, r)
            sc1 = sb("sc1", [P, NT], F32, r)
            sc2 = sb("sc2", [P, NT], F32, r)

        sems = {}

        def S(name):
            if name not in sems:
                sems[name] = sem(name)
            return sems[name]

        s_sc = [sem("s_scattered0"), sem("s_scattered1")]
        s_gath = [sem("s_gathered0"), sem("s_gathered1")]
        s_yout = [sem("s_sums_out0"), sem("s_sums_out1")]
        H = bank[0][:, 0:NT]
        sorted_d, start_d, row_d, adst_d, sums_d, carry_d = (scratch[n] for n in ("sorted", "start", "row", "adst", "sums", "carry"))
        n_w = n_chan[:, :].rearrange("w (t p c) -> w t p c", p=2, c=C)
        MIXERS = (0, 2, 4, 6)
        last_stage = max(stages)

        def steps(st, name):
            if name in ("normed", "centred", "squared", "var", "std"):
                return 4
            if name in ("chan", "chan_t"):
                return 16 if st else 0
            if name in ("conv", "conv_sum", "conv_back", "conv_used", "img"):
                return 16 if st in (2, 4, 6) else 0
            if name == "conv_up":
                return 18 if st in (2, 4, 6) else 0
            if name == "conv_below":
                return B if st in (2, 4, 6) else 0
            if name == "img_zero":
                return int(st in (2, 4, 6))
            if st not in FFN:
                return 0
            if name in ("up", "hid"):
                return 16 * FFN[st][0] * FFN[st][1] // P
            if name in ("down", "gated"):
                return NT
            if name == "router":
                return int(st != 3)
            return int(name in ("b2", "gate_in", "gate_exp"))

        def at(st, name):
            return sum(steps(e, name) for e in stages if e < st)

        def done(st):
            return S("stage_done"), stages.index(st) + 1

        def ln_vector(v, link, st):
            eps = 1e-6 if st in MIXERS else 1e-5
            Q = 16
            for q in range(4):
                x, m = x_tok[:, q * Q:(q + 1) * Q, :], mean[:, q * Q:(q + 1) * Q]
                link(v.tensor_reduce(m, x, AX, ALU.add))
                link(v.tensor_scalar(m, m, 1.0 / C, None, ALU.mult))
                link(v.tensor_tensor(n_tok[:, q * Q:(q + 1) * Q, :], x, m.unsqueeze(2).broadcast_to([P, Q, C]), ALU.subtract))
                v.sem_inc(S("centred"), 1)
            for q in range(4):
                m = var[:, q * Q:(q + 1) * Q]
                v.wait_ge(S("squared"), at(st, "squared") + q + 1)
                link(v.tensor_reduce(m, hsq[:, q * Q:(q + 1) * Q, :], AX, ALU.add))
                link(v.tensor_scalar(m, m, 1.0 / C, eps, ALU.mult, ALU.add))
                v.sem_inc(S("var"), 1)
            for q in range(4):
                m = var[:, q * Q:(q + 1) * Q]
                n = n_tok[:, q * Q:(q + 1) * Q, :]
                v.wait_ge(S("std"), at(st, "std") + q + 1)
                link(v.reciprocal(m, m))
                v.tensor_tensor(n, n, m.unsqueeze(2).broadcast_to([P, Q, C]), ALU.mult).then_inc(S("normed"), 1)

        def ln_scalar(a, st):
            Q = 16
            for q in range(4):
                a.wait_ge(S("centred"), at(st, "centred") + q + 1)
                nc.scalar.activation(hsq[:, q * Q:(q + 1) * Q, :], n_tok[:, q * Q:(q + 1) * Q, :], ACT.Square).then_inc(S("squared"), 1)
            for q in range(4):
                a.wait_ge(S("var"), at(st, "var") + q + 1)
                m = var[:, q * Q:(q + 1) * Q]
                nc.scalar.activation(m, m, ACT.Sqrt).then_inc(S("std"), 1)

        def channels_tensor(pe, st, src=None, kind="chan"):
            src = n_tok if src is None else src
            for g in range(NT // 4):
                if g % 4 == 0 and kind == "chan":
                    pe.wait_ge(S("normed"), at(st, "normed") + g // 4 + 1)
                if g >= 2:
                    pe.wait_ge(S(kind), at(st, kind) + g - 1)
                for t in range(4):
                    m = nc.tensor.transpose(bank[6 + g % 2][0:C, t * P:(t + 1) * P], src[:, 4 * g + t, :], ident[:, :])
                m.then_inc(S(kind + "_t"), 1)

        def channels_scalar(a, st, kind="chan", bias=None):
            for g in range(NT // 4):
                a.wait_ge(S(kind + "_t"), at(st, kind + "_t") + g + 1)
                dst, src = n_chan[:, g * 512:(g + 1) * 512], bank[6 + g % 2][0:C, :]
                m = nc.scalar.copy(dst, src) if bias is None else nc.scalar.activation(dst, src, ACT.Identity, bias=bias)
                m.then_inc(S(kind), 1)

        def ffn_tensor(pe, st):
            E, HD, _ = FFN[st]
            NH = E * HD // P
            cols = E * C
            w1 = W[st, "w1"].rearrange("p e h -> p (e h)")
            pe.wait_ge(S(f"s{st}_weights"), 16 * len(loads[st]))
            if st != 3:
                for t in range(NT):
                    if t % 4 == 0:
                        pe.wait_ge(S("chan"), at(st, "chan") + t // 4 + 1)
                    m = nc.tensor.matmul(bank[5][:, t * E:(t + 1) * E], n_chan[:, t * P:(t + 1) * P], W[st, "router"], start=True, stop=True)
                m.then_inc(S("router"), 1)

            def up(n):
                pe.wait_ge(S("chan"), at(st, "chan") + n + 1)
                for k in range(NH):
                    i = n * NH + k
                    if i >= 3:
                        pe.wait_ge(S("hid"), at(st, "hid") + i - 2)
                    nc.tensor.matmul(bank[i % 3][:, :], w1[:, k * P:(k + 1) * P], n_chan[:, n * 512:(n + 1) * 512],
                                     start=True, stop=True).then_inc(S("up"), 1)

            def down(n):
                pe.wait_ge(S("hid"), at(st, "hid") + (n + 1) * NH)
                for t in range(4):
                    T = 4 * n + t
                    y = bank[3 + T % 2]
                    if T >= 2:
                        pe.wait_ge(S("gated"), at(st, "gated") + T - 1)
                    nc.tensor.matmul(y[:, 0:cols], ones_b[:, :], W[st, "b2_parts"][:, 3, :], start=True, stop=False, skip_group_check=True)
                    for k in range(NH):
                        lhs = hid[:, n % 2, k, t * P:(t + 1) * P]
                        if HD == 64:
                            o = y[:, k * P:(k + 1) * P]
                        else:
                            e = k * P // HD
                            o = y[:, e * C:(e + 1) * C]
                        m = nc.tensor.matmul(o, lhs, W[st, "w2"][:, k, :], start=False, stop=(k == NH - 1), skip_group_check=True)
                    m.then_inc(S("down"), 1)

            pe.wait_ge(S("b2"), at(st, "b2") + 1)
            for n in range(17):
                if n < 16:
                    up(n)
                if n >= 1:
                    down(n - 1)

        def ffn_scalar(a, st):
            E, HD, _ = FFN[st]
            NH = E * HD // P
            a.wait_ge(S(f"s{st}_weights"), 16 * len(loads[st]))
            gate_scalar(a, st)
            for n in range(16):
                if n >= 2:
                    a.wait_ge(S("down"), at(st, "down") + 4 * (n - 1))
                for k in range(NH):
                    i = n * NH + k
                    a.wait_ge(S("up"), at(st, "up") + i + 1)
                    nc.scalar.activation(hid[:, n % 2, k, :], bank[i % 3][:, :], ACT.Gelu,
                                         bias=W[st, "b1"][:, k:k + 1]).then_inc(S("hid"), 1)

        def top2(v, link, E, values, order, mask, m1, m2, eq, rest):
            def bc(m):
                return m.unsqueeze(2).broadcast_to([P, NT, E])
            cur = values
            for i, m in enumerate((m1, m2)):
                link(v.tensor_reduce(m, cur, AX, ALU.max))
                link(v.tensor_tensor(eq, cur, bc(m), ALU.is_equal))
                link(v.tensor_tensor(eq, eq, order, ALU.mult))
                link(v.tensor_reduce(gs[3][:, :], eq, AX, ALU.max))
                if i == 0:
                    link(v.tensor_tensor(mask, eq, bc(gs[3][:, :]), ALU.is_equal))
                    link(v.scalar_tensor_tensor(rest, mask, 2 * NEG, cur, ALU.mult, ALU.add))
                    cur = rest
                else:
                    link(v.tensor_tensor(eq, eq, bc(gs[3][:, :]), ALU.is_equal))
                    link(v.tensor_tensor(mask, mask, eq, ALU.add))

        def gate_vector(v, link, st):
            E = FFN[st][0]
            n = NT * E
            val, ex, eq, rest, mask = (g[:, 0:n].rearrange("p (t e) -> p t e", e=E) for g in gt[:5])
            G = gates[:, :, 0:E]
            order = (order8 if E == 8 else order4)[:, :].unsqueeze(1).broadcast_to([P, NT, E])

            def bc(m):
                return m.unsqueeze(2).broadcast_to([P, NT, E])
            m1, m2, m3 = gs[0][:, :], gs[1][:, :], gs[2][:, :]
            logits = bank[5][:, 0:n].rearrange("p (t e) -> p t e", e=E)
            if st in (1, 7):
                v.wait_ge(S("router"), at(st, "router") + 1)
                link(v.tensor_reduce(m1, logits, AX, ALU.max))
                link(v.tensor_tensor(ex, logits, bc(m1), ALU.subtract))
                v.sem_inc(S("gate_in"), 1)
                v.wait_ge(S("gate_exp"), at(st, "gate_exp") + 1)
                link(v.tensor_reduce(m1, ex, AX, ALU.add))
                link(v.reciprocal(m1, m1))
                link(v.tensor_tensor(val, ex, bc(m1), ALU.mult))
                top2(v, link, E, val, order, mask, m1, m2, eq, rest)
                link(v.tensor_tensor(m3, m1, m2, ALU.add))
                link(v.tensor_scalar(m3, m3, 1e-12, None, ALU.max))
                link(v.reciprocal(m3, m3))
                link(v.tensor_tensor(val, val, mask, ALU.mult))
                link(v.tensor_tensor(G, val, bc(m3), ALU.mult))
                return
            if st == 5:
                v.wait_ge(S("router"), at(st, "router") + 1)
                link(v.tensor_tensor(val, logits, W[st, "bg"].unsqueeze(1).broadcast_to([P, NT, E]), ALU.add))
            top2(v, link, E, val, order, mask, m1, m2, eq, rest)
            link(v.tensor_tensor(ex, val, bc(m1), ALU.subtract))
            v.sem_inc(S("gate_in"), 1)
            v.wait_ge(S("gate_exp"), at(st, "gate_exp") + 1)
            link(v.tensor_tensor(ex, ex, mask, ALU.mult))
            link(v.tensor_reduce(m3, ex, AX, ALU.add))
            link(v.reciprocal(m3, m3))
            link(v.tensor_tensor(G, ex, bc(m3), ALU.mult))

        def gate_scalar(a, st):
            E = FFN[st][0]
            ex = gt[1][:, 0:NT * E]
            a.wait_ge(S("gate_in"), at(st, "gate_in") + 1)
            nc.scalar.activation(ex, ex, ACT.Exp).then_inc(S("gate_exp"), 1)

        def ffn_b2(v, link, st):
            b2, parts = W[st, "b2"], W[st, "b2_parts"]
            n = b2.shape[1]
            rest = b2_rest[:, 0:n]
            v.wait_ge(S(f"s{st}_weights"), 16 * len(loads[st]))
            link(v.tensor_copy(parts[:, 0, :], b2))
            link(v.tensor_tensor(rest, b2, parts[:, 0, :], ALU.subtract))
            link(v.tensor_copy(parts[:, 1, :], rest))
            link(v.tensor_tensor(rest, rest, parts[:, 1, :], ALU.subtract))
            link(v.tensor_copy(parts[:, 2, :], rest))
            link(v.memset(parts[:, 3, :], 0.0))
            for i in range(3):
                link(v.tensor_copy(parts[32 * i:32 * i + 32, 3, :], parts[32 * i:32 * i + 32, i, :]))
            v.sem_inc(S("b2"), 1)

        def ffn_vector(v, link, st):
            E, HD, _ = FFN[st]
            cols = E * C
            ffn_b2(v, link, st)
            gate_vector(v, link, st)
            if st in (1, 7):
                link(v.tensor_tensor(x_tok[:, :, :], x_tok[:, :, :], n_tok[:, :, :], ALU.add))
            for T in range(NT):
                v.wait_ge(S("down"), at(st, "down") + T + 1)
                p = prod[:, T % 2, 0:cols]
                v.tensor_tensor(p.rearrange("p (e c) -> p e c", c=C), bank[3 + T % 2][:, 0:cols].rearrange("p (e c) -> p e c", c=C),
                                gates[:, T, 0:E].unsqueeze(2).broadcast_to([P, E, C]), ALU.mult).then_inc(S("gated"), 1)
                v.wait_ge(S("gated"), at(st, "gated") + T + 1)
                link(v.tensor_reduce(y_sum[:, (T // 4) % 2, T % 4, :], p.rearrange("p (e c) -> p c e", c=C), AX, ALU.add))
                if T % 4 == 3:
                    x = x_tok[:, T - 3:T + 1, :]
                    link(v.tensor_tensor(x, x, y_sum[:, (T // 4) % 2, :, :], ALU.add))
            v.sem_inc(done(st)[0], 1)

        def conv_pad(st):
            return {2: 1, 4: 2, 6: 3}[st]

        def img(st):
            side = IMG + 2 * conv_pad(st)
            return image[:, 0:B * side * side].rearrange("p (b r w) -> p b r w", b=B, w=side)

        def conv_memory(st):
            if st == 2:
                mem = diag[0:C, :, :, :].rearrange("p b n c -> p (b n c)")
                upper, y = mem[:, 0:2048], mem[:, 2048:3072]
            else:
                upper, y = packed[0:C, 0:2048].bitcast(F32), pos_all[0:C, 0:1024].bitcast(F32)
            return upper.rearrange("p (s n) -> p s n", s=4), y.rearrange("p (s n) -> p s n", s=2)

        def image_zero(v, link, st):
            p, im = conv_pad(st), img(st)
            link(v.memset(im[:, :, 0:p, :], 0.0))
            link(v.memset(im[:, :, p + IMG:, :], 0.0))
            link(v.memset(im[0:C, :, :, 0:p], 0.0))
            link(v.memset(im[0:C, :, :, p + IMG:], 0.0))
            if p > 1:
                link(v.memset(im[C:P, :, :, 0:p - 1], 0.0))
            link(v.memset(im[C:P, :, :, p - 1 + IMG:], 0.0))
            v.sem_inc(S("img_zero"), 1)

        def image_scalar(a, st, kind):
            p = conv_pad(st)
            a.wait_ge(S("img_zero"), at(st, "img_zero") + 1)
            for g in range(NT // 4):
                b, t = divmod(g, 8)
                a.wait_ge(S(kind + "_t"), at(st, kind + "_t") + g + 1)
                nc.scalar.copy(img(st)[0:C, b, p + 8 * t:p + 8 * t + 8, p:p + IMG],
                               bank[6 + g % 2][0:C, :].rearrange("c (r w) -> c r w", w=IMG)).then_inc(S(kind), 1)

        def image_vector(v, st, kind):
            p = conv_pad(st)
            for g in range(NT // 4):
                b, t = divmod(g, 8)
                v.wait_ge(S(kind), at(st, kind) + g + 1)
                rows8 = slice(p + 8 * t, p + 8 * t + 8)
                v.tensor_copy(img(st)[C:P, b, rows8, p - 1:p - 1 + IMG], img(st)[0:C, b, rows8, p:p + IMG]).then_inc(S("img"), 1)

        def conv_tensor(pe, st, weights):
            p = conv_pad(st)
            pairs = p + 1

            def window(b, r, n, px, py):
                return img(st)[:, b, r + 2 * py:r + 2 * py + n, 2 * px:2 * px + IMG]

            def back(g):
                pe.wait_ge(S("conv_sum"), at(st, "conv_sum") + g + 1)
                if g >= 2:
                    pe.wait_ge(S("conv_used"), at(st, "conv_used") + g - 1)
                for t in range(4):
                    m = nc.tensor.transpose(bank[3 + g % 2][:, t * C:(t + 1) * C], conv_memory(st)[1][:, g % 2, t * P:(t + 1) * P], ident[0:C, 0:C])
                m.then_inc(S("conv_back"), 1)

            for g in range(NT // 4):
                b, t = divmod(g, 8)
                pe.wait_ge(S("img"), at(st, "img") + 8 * b + min(8, t + 2))
                if g >= 3:
                    pe.wait_ge(S("conv_sum"), at(st, "conv_sum") + g - 2)
                    pe.wait_ge(S("conv_up"), at(st, "conv_up") + 9 * ((g - 3) // 8) + (g - 3) % 8 + 1)
                for n in range(pairs * pairs):
                    px, py = divmod(n, pairs)
                    m = nc.tensor.matmul(bank[g % 3][:, :], weights(b, px, py), window(b, 8 * t, 8, px, py), start=(n == 0), stop=(n == pairs * pairs - 1))
                m.then_inc(S("conv"), 1)
                if t == 7:
                    for n in range(pairs * p):
                        px, py = divmod(n, p)
                        m = nc.tensor.matmul(bank[5][0:C, b * C:(b + 1) * C], weights(b, px, py)[:, C:P], window(b, IMG, 1, px, py),
                                             start=(n == 0), stop=(n == pairs * p - 1))
                    m.then_inc(S("conv_below"), 1)
                if g >= 2:
                    back(g - 2)
            back(NT // 4 - 2)
            back(NT // 4 - 1)

        def conv_scalar(a, st):
            upper = conv_memory(st)[0]
            for i in range(9 * B):
                b, t = divmod(i, 9)
                if i >= 4:
                    pb, pt = divmod(i - 4, 9)
                    a.wait_ge(S("conv_sum"), at(st, "conv_sum") + 8 * pb + min(pt + 1, 8))
                if t < 8:
                    g = 8 * b + t
                    a.wait_ge(S("conv"), at(st, "conv") + g + 1)
                    nc.scalar.copy(upper[:, i % 4, :], bank[g % 3][C:P, :]).then_inc(S("conv_up"), 1)
                else:
                    a.wait_ge(S("conv_below"), at(st, "conv_below") + b + 1)
                    nc.scalar.copy(upper[:, i % 4, 0:IMG], bank[5][0:C, b * C:(b + 1) * C]).then_inc(S("conv_up"), 1)

        def conv_vector(v, link, st, kind="chan"):
            upper, y = conv_memory(st)
            image_vector(v, st, kind)

            def add(g):
                v.wait_ge(S("conv_back"), at(st, "conv_back") + g + 1)
                x = x_tok[:, 4 * g:4 * g + 4, :]
                v.tensor_tensor(x, x, bank[3 + g % 2][:, 0:4 * C].rearrange("p (t c) -> p t c", c=C), ALU.add).then_inc(S("conv_used"), 1)

            for g in range(NT // 4):
                b, t = divmod(g, 8)
                i = 9 * b + t
                v.wait_ge(S("conv"), at(st, "conv") + g + 1)
                v.wait_ge(S("conv_up"), at(st, "conv_up") + i + 2)
                if g >= 2:
                    v.wait_ge(S("conv_back"), at(st, "conv_back") + g - 1)
                low = bank[g % 3][0:C, :]
                v.tensor_tensor(y[:, g % 2, 0:7 * IMG], low[:, 0:7 * IMG], upper[:, i % 4, IMG:8 * IMG], ALU.add)
                v.tensor_tensor(y[:, g % 2, 7 * IMG:8 * IMG], low[:, 7 * IMG:8 * IMG], upper[:, (i + 1) % 4, 0:IMG], ALU.add).then_inc(S("conv_sum"), 1)
                if g >= 1:
                    add(g - 1)
            add(NT // 4 - 1)
            v.wait_ge(S("conv_used"), at(st, "conv_used") + NT // 4)
            v.sem_inc(done(st)[0], 1)

        def bias_vector(v, link, bias):
            link(v.tensor_tensor(x_tok[:, :, :], x_tok[:, :, :], bias.unsqueeze(1).broadcast_to([P, NT, C]), ALU.add))

        def l0_tensor(pe):
            pe.wait_ge(S("s0_weights"), 16 * len(loads[0]))
            pe.wait_ge(S("s0_rows"), 32)
            rows_w = n_chan
            for j in range(16):
                if j >= 2:
                    pe.wait_ge(S("s0_a"), j - 1)
                    pe.wait_ge(S("s0_g"), j - 1)
                nc.tensor.matmul(bank[j % 2][0:C, :], W[0, "Wa"], rows_w[:, j * 512:(j + 1) * 512], start=True, stop=True).then_inc(S("s0_a_t"), 1)
                nc.tensor.matmul(bank[2 + j % 2][0:C, :], W[0, "Wg"], rows_w[:, j * 512:(j + 1) * 512], start=True, stop=True).then_inc(S("s0_g_t"), 1)
            ak = a_k[:, :].rearrange("k (b h c) -> k b h c", b=B, c=C)
            for b in range(B):
                for g in range(8 * b, 8 * b + 8):
                    c0 = (g % 8) * 8
                    if g >= 2:
                        pe.wait_ge(S("s0_b"), g - 1)
                    for i in range(8):
                        lhs = n_w[:, b * TPB:(b + 1) * TPB, :, c0 + i].rearrange("w t p -> w (t p)")
                        m = nc.tensor.matmul(bank[4 + g % 2][0:C, i * C:(i + 1) * C], lhs, W[0, "Wb"], start=True, stop=True)
                    m.then_inc(S("s0_b_t"), 1)
                pe.wait_ge(S("s0_a"), 16)
                for g in range(8 * b, 8 * b + 8):
                    c0 = (g % 8) * 8
                    pe.wait_ge(S("s0_b"), g + 1)
                    if g >= 2:
                        pe.wait_ge(S("s0_gab"), g - 1)
                    for i in range(8):
                        m = nc.tensor.matmul(bank[6 + g % 2][0:C, i * C:(i + 1) * C], b_h[:, c0 + i, :], ak[:, b, :, c0 + i], start=True, stop=True)
                    m.then_inc(S("s0_ab_t"), 1)
            gl = g_l[:, :].rearrange("l (t p c) -> l t p c", p=2, c=C)
            for m8 in range(8):
                pe.wait_ge(S("s0_gab"), 8 if m8 < 4 else 16)
                if m8 >= 2:
                    pe.wait_ge(S("s0_out"), m8 - 1)
                for par in range(2):
                    m = nc.tensor.matmul(bank[m8 % 2][par * C:(par + 1) * C, :], W[0, "Wo"], gl[:, m8 * 8:(m8 + 1) * 8, par, :], start=True, stop=True)
                m.then_inc(S("s0_out_t"), 1)

        def l0_scalar(a):
            a.wait_ge(S("s0_weights"), 16 * len(loads[0]))
            for j in range(16):
                a.wait_ge(S("s0_g_t"), j + 1)
                nc.scalar.activation(g_l[:, j * 512:(j + 1) * 512], bank[2 + j % 2][0:C, :], ACT.Sigmoid, bias=W[0, "bg"]).then_inc(S("s0_g"), 1)

        def l0_vector(v, link):
            v.wait_ge(S("s0_weights"), 16 * len(loads[0]))
            for j in range(16):
                v.wait_ge(S("s0_a_t"), j + 1)
                v.tensor_scalar(a_k[:, j * 512:(j + 1) * 512], bank[j % 2][0:C, :], W[0, "ba"], None, ALU.add).then_inc(S("s0_a"), 1)
            gl = g_l[:, :].rearrange("l (b h c) -> l b h c", b=B, c=C)
            for b in range(B):
                for g in range(8 * b, 8 * b + 8):
                    c0 = (g % 8) * 8
                    v.wait_ge(S("s0_b_t"), g + 1)
                    if b:
                        v.wait_ge(S("s0_ab_t"), g - 7)
                    v.tensor_tensor(b_h[:, c0:c0 + 8, :], bank[4 + g % 2][0:C, :].rearrange("p (i l) -> p i l", l=C),
                                    W[0, "bb"].unsqueeze(1).broadcast_to([C, 8, C]), ALU.add).then_inc(S("s0_b"), 1)
                v.wait_ge(S("s0_g"), 16)
                for g in range(8 * b, 8 * b + 8):
                    c0 = (g % 8) * 8
                    v.wait_ge(S("s0_ab_t"), g + 1)
                    dst = gl[:, b, :, c0:c0 + 8]
                    v.tensor_tensor(dst, dst, bank[6 + g % 2][0:C, :].rearrange("l (c j) -> l j c", j=C), ALU.mult).then_inc(S("s0_gab"), 1)
            for m8 in range(8):
                v.wait_ge(S("s0_out_t"), m8 + 1)
                x = x_tok[:, m8 * 8:(m8 + 1) * 8, :]
                v.scalar_tensor_tensor(x, bank[m8 % 2][:, :].rearrange("p (t c) -> p t c", c=C), W[0, "bo"], x, ALU.add, ALU.add).then_inc(S("s0_out"), 1)
            v.wait_ge(S("s0_out"), 8)
            v.sem_inc(done(0)[0], 1)

        def l2_tensor(pe):
            channels_tensor(pe, 4)
            pe.wait_ge(S("s4_weights"), 16 * len(loads[4]))
            for g in range(NT // 2):
                pe.wait_ge(S("chan"), at(4, "chan") + g // 2 + 1)
                if g >= 2:
                    pe.wait_ge(S("s4_qkv"), g - 1)
                for t in range(2):
                    T = 2 * g + t
                    m = nc.tensor.matmul(bank[g % 2][:, t * 192:(t + 1) * 192], n_chan[:, T * P:(T + 1) * P], W[4, "qkv"], start=True, stop=True)
                m.then_inc(S("s4_qkv_t"), 1)
            pe.wait_ge(S("s4_k"), 2)
            for b in range(B):
                for t in range(TPB):
                    T = b * TPB + t
                    m = nc.tensor.matmul(bank[2][0:C, b * 128:b * 128 + C + 1], k_tok[:, T, :], v_tok[:, T, :], start=(t == 0), stop=(t == TPB - 1))
            m.then_inc(S("s4_kv_t"), 1)
            pe.wait_ge(S("s4_q"), 2)
            channels_tensor(pe, 4, kind="qchan")
            pe.wait_ge(S("s4_kv"), 1)
            for g in range(NT // 4):
                pe.wait_ge(S("qchan"), g + 1)
                if g >= 2:
                    pe.wait_ge(S("s4_att"), g - 1)
                for t in range(4):
                    T = 4 * g + t
                    m = nc.tensor.matmul(bank[g % 2][:, t * 128:t * 128 + C + 1], n_chan[:, T * P:(T + 1) * P], kv[:, T // TPB, :], start=True, stop=True)
                m.then_inc(S("s4_att_t"), 1)
            pe.wait_ge(S("s4_att_done"), 1)
            channels_tensor(pe, 4, src=k_tok, kind="attchan")
            for g in range(NT // 8):
                pe.wait_ge(S("attchan"), 2 * g + 2)
                if g >= 2:
                    pe.wait_ge(S("s4_proj"), g - 1)
                for t in range(8):
                    T = 8 * g + t
                    m = nc.tensor.matmul(bank[3 + g % 2][:, t * C:(t + 1) * C], n_chan[:, T * P:(T + 1) * P], W[4, "proj"][0:C], start=True, stop=True)
                m.then_inc(S("s4_proj_t"), 1)
            channels_tensor(pe, 4, src=v_tok[:, :, 0:C], kind="vchan")
            pe.wait_ge(S("s4_conv_w"), 1)
            conv_tensor(pe, 4, lambda b, px, py: W[4, "conv"][:, 2 * (3 * px + py):2 * (3 * px + py) + 2, :].rearrange("p h c -> p (h c)"))

        def l2_scalar(a):
            channels_scalar(a, 4)
            sq = image[:, 0:4096].rearrange("p (t c) -> p t c", c=C)
            for kind, x in (("k", k_tok), ("q", n_tok)):
                for b in range(B):
                    t = x[:, b * TPB:(b + 1) * TPB, :]
                    u = sq[:, b * TPB:(b + 1) * TPB, :]
                    a.wait_ge(S(f"s4_{kind}_relu"), b + 1)
                    nc.scalar.activation(t, t, ACT.Square).then_inc(S("s4_sq_a"), 1)
                    a.wait_ge(S("s4_sq_a"), (0 if kind == "k" else 2) + b + 1)
                    nc.scalar.activation(u, t, ACT.Square).then_inc(S(f"s4_{kind}_sq"), 1)
                    a.wait_ge(S(f"s4_{kind}_ssq"), b + 1)
                    w = ssq[:, 0, b * TPB:(b + 1) * TPB]
                    nc.scalar.activation(w, w, ACT.Sqrt).then_inc(S(f"s4_{kind}_norm"), 1)
            channels_scalar(a, 4, "qchan")
            a.wait_ge(S("s4_att"), 16)
            nc.scalar.activation(n_tok[:, :, :], k_tok[:, :, :], ACT.Square).then_inc(S("s4_att_sq"), 1)
            a.wait_ge(S("s4_att_ms"), 1)
            nc.scalar.activation(ssq[:, 1, :], ssq[:, 1, :], ACT.Sqrt).then_inc(S("s4_att_rms"), 1)
            a.wait_ge(S("s4_weights"), 16 * len(loads[4]))
            channels_scalar(a, 4, "attchan", W[4, "dwc_b"])
            a.wait_ge(S("s4_proj_t"), 8)
            image_scalar(a, 4, "vchan")
            conv_scalar(a, 4)

        def l2_vector(v, link):
            bias = W[4, "qkv_b"].unsqueeze(1).broadcast_to([P, 2, 192])
            v.wait_ge(S("s4_weights"), 16 * len(loads[4]))
            link(v.memset(v_tok[:, :, C:C + 1], 1.0))
            link(v.tensor_tensor(W[4, "conv"], W[4, "proj"].unsqueeze(1).broadcast_to([P, 18, C]),
                                 W[4, "dwc"].unsqueeze(2).broadcast_to([P, 18, C]), ALU.mult))
            v.sem_inc(S("s4_conv_w"), 1)
            for g in range(NT // 2):
                v.wait_ge(S("s4_qkv_t"), g + 1)
                src = bank[g % 2][:, 0:384].rearrange("p (t c) -> p t c", c=192)
                for i, x in enumerate((n_tok, k_tok, v_tok)):
                    m = v.tensor_tensor(x[:, 2 * g:2 * g + 2, 0:C], src[:, :, i * C:(i + 1) * C], bias[:, :, i * C:(i + 1) * C], ALU.add)
                m.then_inc(S("s4_qkv"), 1)
            v.wait_ge(S("s4_qkv"), NT // 2)
            sq = image[:, 0:4096].rearrange("p (t c) -> p t c", c=C)
            for kind, x in (("k", k_tok), ("q", n_tok)):
                for b in range(B):
                    t = x[:, b * TPB:(b + 1) * TPB, :]
                    v.tensor_scalar(t, t, 0.0, 1e-5, ALU.max, ALU.add).then_inc(S(f"s4_{kind}_relu"), 1)
            for kind, x in (("k", k_tok), ("q", n_tok)):
                for b in range(B):
                    t = x[:, b * TPB:(b + 1) * TPB, :]
                    w = ssq[:, 0, b * TPB:(b + 1) * TPB]
                    v.wait_ge(S(f"s4_{kind}_sq"), b + 1)
                    link(v.tensor_reduce(w, sq[:, b * TPB:(b + 1) * TPB, :], AX, ALU.add))
                    v.sem_inc(S(f"s4_{kind}_ssq"), 1)
                    v.wait_ge(S(f"s4_{kind}_norm"), b + 1)
                    link(v.tensor_scalar(w, w, 1e-12, None, ALU.max))
                    link(v.reciprocal(w, w))
                    link(v.tensor_tensor(t, t, w.unsqueeze(2).broadcast_to([P, TPB, C]), ALU.mult))
                    v.sem_inc(S(f"s4_{kind}"), 1)
            v.wait_ge(S("s4_kv_t"), 1)
            link(v.tensor_scalar(kv[:, :, :], bank[2][0:C, 0:256].rearrange("p (b c) -> p b c", b=B)[:, :, 0:C + 1], 1.0 / (IMG * IMG), None, ALU.mult))
            v.sem_inc(S("s4_kv"), 1)
            image_zero(v, link, 4)
            for g in range(NT // 4):
                v.wait_ge(S("s4_att_t"), g + 1)
                src = bank[g % 2][:, :].rearrange("p (t c) -> p t c", c=128)
                w = zrec[:, 4 * g:4 * g + 4]
                link(v.tensor_scalar(w, src[:, :, C], 1e-5, None, ALU.add))
                link(v.reciprocal(w, w))
                v.tensor_tensor(k_tok[:, 4 * g:4 * g + 4, :], src[:, :, 0:C], w.unsqueeze(2).broadcast_to([P, 4, C]), ALU.mult).then_inc(S("s4_att"), 1)
            w = ssq[:, 1, :]
            v.wait_ge(S("s4_att_sq"), 1)
            link(v.tensor_reduce(w, n_tok[:, :, :], AX, ALU.add))
            link(v.tensor_scalar(w, w, 1.0 / C, 1e-5, ALU.mult, ALU.add))
            v.sem_inc(S("s4_att_ms"), 1)
            v.wait_ge(S("s4_att_rms"), 1)
            link(v.reciprocal(w, w))
            link(v.tensor_tensor(k_tok[:, :, :], k_tok[:, :, :], w.unsqueeze(2).broadcast_to([P, NT, C]), ALU.mult))
            link(v.tensor_tensor(k_tok[:, :, :], k_tok[:, :, :], W[4, "norm_w"].unsqueeze(1).broadcast_to([P, NT, C]), ALU.mult))
            v.sem_inc(S("s4_att_done"), 1)
            bias_vector(v, link, W[4, "proj_b"])
            for g in range(NT // 8):
                v.wait_ge(S("s4_proj_t"), g + 1)
                x = x_tok[:, 8 * g:8 * g + 8, :]
                v.tensor_tensor(x, x, bank[3 + g % 2][:, :].rearrange("p (t c) -> p t c", c=C), ALU.add).then_inc(S("s4_proj"), 1)
            v.wait_ge(S("s4_proj"), 8)
            conv_vector(v, link, 4, "vchan")

        def l3_tensor(pe):
            pe.wait_ge(S("normed"), at(6, "normed") + 4)
            for b in range(B):
                for t in range(TPB):
                    m = nc.tensor.matmul(bank[2][0:C, b:b + 1], n_tok[:, b * TPB + t, :], ones_f[:, 0:1], start=(t == 0), stop=(t == TPB - 1))
            m.then_inc(S("s6_pool_t"), 1)
            pe.wait_ge(S("s6_weights"), 16 * len(loads[6]))
            pe.wait_ge(S("s6_pool"), 1)
            nc.tensor.matmul(bank[3][0:16, 0:B], W[6, "dk_w1"], pooled[:, :], start=True, stop=True)
            nc.tensor.matmul(bank[3][0:16, B:2 * B], W[6, "cg_w1"], pooled[:, :], start=True, stop=True).then_inc(S("s6_hid_t"), 1)
            pe.wait_ge(S("s6_hidden"), 2)
            for h in range(2):
                m = nc.tensor.matmul(bank[4][h * C:(h + 1) * C, 0:B], W[6, "cg_w2"], hid16[:, 1, :], start=True, stop=True)
            m.then_inc(S("s6_gate_t"), 1)
            pe.wait_ge(S("s6_rep"), 1)
            for b in range(B):
                m = nc.tensor.matmul(bank[5][:, b * 8 * TAPS:(b + 1) * 8 * TAPS], hid_rep[:, b, :], W[6, "dk_w2"], start=True, stop=True)
            m.then_inc(S("s6_dyn_t"), 1)
            channels_tensor(pe, 6)
            pe.wait_ge(S("s6_diag"), 1)
            conv_tensor(pe, 6, lambda b, px, py: diag[:, b, 2 * (4 * px + py):2 * (4 * px + py) + 2, :].rearrange("p h c -> p (h c)"))

        def l3_scalar(a):
            a.wait_ge(S("s6_weights"), 16 * len(loads[6]))
            a.wait_ge(S("s6_hid_t"), 1)
            for i, n in enumerate(("dk_b1", "cg_b1")):
                nc.scalar.activation(hid16[:, i, :], bank[3][0:16, i * B:(i + 1) * B], ACT.Gelu, bias=W[6, n]).then_inc(S("s6_hidden"), 1)
            a.wait_ge(S("s6_gate_t"), 1)
            nc.scalar.activation(gate3[:, :], bank[4][:, 0:B], ACT.Sigmoid, bias=W[6, "cg_b2"]).then_inc(S("s6_gate"), 1)
            image_scalar(a, 6, "chan")
            conv_scalar(a, 6)

        def l3_vector(v, link):
            v.wait_ge(S("s6_pool_t"), 1)
            link(v.tensor_scalar(pooled[:, :], bank[2][0:C, 0:B], 1.0 / (IMG * IMG), None, ALU.mult))
            v.sem_inc(S("s6_pool"), 1)
            image_zero(v, link, 6)
            v.wait_ge(S("s6_hidden"), 2)
            link(v.tensor_copy(hid_rep[:, :, :], hid16[:, 0, :].unsqueeze(2).broadcast_to([16, B, P])))
            v.sem_inc(S("s6_rep"), 1)
            v.wait_ge(S("s6_weights"), 16 * len(loads[6]))
            v.wait_ge(S("s6_dyn_t"), 1)
            v.wait_ge(S("s6_gate"), 1)
            for h in range(2):
                p = slice(h * C, (h + 1) * C)
                src = bank[5][p, :].rearrange("p (b g h n) -> p b g h n", b=B, g=4, h=2)
                b2 = W[6, "dk_b2"][p].rearrange("p (g h n) -> p g h n", g=4, h=2)
                for b in range(B):
                    f = fused[p, b, :]
                    d4 = dyn[p, b, :].rearrange("p (g n) -> p g n", g=4)
                    link(v.tensor_tensor(d4, src[:, b, :, h, :], b2[:, :, h, :], ALU.add))
                    for g in range(4):
                        link(v.scalar_tensor_tensor(f, d4[:, g, :], gsel[p, g:g + 1], W[6, "dw"][p] if g == 0 else f, ALU.mult, ALU.add))
                    link(v.tensor_scalar(f, f, gate3[p, b:b + 1], None, ALU.mult))
            for b in range(B):
                link(v.tensor_tensor(diag[:, b, :, :], ident2[:, :].unsqueeze(1).broadcast_to([P, TAPS, C]),
                                     fused[:, b, :].unsqueeze(2).broadcast_to([P, TAPS, C]), ALU.mult))
            v.sem_inc(S("s6_diag"), 1)
            conv_vector(v, link, 6)

        SPLIT_STEPS = 10

        def split_position(v, step, pos, part, tmp, tmp_i):
            quot, rest, off = tmp
            step(v.tensor_scalar(quot, pos, span[:, 1:2], None, ALU.mult))
            step(v.tensor_copy(tmp_i, quot))
            step(v.tensor_copy(part, tmp_i))
            step(v.scalar_tensor_tensor(rest, part, span[:, 2:3], pos, ALU.mult, ALU.add))
            step(v.tensor_scalar(off, rest, 0.0, None, ALU.is_lt))
            step(v.tensor_tensor(part, part, off, ALU.subtract))
            step(v.scalar_tensor_tensor(rest, off, span[:, 0:1], rest, ALU.mult, ALU.add))
            step(v.tensor_scalar(off, rest, span[:, 0:1], None, ALU.is_ge))
            step(v.tensor_tensor(part, part, off, ALU.add))
            step(v.scalar_tensor_tensor(pos, part, span[:, 3:4], pos, ALU.mult, ALU.add))

        def pairs_in_use(eng):
            eng.wait_ge(S("sort_base"), 1)
            return eng.value_load(pairs_i[0:1, 0:1], min_val=1, max_val=NW // 2)

        def graph_tensor(pe):
            pe.wait_ge(S("s3_weights"), 16 * len(loads[3]))
            for T in range(NT):
                pe.wait_ge(S("chan"), at(3, "chan") + T // 4 + 1)
                m = nc.tensor.matmul(bank[T // 32][:, (T % 32) * 16:(T % 32) * 16 + 16], n_chan[:, T * P:(T + 1) * P], W[3, "w_gat"], start=True, stop=True)
            m.then_inc(S("s3_h_t"), 1)
            pe.wait_ge(S("s3_last"), 1)
            for i in range(3):
                m = nc.tensor.transpose(bank[2][0:ROW, i * P:(i + 1) * P], last[:, i, :], ident[:, :])
            m.then_inc(S("s3_last_t"), 1)
            pe.wait_ge(S("s3_across"), 1)
            nc.tensor.transpose(bank[3][:, 0:ROW], last_t[0:ROW, 4, 1:P + 1], ident[0:ROW, 0:ROW])
            nc.tensor.transpose(bank[3][:, 32:32 + ROW], last_t[0:ROW, 0, 1:P + 1], ident[0:ROW, 0:ROW]).then_inc(S("s3_carry_t"), 1)

        def graph_scalar(a):
            def window(i, b):
                a.wait_ge(S("s3_expo"), 2 * i + b + 1)
                nc.scalar.activation(scale[:, b, :, :, :], expo[:, :, :, :], ACT.Exp).then_inc(S("s3_scale"), 1)
            pairs = pairs_in_use(a)
            with a.Fori(0, NW // 2) as i:
                with a.If(i < pairs):
                    for b in range(2):
                        window(i, b)
            a.wait_ge(S("s3_across_in"), 1)
            nc.scalar.activation(last_t[0:ROW, 2, 1:P + 1], last_t[0:ROW, 1, 1:P + 1], ACT.Exp).then_inc(S("s3_across_exp"), 1)
            nc.scalar.activation(last_t[0:ROW, 3, 1:P + 1], last_t[0:ROW, 5, 1:P + 1], ACT.Exp).then_inc(S("s3_across_exp"), 1)
            a.wait_ge(S("s3_merge_in"), 1)
            nc.scalar.activation(wgt[:, :, :, :], wgt[:, :, :, :], ACT.Exp).then_inc(S("s3_merge_exp"), 1)
            a.wait_ge(S("s3_score_var"), 1)
            nc.scalar.activation(sc2[:, :], sc2[:, :], ACT.Sqrt).then_inc(S("s3_score_std"), 1)

        def graph_vector(v, link):
            H16 = HEADS * GE

            def rep(ap, n):
                return ap.unsqueeze(1).broadcast_to([P, NT, n])
            v.wait_ge(S("s3_weights"), 16 * len(loads[3]))
            v.wait_ge(S("s3_h_t"), 1)
            for i in range(2):
                link(v.tensor_copy(h_tok[:, 32 * i:32 * i + 32, 0:H16], bank[i][:, :].rearrange("p (t f) -> p t f", f=H16)))
            prod16 = src_i[:, 0:NT * H16].bitcast(F32).rearrange("p (t f) -> p t f", f=H16)
            for att, dst in (("att_src", h_tok[:, :, H16:ROW]), ("att_dst", a_dst[:, :, :])):
                link(v.tensor_tensor(prod16, h_tok[:, :, 0:H16], rep(W[3, att], H16), ALU.mult))
                link(v.tensor_reduce(dst, prod16.rearrange("p t (h g) -> p t h g", g=GE), AX, ALU.add))
            link(v.tensor_scalar(has[:, :], seg_size[:, :], 0.0, None, ALU.is_gt))
            link(v.tensor_scalar(start_f[:, :], has[:, :], -1.0, -1.0e9, ALU.add, ALU.mult))
            tmp3 = tuple(tok_split[:, i, :] for i in range(3))
            link(v.tensor_copy(part_f[:, :], seg_base[:, :]))
            split_position(v, link, part_f[:, :], tok_part[:, :], tmp3, part_i[:, :])
            link(v.tensor_tensor(start_f[:, :], start_f[:, :], part_f[:, :], ALU.add))
            link(v.tensor_copy(start_i[:, :], start_f[:, :]))
            link(v.tensor_tensor(start_f[:, :], seg_base[:, :], seg_size[:, :], ALU.add))
            link(v.tensor_scalar(start_f[:, :], start_f[:, :], -1.0, 0.0, ALU.add, ALU.max))
            split_position(v, link, start_f[:, :], part_f[:, :], tmp3, part_i[:, :])
            link(v.tensor_copy(end_i[:, :], start_f[:, :]))
            link(v.tensor_scalar(cont[:, :], part_f[:, :], span[:, 0:1], None, ALU.mult))
            link(v.tensor_tensor(cont[:, :], seg_base[:, :], cont[:, :], ALU.is_lt))
            link(v.tensor_tensor(cont[:, :], cont[:, :], has[:, :], ALU.mult))
            link(v.tensor_scalar(part_f[:, :], part_f[:, :], -1.0, 0.0, ALU.add, ALU.max))
            link(v.tensor_copy(part_i[:, :], part_f[:, :]))
            v.sem_inc(S("s3_tok"), 1)
            link(v.memset(prev_dst[:, :], -1.0))
            v.wait_ge(S("s3_sorted"), 16)
            link(v.memset(src_i[:, EPP:EPP + 2 * WIN], 0))
            link(v.tensor_scalar(src_i[:, 0:EPP], sorted_e[:, :], TOK - 1, None, ALU.bitwise_and))
            link(v.tensor_scalar(dst_i[:, :], sorted_e[:, :], 13, None, ALU.logical_shift_right))
            link(v.tensor_copy(dst_f[:, :], dst_i[:, :]))
            link(v.scalar_tensor_tensor(same[:, :], dst_f[:, :], float(TOK), dst_f[:, :], ALU.is_lt, ALU.mult))
            link(v.tensor_reduce(last_dst[:, 0:1], same[:, :], AX, ALU.max))
            link(v.tensor_copy(last_dst[:, 1:2], last_dst[:, 0:1]))
            v.sem_inc(S("s3_last_dst"), 1)
            link(v.tensor_tensor(same[:, 1:EPP], dst_f[:, 1:EPP], dst_f[:, 0:EPP - 1], ALU.is_equal))
            link(v.tensor_scalar(first_f[:, :], dst_f[:, 0:1], float(TOK - 1), None, ALU.min))
            link(v.tensor_copy(first_i[:, :], first_f[:, :]))
            link(v.tensor_tensor(join[:, 1:2], dst_f[:, 0:1], last_dst[:, 0:1], ALU.is_equal))
            v.wait_ge(S("s3_prev_dst"), 16)
            link(v.tensor_tensor(join[:, 0:1], dst_f[:, 0:1], prev_dst[:, 0:1], ALU.is_equal))
            link(v.memset(same[:, 0:1], 0.0))
            v.sem_inc(S("s3_idx_all"), 1)
            for b in range(2):
                link(v.tensor_copy(idx_ring[:, b, :], src_i[:, b * WIN:(b + 1) * WIN]))
                v.sem_inc(S("s3_idx"), 1)
            v.wait_ge(S("s3_adst"), 16)
            for h in range(HEADS):
                link(v.tensor_tensor_scan(a_dst_e[:, :, h], same[:, :], a_dst_e[:, :, h], 0.0, ALU.mult, ALU.add))
            link(v.memset(runmax[:, 1, :, WIN:WIN + 1], NEG))
            link(v.memset(sums[:, 1, WIN - 1, :], 0.0))

            STEPS = 34

            def window(i, b, first=False):
                g = 2 * i + b
                k = [0]

                def step(ins):
                    k[0] += 1
                    ins.then_inc(S("s3_window"), 1)
                    v.wait_ge(S("s3_window"), g * STEPS + k[0])
                prev = 1 - b
                v.wait_ge(s_gath[b], (i + 1) * (16 * WIN))
                at = bass.ds(g * WIN, WIN)
                step(v.tensor_tensor(z[:, :, :], rows[:, b, :, H16:ROW], a_dst_e[:, at, :], ALU.add))
                zt = z[:, :, :].rearrange("p c h -> p h c")
                step(v.scalar_tensor_tensor(e4[:, :, :], zt, 0.2, zt, ALU.mult, ALU.max))
                step(v.tensor_scalar(restart[:, :], same[:, at], -1.0, -NEG, ALU.add, ALU.mult))
                step(v.tensor_copy(runmax[:, b, :, 0:1], runmax[:, prev, :, WIN:WIN + 1]))
                for h in range(HEADS):
                    step(v.tensor_tensor_scan(runmax[:, b, h, 1:WIN + 1], restart[:, :], e4[:, h, :], runmax[:, prev, h, WIN:WIN + 1], ALU.add, ALU.max))
                step(v.tensor_tensor(expo[:, 0, :, :], runmax[:, b, :, 0:WIN], restart[:, :].unsqueeze(1).broadcast_to([P, HEADS, WIN]), ALU.add))
                step(v.tensor_tensor(expo[:, 0, :, :], expo[:, 0, :, :], runmax[:, b, :, 1:WIN + 1], ALU.subtract))
                step(v.tensor_tensor(expo[:, 1, :, :], e4[:, :, :], runmax[:, b, :, 1:WIN + 1], ALU.subtract))
                v.sem_inc(S("s3_expo"), 1)
                v.wait_ge(S("s3_scale"), g + 1)
                step(v.tensor_tensor(msg[:, :, :, :], rows[:, b, :, 0:H16].rearrange("p c (h t) -> p h t c", t=GE),
                                     scale[:, b, 1, :, :].unsqueeze(2).broadcast_to([P, HEADS, GE, WIN]), ALU.mult))
                if not first:
                    v.wait_ge(s_yout[b], i * 16)
                for f in range(ROW):
                    h = f // GE if f < H16 else f - H16
                    val = msg[:, h, f % GE, :] if f < H16 else scale[:, b, 1, h, :]
                    step(v.tensor_tensor_scan(sums[:, b, :, f], scale[:, b, 0, h, :], val, sums[:, prev, WIN - 1, f:f + 1], ALU.mult, ALU.add))
                step(v.tensor_copy(sums[:, b, :, ROW:ACC].rearrange("p c h -> p h c"), runmax[:, b, :, 1:WIN + 1]))
                step(v.tensor_copy(idx_ring[:, b, :], src_i[:, bass.ds((g + 2) * WIN, WIN)]))
                v.sem_inc(S("s3_sums"), 1)
                v.sem_inc(S("s3_idx"), 1)
                assert k[0] == STEPS, k[0]

            for b in range(2):
                window(0, b, True)
            pairs = pairs_in_use(v)
            with v.Fori(1, NW // 2) as i:
                with v.If(i < pairs):
                    for b in range(2):
                        window(i, b)

            end = sums[:, 1, WIN - 1, :]
            link(v.tensor_copy(last[:, 0, :], end[:, 0:ROW]))
            link(v.tensor_copy(last[:, 1, 0:H16].rearrange("p (h t) -> p h t", t=GE), end[:, ROW:ACC].unsqueeze(2).broadcast_to([P, HEADS, GE])))
            link(v.tensor_copy(last[:, 1, H16:ROW], end[:, ROW:ACC]))
            link(v.tensor_tensor(join[:, 0:1], join[:, 0:1], join[:, 1:2], ALU.mult))
            link(v.tensor_scalar(join[:, 0:1], join[:, 0:1], -1.0, -NEG, ALU.add, ALU.mult))
            link(v.tensor_copy(last[:, 2, :], join[:, 0:1].broadcast_to([P, ROW])))
            v.sem_inc(S("s3_last"), 1)
            v.wait_ge(S("s3_last_t"), 1)
            R = last_t[0:ROW, :, :]
            src = bank[2][0:ROW, :]
            one = slice(1, P + 1)
            link(v.tensor_copy(R[:, 6, one], src[:, 2 * P:3 * P]))
            link(v.tensor_copy(R[:, 7, one], src[:, P:2 * P]))
            link(v.memset(R[:, 0, 0:1], NEG))
            link(v.tensor_tensor_scan(R[:, 0, one], R[:, 6, one], R[:, 7, one], NEG, ALU.add, ALU.max))
            link(v.tensor_tensor(R[:, 1, one], R[:, 0, 0:P], R[:, 6, one], ALU.add))
            link(v.tensor_tensor(R[:, 1, one], R[:, 1, one], R[:, 0, one], ALU.subtract))
            link(v.tensor_tensor(R[:, 5, one], R[:, 7, one], R[:, 0, one], ALU.subtract))
            v.sem_inc(S("s3_across_in"), 1)
            v.wait_ge(S("s3_across_exp"), 2)
            link(v.tensor_tensor(R[:, 3, one], R[:, 3, one], src[:, 0:P], ALU.mult))
            link(v.tensor_tensor_scan(R[:, 4, one], R[:, 2, one], R[:, 3, one], 0.0, ALU.mult, ALU.add))
            v.sem_inc(S("s3_across"), 1)
            v.wait_ge(S("s3_carry_t"), 1)
            link(v.tensor_copy(carry[:, 0:ROW], bank[3][:, 0:ROW]))
            link(v.tensor_copy(carry[:, ROW:ACC], bank[3][:, 32 + H16:32 + ROW]))
            v.sem_inc(S("s3_carry"), 1)

            link(v.tensor_tensor(e_self[:, :, :], h_tok[:, :, H16:ROW], a_dst[:, :, :], ALU.add))
            link(v.scalar_tensor_tensor(e_self[:, :, :], e_self[:, :, :], 0.2, e_self[:, :, :], ALU.mult, ALU.max))
            link(v.tensor_scalar(has[:, :], has[:, :], -1.0, -NEG, ALU.add, ALU.mult))
            link(v.tensor_scalar(cont[:, :], cont[:, :], -1.0, -NEG, ALU.add, ALU.mult))
            v.wait_ge(S("s3_tok_end"), 16 * NT)
            v.wait_ge(S("s3_tok_carry"), 16 * NT)

            def bc4(ap):
                return ap.unsqueeze(2).broadcast_to([P, NT, HEADS])
            link(v.tensor_tensor(wgt[:, 0, :, :], tok_end[:, :, ROW:ACC], bc4(has[:, :]), ALU.add))
            link(v.tensor_tensor(wgt[:, 1, :, :], tok_carry[:, :, ROW:ACC], bc4(cont[:, :]), ALU.add))
            link(v.tensor_tensor(m_all[:, :, :], wgt[:, 0, :, :], wgt[:, 1, :, :], ALU.max))
            link(v.tensor_tensor(m_all[:, :, :], m_all[:, :, :], e_self[:, :, :], ALU.max))
            link(v.tensor_tensor(wgt[:, 0, :, :], wgt[:, 0, :, :], m_all[:, :, :], ALU.subtract))
            link(v.tensor_tensor(wgt[:, 1, :, :], wgt[:, 1, :, :], m_all[:, :, :], ALU.subtract))
            link(v.tensor_tensor(wgt[:, 2, :, :], e_self[:, :, :], m_all[:, :, :], ALU.subtract))
            v.sem_inc(S("s3_merge_in"), 1)
            v.wait_ge(S("s3_merge_exp"), 1)

            def weigh(out, src, w, ones_too=True):
                link(v.tensor_tensor(out[:, :, 0:H16].rearrange("p t (h g) -> p t h g", g=GE), src[:, :, 0:H16].rearrange("p t (h g) -> p t h g", g=GE),
                                     w.unsqueeze(3).broadcast_to([P, NT, HEADS, GE]), ALU.mult))
                if ones_too:
                    link(v.tensor_tensor(out[:, :, H16:ROW], src[:, :, H16:ROW], w, ALU.mult))
                else:
                    link(v.tensor_copy(out[:, :, H16:ROW], w))
            weigh(agg, tok_end, wgt[:, 0, :, :])
            weigh(tmp, tok_carry, wgt[:, 1, :, :])
            link(v.tensor_tensor(agg[:, :, :], agg[:, :, :], tmp[:, :, :], ALU.add))
            weigh(tmp, h_tok, wgt[:, 2, :, :], False)
            link(v.tensor_tensor(agg[:, :, :], agg[:, :, :], tmp[:, :, :], ALU.add))
            den = agg[:, :, H16:ROW]
            link(v.tensor_scalar(den, den, 1e-16, None, ALU.add))
            link(v.reciprocal(den, den))
            A = agg[:, :, 0:H16]
            A4 = A.rearrange("p t (h g) -> p t h g", g=GE)
            link(v.tensor_tensor(A4, A4, den.unsqueeze(3).broadcast_to([P, NT, HEADS, GE]), ALU.mult))
            link(v.tensor_tensor(A, A, rep(W[3, "b_gat"], H16), ALU.add))
            link(v.tensor_reduce(sc1[:, :], A, AX, ALU.add))
            link(v.tensor_scalar(sc1[:, :], sc1[:, :], 1.0 / H16, None, ALU.mult))
            link(v.tensor_tensor(A, A, sc1[:, :].unsqueeze(2).broadcast_to([P, NT, H16]), ALU.subtract))
            T16 = tmp[:, :, 0:H16]
            link(v.tensor_tensor(T16, A, A, ALU.mult))
            link(v.tensor_reduce(sc2[:, :], T16, AX, ALU.add))
            link(v.tensor_scalar(sc2[:, :], sc2[:, :], 1.0 / H16, 1e-5, ALU.mult, ALU.add))
            v.sem_inc(S("s3_score_var"), 1)
            v.wait_ge(S("s3_score_std"), 1)
            link(v.reciprocal(sc2[:, :], sc2[:, :]))
            link(v.tensor_tensor(A, A, sc2[:, :].unsqueeze(2).broadcast_to([P, NT, H16]), ALU.mult))
            link(v.tensor_tensor(A, A, rep(W[3, "ln_gamma"], H16), ALU.mult))
            link(v.tensor_tensor(A, A, rep(W[3, "ln_beta"], H16), ALU.add))
            link(v.tensor_reduce(gates[:, :, 4:8], A.rearrange("p t (h g) -> p t g h", g=GE), AX, ALU.add))
            val = gt[0][:, 0:NT * 4].rearrange("p (t e) -> p t e", e=4)
            link(v.tensor_scalar(val, gates[:, :, 4:8], 1.0 / HEADS, None, ALU.mult))

        def blank_sync(sp):
            pairs = pairs_in_use(sp)
            out_v = sums_d.rearrange("(p j) f -> p j f", p=P)
            blank = packed[:, 0:WIN * ACC].bitcast(F32).rearrange("p (w f) -> p w f", f=ACC)
            with sp.Fori(0, NW // 2) as i:
                with sp.If(i >= pairs - 1):
                    for b in range(2):
                        sp.dma_start(out_v[:, bass.ds((2 * i + b) * WIN, WIN), :], blank).then_inc(S("blank_out"), 16)
            return pairs

        def graph_sync(sp, pairs):
            rows_v = row_d.rearrange("(t p) f -> p t f", p=P)
            sp.wait_ge(S("s3_tok"), 1)
            sp.dma_start(rows_v, h_tok[:, :, :]).then_inc(S("s3_tables"), 16)
            sp.dma_start(adst_d.rearrange("(t p) f -> p t f", p=P), a_dst[:, :, :]).then_inc(S("s3_tables"), 16)
            blanked = sp.value_load(pairs_i[0:1, 1:2], min_val=1, max_val=NW // 2)
            sp.wait_ge(S("blank_out"), blanked * (2 * 16))
            for b in range(2):
                sp.wait_ge(s_sc[b], 8 * EPP)
            lists = sorted_d.rearrange("(p j) t -> p (j t)", p=P)
            sp.dma_start(sorted_e[:, :], lists).then_inc(S("s3_sorted"), 16)
            sp.wait_ge(S("s3_last_dst"), 1)
            sp.dma_start(prev_dst[1:P, :], last_dst[0:P - 1, :]).then_inc(S("s3_prev_dst"), 16)
            sp.wait_ge(S("s3_starts"), 16 * NT)
            sp.dma_start(a_dst_e[:, :, :].rearrange("p j h -> p (j h)"), start_d.rearrange("(p j) h -> p (j h)", p=P)).then_inc(S("s3_starts_in"), 16)
            out_v = sums_d.rearrange("(p j) f -> p j f", p=P)

            with sp.Fori(0, NW // 2) as i:
                with sp.If(i < pairs):
                    for b in range(2):
                        sp.wait_ge(S("s3_sums"), 2 * i + b + 1)
                        sp.dma_start(out_v[:, bass.ds((2 * i + b) * WIN, WIN), :], sums[:, b, :, :]).then_inc(s_yout[b], 16)
            sp.wait_ge(S("s3_carry"), 1)
            sp.dma_start(carry_d, carry[:, :]).then_inc(S("s3_carry_out"), 16)

        def graph_pool(g):
            def at(ap):
                return bass.IndirectOffsetOnAxis(ap=ap, axis=0)
            g.wait_ge(S("s3_tok"), 1)
            for T in range(NT):
                g.indirect_dma_start(out=start_d[:, :], out_offset=at(start_i[:, T:T + 1]), in_=a_dst[:, T, :], in_offset=None,
                                     bounds_check=EDGES - 1, oob_is_err=False).then_inc(S("s3_starts"), 16)
            g.wait_ge(S("s3_tables"), 32)
            g.wait_ge(S("s3_idx_all"), 1)
            g.wait_ge(S("s3_starts_in"), 16)
            g.indirect_dma_start(out=a_dst_e[:, 0, :], out_offset=None, in_=adst_d[:, :], in_offset=at(first_i[:, 0:1])).then_inc(S("s3_adst"), 16)
            pairs = pairs_in_use(g)
            with g.Fori(0, NW // 2) as i:
                with g.If(i < pairs):
                    for b in range(2):
                        g.wait_ge(S("s3_idx"), 2 * i + b + 1)
                        g.sem_inc(S("s3_pool_go"), 1)
                        for c in range(WIN):
                            g.indirect_dma_start(out=rows[:, b, c, :], out_offset=None, in_=row_d[:, :], in_offset=at(idx_ring[:, b, c:c + 1])).then_inc(s_gath[b], 16)
            for b in range(2):
                g.wait_ge(s_yout[b], pairs * 16)
                g.sem_inc(S("s3_pool_go"), 1)
            for T in range(NT):
                g.indirect_dma_start(out=tok_end[:, T, :], out_offset=None, in_=sums_d[:, :], in_offset=at(end_i[:, T:T + 1])).then_inc(S("s3_tok_end"), 16)
            g.wait_ge(S("s3_carry_out"), 16)
            for T in range(NT):
                g.indirect_dma_start(out=tok_carry[:, T, :], out_offset=None, in_=carry_d[:, :], in_offset=at(part_i[:, T:T + 1])).then_inc(S("s3_tok_carry"), 16)

        NQ = GROUP // SUB

        def sort_sync(sp):
            sp.dma_start(edge_i[:, :, :], d["L1_ffn_edge_index"].rearrange("t (p j) -> p t j", p=P)).then_inc(S("sort_edges"), 16)
            sp.wait_ge(S("sort_fill"), 1)
            sp.dma_start(sorted_d.rearrange("(p j) t -> p (j t)", p=P), n_tok[:, 0:NT // 2, :].bitcast(I32).rearrange("p t c -> p (t c)")).then_inc(S("sort_filled"), 16)
            sv = start_d.rearrange("(h p j) f -> h p (j f)", p=P, h=2)
            for h in range(2):
                sp.dma_start(sv[h], x_tok[:, :, :].rearrange("p t c -> p (t c)")).then_inc(S("sort_zeroed"), 16)

        def sort_pool(g):
            g.iota(iota[:, :, :], pattern=[[1, P], [0, SUB]], base=0, channel_multiplier=0, allow_small_or_imprecise_dtypes=True).then_inc(S("c_made"), 1)
            g.iota(iota_p[:, :], pattern=[[0, 1]], base=0, channel_multiplier=1, allow_small_or_imprecise_dtypes=True).then_inc(S("c_made"), 1)
            g.iota(order8[:, :], pattern=[[-1, 8]], base=8, channel_multiplier=0, allow_small_or_imprecise_dtypes=True).then_inc(S("c_made"), 1)
            g.iota(order4[:, :], pattern=[[-1, 4]], base=4, channel_multiplier=0, allow_small_or_imprecise_dtypes=True).then_inc(S("c_made"), 1)
            for t, x in ((ident, 0.0), (ident2, 0.0), (tri, 1.0), (tri_f, 1.0), (ones_f, 1.0), (ones_b, 1.0), (gsel, 1.0)):
                g.memset(t[:, :], x).then_inc(S("c_made"), 1)
            g.memset(sel[:, :, :], 1.0).then_inc(S("c_made"), 1)
            g.wait_ge(S("c_made"), 12)

            def pick(t, op, fill, base, pattern, cm):
                return g.affine_select(out=t, in_=t, compare_op=op, fill=fill, base=base, pattern=pattern, channel_multiplier=cm)
            pick(ident[:, :], ALU.not_equal, 1.0, 0, [[-1, P]], 1).then_inc(S("c_ready"), 1)
            pick(tri[:, :], ALU.is_gt, 0.0, 0, [[1, P]], -1).then_inc(S("c_ready"), 1)
            pick(tri_f[:, :], ALU.is_gt, 0.0, 0, [[1, P]], -1).then_inc(S("c_ready"), 1)
            pick(sel[:, :, :], ALU.is_equal, 0.0, 0, [[1, GROUP], [0, P]], -1).then_inc(S("c_ready"), 1)
            for h in range(2):
                p = slice(h * C, (h + 1) * C)
                pick(ident2[p, :], ALU.not_equal, 1.0, 0, [[-1, C]], 1).then_inc(S("c_ready"), 1)
                pick(gsel[p, :], ALU.is_ge, 0.0, 0, [[-16, 4]], 1).then_inc(S("c_gsel"), 1)
                g.wait_ge(S("c_gsel"), h + 1)
                pick(gsel[p, :], ALU.is_ge, 0.0, 15, [[16, 4]], -1).then_inc(S("c_ready"), 1)
            g.wait_ge(S("sort_filled"), 16)

            def scatter_pair(i, first):
                for b in range(2):
                    at_group = bass.ds((i * 2 + b) * GROUP, GROUP)
                    g.wait_ge(S("sort_pos"), i * 2 + b + 1)
                    g.sem_inc(S("sort_pool_go"), 1)
                    if not first:
                        g.wait_ge(s_sc[b], i * (16 * GROUP))
                        g.sem_inc(S("sort_pool_go"), 1)
                    g.tensor_copy(pos_ring[:, b, :], pos_all[:, at_group]).then_inc(S("sort_rings"), 1)
                    g.tensor_copy(packed_ring[:, b, :], packed[:, at_group]).then_inc(S("sort_rings"), 1)
                    g.wait_ge(S("sort_rings"), (i * 2 + b) * 2 + 2)
                    g.sem_inc(S("sort_pool_go"), 1)
                    for c in range(GROUP):
                        g.indirect_dma_start(out=sorted_d[:, :], out_offset=bass.IndirectOffsetOnAxis(ap=pos_ring[:, b, c:c + 1], axis=0),
                                             in_=packed_ring[:, b, c:c + 1], in_offset=None, bounds_check=EDGES - 1, oob_is_err=False).then_inc(s_sc[b], 16)

            scatter_pair(0, True)
            with g.Fori(1, NG // 2) as i:
                scatter_pair(i, False)

        def sort_scalar(a):
            a.wait_ge(S("sort_base_in"), 1)
            nc.scalar.copy(hist[:, 0, :], H).then_inc(S("sort_hist"), 1)
            with a.Fori(0, EPP // 2) as i:
                for b in range(2):
                    c = i * 2 + b
                    a.wait_ge(S("sort_counted"), c + 1)
                    a.wait_ge(S("sort_ranked_t"), c + 1)
                    nc.scalar.copy(hist[:, (b + 1) % 2, :], H).then_inc(S("sort_hist"), 1)

        def sort_tensor(pe):
            pe.wait_ge(S("c_made"), 12)
            pe.wait_ge(S("sort_fill"), 1)
            nc.tensor.matmul(H, ones_f[:, :], x_tok[:, 0, :], start=True, stop=False, skip_group_check=True)
            with pe.Fori(0, NSUB // 2) as i:
                for b in range(2):
                    pe.wait_ge(S("sort_one1"), i * 2 + b + 1)
                    for c in range(SUB):
                        m = nc.tensor.matmul(H, onehot_lo[:, b, :, c], onehot_hi[:, b, :, c], start=False, stop=False, skip_group_check=True)
                    m.then_inc(S("sort_total_t"), 1)
            pe.wait_ge(S("c_ready"), 8)
            pe.wait_ge(S("sort_total"), 1)
            nc.tensor.matmul(bank[1][:, 0:NT], tri_f[:, :], seg_size[:, :], start=True, stop=True)
            nc.tensor.matmul(bank[1][:, NT:2 * NT], ones_f[:, :], seg_size[:, :], start=True, stop=True).then_inc(S("sort_cums_t"), 1)
            pe.wait_ge(S("sort_base"), 1)
            nc.tensor.matmul(H, ident[:, :], seg_base[:, :], start=True, stop=False, skip_group_check=True).then_inc(S("sort_base_in"), 1)

            def rows_of(gi, b):
                pe.wait_ge(S("sort_ring"), gi + 1)
                nc.tensor.transpose(bank[1][0:GROUP, 0:P], ring_low[:, b, :], ident[:, :]).then_inc(S("sort_rows_t"), 1)
                pe.wait_ge(S("sort_rows"), gi + 1)

            def spread(sub, b, q):
                pe.wait_ge(S("sort_one"), sub)
                for k in range(SUB):
                    m = nc.tensor.matmul(bank[2 + k // 4][:, (k % 4) * P:(k % 4 + 1) * P], sel[:, q * SUB + k, :], lo_rows[:, b, :], start=True, stop=True)
                m.then_inc(S("sort_bc_t"), 1)

            def ranks(sub, q):
                sbuf = q % 2
                pe.wait_ge(S("sort_one"), sub + 1)
                for k in range(SUB):
                    ch = sub * SUB + k
                    R = bank[4 + k % 4][:, 0:NT]
                    pe.wait_ge(S("sort_rank"), ch + 1)
                    nc.tensor.matmul(R, same_before[:, sbuf, k, :], onehot_hi[:, sbuf, :, k], start=True, stop=False)
                    pe.wait_ge(S("sort_hist"), ch + 1)
                    nc.tensor.matmul(H, onehot_lo[:, sbuf, :, k], onehot_hi[:, sbuf, :, k], start=False, stop=False, skip_group_check=True).then_inc(S("sort_counted"), 1)
                    nc.tensor.matmul(R, lo_on_part[:, sbuf, k, :], hist[:, k % 2, :], start=False, stop=True).then_inc(S("sort_ranked_t"), 1)

            def rank_pair(i, more):
                for b in range(2):
                    gi = i * 2 + b
                    for q in range(NQ):
                        sub = gi * NQ + q
                        if q < NQ - 1:
                            spread(sub + 1, b, q + 1)
                        elif b == 0 or more:
                            rows_of(gi + 1, 1 - b)
                            spread(sub + 1, 1 - b, 0)
                        ranks(sub, q)

            pe.sem_inc(S("sort_ranked_t"), 1)
            rows_of(0, 0)
            spread(0, 0, 0)
            with pe.Fori(0, NG // 2 - 1) as i:
                rank_pair(i, True)
            rank_pair(NG // 2 - 1, False)

        def sort_vector(v, link):
            link(v.memset(n_tok[:, 0:NT // 2, :].bitcast(I32), (2 * TOK) << 13))
            link(v.memset(x_tok[:, :, :], 0.0))
            v.sem_inc(S("sort_fill"), 1)
            v.wait_ge(S("c_made"), 12)
            v.wait_ge(S("sort_edges"), 16)
            link(v.tensor_scalar(bits_i[:, 0, :], edge_i[:, 1, :], P - 1, None, ALU.bitwise_and))
            link(v.tensor_scalar(bits_i[:, 1, :], edge_i[:, 1, :], 7, None, ALU.logical_shift_right))

            def groups(ap):
                return ap.rearrange("p (g c) -> p g c", c=GROUP)
            link(v.tensor_copy(low_high[:, :, 0, :], groups(bits_i[:, 0, :])))
            link(v.tensor_copy(low_high[:, :, 1, :], groups(bits_i[:, 1, :])))
            link(v.tensor_scalar(edge_i[:, 0, :], edge_i[:, 0, :], float(TOK - 1), None, ALU.min))
            link(v.tensor_scalar(bits_i[:, 0, :], edge_i[:, 1, :], 13, None, ALU.logical_shift_left))
            link(v.tensor_tensor(packed[:, :], bits_i[:, 0, :], edge_i[:, 0, :], ALU.bitwise_or))

            def onehots(sbuf, rb, q):
                at_sub = slice(q * SUB, (q + 1) * SUB)
                v.tensor_tensor(onehot_lo[:, sbuf, :, :], iota[:, :, :], ring[:, rb, 0, at_sub].unsqueeze(1).broadcast_to([P, P, SUB]), ALU.is_equal)
                return v.tensor_tensor(onehot_hi[:, sbuf, :, :], iota[:, 0:NT, :], ring[:, rb, 1, at_sub].unsqueeze(1).broadcast_to([P, NT, SUB]), ALU.is_equal)
            v.sem_inc(S("sort_total_t"), 2)
            v.sem_inc(S("sort_rank"), 4)
            with v.Fori(0, NG // 2) as i:
                for b in range(2):
                    gi = i * 2 + b
                    v.tensor_copy(ring[:, b, :, :], low_high[:, bass.ds(gi, 1), :, :].rearrange("p o k c -> p (o k) c")).then_inc(S("sort_ring1"), 1)
                    v.wait_ge(S("sort_ring1"), gi + 1)
                    for q in range(NQ):
                        v.wait_ge(S("sort_total_t"), gi * NQ + q + 1)
                        onehots(q % 2, b, q).then_inc(S("sort_one1"), 1)
            v.wait_ge(S("sort_total_t"), NSUB + 2)
            link(v.tensor_copy(seg_size[:, :], H))
            v.sem_inc(S("sort_total"), 1)
            v.wait_ge(S("sort_cums_t"), 1)
            link(v.tensor_tensor_scan(cums[:, :], ones_f[:, 0:NT], bank[1][:, NT:2 * NT], 0.0, ALU.mult, ALU.add))
            link(v.tensor_scalar(limits[:, :], iota[:, 0:NW // 2, 0], float(2 * WIN * P), None, ALU.mult))
            link(v.memset(limits[:, 0:1], -1.0))
            link(v.tensor_scalar(limits[:, :], limits[:, :], cums[:, NT - 1:NT], None, ALU.is_lt))
            link(v.tensor_reduce(span[:, 1:2], limits[:, :], AX, ALU.add))
            link(v.tensor_copy(pairs_i[:, 0:1], span[:, 1:2]))
            link(v.tensor_scalar(span[:, 0:1], span[:, 1:2], -1.0, float(NW // 2 + 1), ALU.mult, ALU.add))
            link(v.tensor_copy(pairs_i[:, 1:2], span[:, 0:1]))
            link(v.tensor_scalar(span[:, 0:1], span[:, 1:2], float(2 * WIN), None, ALU.mult))
            link(v.reciprocal(span[:, 1:2], span[:, 0:1]))
            link(v.tensor_scalar(span[:, 2:3], span[:, 0:1], -1.0, None, ALU.mult))
            link(v.tensor_scalar(span[:, 3:4], span[:, 0:1], -1.0, float(EPP), ALU.mult, ALU.add))
            link(v.tensor_tensor(cums[:, :], cums[:, :], bank[1][:, NT:2 * NT], ALU.subtract))
            link(v.tensor_tensor(seg_base[:, :], cums[:, :], bank[1][:, 0:NT], ALU.add))
            v.sem_inc(S("sort_base"), 1)
            v.wait_ge(S("c_ready"), 8)

            def ring_of(gi, b):
                v.tensor_copy(ring[:, b, :, :], low_high[:, bass.ds(gi, 1), :, :].rearrange("p o k c -> p (o k) c")).then_inc(S("sort_ring_b"), 1)
                v.wait_ge(S("sort_ring_b"), gi + 1)
                v.tensor_copy(ring_low[:, b, :], ring[:, b, 0, :]).then_inc(S("sort_ring"), 1)
                v.wait_ge(S("sort_rows_t"), gi + 1)
                v.tensor_copy(lo_rows[:, b, :], bank[1][0:GROUP, 0:P]).then_inc(S("sort_rows"), 1)

            def make(sub, b, q):
                sbuf = q % 2
                onehots(sbuf, b, q)
                v.wait_ge(S("sort_bc_t"), sub + 1)
                for k in range(SUB):
                    low = bank[2 + k // 4][:, (k % 4) * P:(k % 4 + 1) * P]
                    j = q * SUB + k
                    v.scalar_tensor_tensor(same_before[:, sbuf, k, :], low, ring_low[:, b, j:j + 1], tri[:, :], ALU.is_equal, ALU.mult)
                for t in range(2):
                    m = v.tensor_scalar(lo_on_part[:, sbuf, 4 * t:4 * t + 4, :], bank[2 + t][:, :].rearrange("p (a b) -> p a b", b=P), iota_p[:, 0:1], None, ALU.is_equal)
                m.then_inc(S("sort_one"), 1)

            def read_ranks(sub, b, q):
                for k in range(SUB):
                    j = q * SUB + k
                    v.wait_ge(S("sort_ranked_t"), sub * SUB + k + 2)
                    v.tensor_tensor_reduce(junk[:, k % 4, :], bank[4 + k % 4][:, 0:NT], onehot_hi[:, q % 2, :, k], 1.0, 0.0,
                                           ALU.mult, ALU.add, rank[:, b, j:j + 1]).then_inc(S("sort_rank"), 1)

            def rank_pair(i, more):
                for b in range(2):
                    gi = i * 2 + b
                    for q in range(NQ):
                        sub = gi * NQ + q
                        v.wait_ge(S("sort_rank"), sub * SUB + 4)
                        if q < NQ - 1:
                            make(sub + 1, b, q + 1)
                        elif b == 0 or more:
                            ring_of(gi + 1, 1 - b)
                            make(sub + 1, 1 - b, 0)
                        read_ranks(sub, b, q)
                    k = [0]

                    def step(ins):
                        k[0] += 1
                        ins.then_inc(S("sort_step"), 1)
                        v.wait_ge(S("sort_step"), gi * (SPLIT_STEPS + 1) + k[0])
                    step(v.tensor_scalar(dropped[:, :], ring[:, b, 1, :], float(NT), 1.0e9, ALU.is_ge, ALU.mult))
                    v.wait_ge(S("sort_rank"), (gi + 1) * GROUP + 4)
                    split_position(v, step, rank[:, b, :], split[:, 0, :], (split[:, 1, :], split[:, 2, :], split[:, 3, :]), split_i[:, :])
                    assert k[0] == SPLIT_STEPS + 1
                    v.tensor_tensor(pos_all[:, bass.ds(gi * GROUP, GROUP)], rank[:, b, :], dropped[:, :], ALU.add).then_inc(S("sort_pos"), 1)

            ring_of(0, 0)
            make(0, 0, 0)
            with v.Fori(0, NG // 2 - 1) as i:
                rank_pair(i, True)
            rank_pair(NG // 2 - 1, False)

        def x_tensor(pe):
            pe.wait_ge(S("x_in"), 16)
            pe.wait_ge(S("sort_rank"), EPP + 4)
            pe.wait_ge(S("c_ready"), 8)
            for g in range(8):
                if g >= 2:
                    pe.wait_ge(S("x_copied"), g - 1)
                for t in range(8):
                    T = 8 * g + t
                    m = nc.tensor.transpose(bank[6 + g % 2][:, t * C:(t + 1) * C], n_chan[:, T * P:(T + 1) * P], ident[0:C, 0:C])
                m.then_inc(S("x_t"), 1)

        def x_vector(v):
            v.wait_ge(S("sort_zeroed"), 32)
            for g in range(8):
                v.wait_ge(S("x_t"), g + 1)
                v.tensor_copy(x_tok[:, 8 * g:8 * g + 8, :], bank[6 + g % 2][:, :].rearrange("p (t c) -> p t c", c=C)).then_inc(S("x_copied"), 1)
            v.wait_ge(S("x_copied"), 8)

        SORT = 3 in stages
        block = ctx.enter_context(nc.Block())

        @block.sync
        def _(sp):
            def weights(st):
                if st not in stages:
                    return
                if st - 2 in stages:
                    sp.wait_ge(*done(st - 2))
                for dst, src in loads[st]:
                    sp.dma_start(dst, src).then_inc(S(f"s{st}_weights"), 16)

            sp.dma_start(n_chan[:, :].rearrange("c (b n) -> c b n", b=B), d["x"].rearrange("b c h w -> c b (h w)")).then_inc(S("x_in"), 16)
            sort_sync(sp)
            weights(0)
            weights(1)
            if 3 in stages:
                pairs = blank_sync(sp)
            if 0 in stages:
                sp.wait_ge(S("normed"), at(0, "normed") + 4)
                sp.wait_ge(S("x_copied"), 8)
                for par in range(2):
                    sp.dma_start(n_w[:, :, par, :], n_tok[par * C:(par + 1) * C, :, :]).then_inc(S("s0_rows"), 16)
            weights(2)
            weights(3)
            weights(4)
            if 3 in stages:
                graph_sync(sp, pairs)
            for st in (5, 6, 7):
                weights(st)
            for b in range(B):
                sp.wait_ge(S("out"), 8 * (b + 1))
                sp.dma_start(out.rearrange("b c h w -> c b (h w)")[:, b], n_chan[:, b * TOK // 2:(b + 1) * TOK // 2]).then_inc(S("stored"), 16)
            sp.wait_ge(S("stored"), 32)
            sp.wait_ge(S("sort_zeroed"), 32)

        @block.gpsimd
        def _(g):
            sort_pool(g)
            if 3 in stages:
                graph_pool(g)
            for b in range(2):
                g.wait_ge(s_sc[b], 8 * EPP)

        @block.tensor
        def _(pe):
            sort_tensor(pe)
            x_tensor(pe)
            for st in stages:
                if st == 0:
                    l0_tensor(pe)
                if st in FFN:
                    channels_tensor(pe, st)
                    if st == 3:
                        graph_tensor(pe)
                    ffn_tensor(pe, st)
                if st == 2:
                    channels_tensor(pe, 2)
                    pe.wait_ge(S("s2_weights"), 16 * len(loads[2]))
                    conv_tensor(pe, 2, lambda b, px, py: W[2, "conv"][:, 2 * px + py, :])
                if st == 4:
                    l2_tensor(pe)
                if st == 6:
                    l3_tensor(pe)
            pe.wait_ge(*done(last_stage))
            channels_tensor(pe, 9, src=x_tok, kind="out")

        @block.scalar
        def _(a):
            sort_scalar(a)
            for st in stages:
                ln_scalar(a, st)
                if st == 0:
                    l0_scalar(a)
                if st in FFN:
                    channels_scalar(a, st)
                    if st == 3:
                        graph_scalar(a)
                    ffn_scalar(a, st)
                if st == 2:
                    image_scalar(a, 2, "chan")
                    conv_scalar(a, 2)
                if st == 4:
                    l2_scalar(a)
                if st == 6:
                    l3_scalar(a)
            channels_scalar(a, 9, "out")

        @block.vector
        def _(v):
            chain = [0]

            def link(ins):
                chain[0] += 1
                ins.then_inc(S("vector_chain"), 1)
                v.wait_ge(S("vector_chain"), chain[0])

            sort_vector(v, link)
            x_vector(v)
            for st in stages:
                ln_vector(v, link, st)
                if st == 0:
                    l0_vector(v, link)
                if st in FFN:
                    if st == 3:
                        graph_vector(v, link)
                    ffn_vector(v, link, st)
                if st == 2:
                    v.wait_ge(S("normed"), at(2, "normed") + 4)
                    image_zero(v, link, 2)
                    v.wait_ge(S("s2_weights"), 16 * len(loads[2]))
                    bias_vector(v, link, W[2, "b"])
                    conv_vector(v, link, 2)
                if st == 4:
                    l2_vector(v, link)
                if st == 6:
                    l3_vector(v, link)


def layouts(inputs):
    import numpy as np
    c = np.ascontiguousarray
    d = {}
    for n, a in inputs.items():
        d[n] = np.asarray(a)
    for n in ("L0_ffn", "L1_ffn", "L2_ffn", "L3_ffn"):
        b1, b2, w2 = (d[f"{n}_{x}"] if f"{n}_{x}" in d else d[f"{n}_{x.upper()}"] for x in ("b1", "b2", "w2"))
        if n + "_W1" in d:
            d[n + "_w1"] = d.pop(n + "_W1")
            w2 = d.pop(n + "_W2")
        d[n + "_b1"] = c(b1.reshape(-1, P).T)
        rows = np.zeros((P, b2.size), b2.dtype)
        for r in range(3):
            rows[32 * r] = b2.reshape(-1)
        d[n + "_b2"] = rows
        if w2.shape[1] == 64:
            pairs = np.zeros((w2.shape[0] // 2, P, P), w2.dtype)
            for e in range(2):
                pairs[:, e * 64:(e + 1) * 64, e * 64:(e + 1) * 64] = w2[e::2]
            w2 = pairs
        d[n + "_w2"] = c(w2)
    for n in ("L0_ffn", "L3_ffn"):
        d[n + "_router"] = c(d.pop(n + "_router_w").T)
    d["L2_ffn_router"] = c(d.pop("L2_ffn_Wg"))
    for n in ("att_src", "att_dst"):
        d["L1_ffn_" + n] = c(d["L1_ffn_" + n].reshape(-1))

    def kernel_pairs(taps):
        k = taps.shape[0]
        pairs = (k + 1) // 2
        both = np.zeros((2, taps.shape[2], pairs, pairs, 2) + taps.shape[3:], taps.dtype)
        for y in range(k):
            for x in range(k):
                both[x % 2, :, x // 2, y // 2, y % 2] = taps[y, x]
        return both.reshape((2 * taps.shape[2], pairs * pairs, -1))
    w = d.pop("L1_conv_w").reshape(8, 3, 3, 8, 8)
    full = np.zeros((3, 3, 8, 8, 8, 8), w.dtype)
    for n in range(8):
        for m in range(8):
            full[:, :, :, n, :, m] = w[..., (m - n) % 8].transpose(1, 2, 3, 0)
    d["L1_conv_wk"] = kernel_pairs(full.reshape(3, 3, 64, 64))
    d["L2_qkv_wT"] = c(d.pop("L2_conv_qkv_w").T)
    d["L2_proj_wT"] = c(d.pop("L2_conv_proj_w").T)
    d["L2_dwc_taps"] = kernel_pairs(d.pop("L2_conv_dwc_w")[:, 0].transpose(1, 2, 0)).reshape(P, -1)
    d["L3_dw_taps"] = kernel_pairs(d.pop("L3_conv_dw_weight")[:, 0].transpose(1, 2, 0)).reshape(P, -1)
    d["L3_dk_w1T"] = c(d.pop("L3_conv_dk_w1").T)
    d["L3_cg_w1T"] = c(d.pop("L3_conv_cg_w1").T)
    d["L3_cg_w2T"] = c(d.pop("L3_conv_cg_w2").T)

    def dyn_pairs(a):
        a = a.reshape(4, 7, 7, -1)
        both = np.zeros((4, 2, 4, 4, 2, a.shape[-1]), a.dtype)
        for y in range(7):
            for x in range(7):
                both[:, x % 2, x // 2, y // 2, y % 2] = a[:, y, x]
        return c(both.reshape(8 * TAPS, -1).T)
    d["L3_dk_w2T"] = dyn_pairs(d.pop("L3_conv_dk_w2"))
    d["L3_dk_b2p"] = dyn_pairs(d.pop("L3_conv_dk_b2"))[0]
    return {n: c(a) for n, a in d.items()}


STAGES = (0, 1, 2, 3, 4, 5, 6, 7)


def kernel(**inputs):
    import numpy as np
    import concourse.bacc as bacc
    from concourse.bass_utils import run_bass_kernel_spmd

    nc = bacc.Bacc("TRN2", target_bir_lowering=False, num_devices=1)
    arrays = {"in_" + n: a for n, a in layouts(inputs).items()}
    d = {n[3:]: nc.dram_tensor(n, a.shape, mybir.dt.from_np(a.dtype), kind="ExternalInput").ap() for n, a in arrays.items()}
    out = nc.dram_tensor("out", (B, C, IMG, IMG), F32, kind="ExternalOutput").ap()
    scratch = {n: nc.dram_tensor("scratch_" + n, s, F32, kind="Internal").ap() for n, s in (
        ("start", (EDGES, HEADS)), ("row", (TOK, ROW)), ("adst", (TOK, HEADS)),
        ("sums", (EDGES, ACC)), ("carry", (P, ACC)))}
    scratch["sorted"] = nc.dram_tensor("scratch_sorted", (EDGES, 1), I32, kind="Internal").ap()
    program(nc, d, out, scratch, STAGES)
    r = run_bass_kernel_spmd(nc, [arrays], core_ids=[0])
    return r.results[0]["out"]
```

```python
from contextlib import ExitStack

import concourse.bass as bass
from concourse import mybir

F32 = mybir.dt.float32
I32 = mybir.dt.int32
BF16 = mybir.dt.bfloat16
ALU = mybir.AluOpType
ACT = mybir.ActivationFunctionType
AX = mybir.AxisListType.X

P = 128
B, C, IMG = 2, 64, 64
TOK = B * IMG * IMG
NT = TOK // P
TPB = NT // B
NEG = -1.0e30
EDGES = 262144
EPP = EDGES // P
GROUP = 32
NG = EPP // GROUP
SUB = 8
NSUB = EPP // SUB
WIN = 32
NW = EPP // WIN
HEADS, GE = 4, 4
TAPS = 32
ROW = HEADS * GE + HEADS
ACC = ROW + HEADS


def program(nc, d, out, scratch, stages):
    with ExitStack() as ctx:
        def sb(name, shape, dt=F32, c=ctx):
            return c.enter_context(nc.sbuf_tensor(name, shape, dt))

        def sem(name):
            return ctx.enter_context(nc.semaphore(name))

        bank = [ctx.enter_context(nc.psum_tensor(f"bank{i}", [P, 512], F32)) for i in range(8)]

        x_tok = sb("x_tok", [P, NT, C])
        n_tok = sb("n_tok", [P, NT, C])
        n_chan = sb("n_chan", [C, TOK])
        ident = sb("ident", [P, P])
        ident2 = sb("ident2", [P, C])
        ones_f = sb("ones_f", [P, P])
        ones_b = sb("ones_b", [P, P], BF16)
        gates = sb("gates", [P, NT, 8])
        order8 = sb("order8", [P, 8])
        order4 = sb("order4", [P, 4])
        mean = sb("mean", [P, NT])
        var = sb("var", [P, NT])
        seg_base = sb("seg_base", [P, NT])
        seg_size = sb("seg_size", [P, NT])
        gsel = sb("gsel", [P, 4])
        span = sb("span", [P, 4])
        pairs_i = sb("pairs_i", [P, 2], I32)

        W = {}
        wsize = 4700
        wmem = [sb("weights_even", [P, wsize]), sb("weights_odd", [P, wsize])]
        wpos = [0, 0]

        def wt(stage, name, shape, dt=F32):
            n = 1
            for s in shape[1:]:
                n *= s
            words = n if dt is F32 else (n + 1) // 2
            r = stage % 2
            at = wpos[r]
            wpos[r] += words
            assert wpos[r] <= wsize, (stage, name, wpos[r])
            ap = wmem[r][0:shape[0], at:at + words]
            if dt is not F32:
                ap = ap.bitcast(dt)
            if len(shape) == 3:
                ap = ap.rearrange("p (a b) -> p a b", b=shape[2])
            if len(shape) == 4:
                ap = ap.rearrange("p (a b c) -> p a b c", b=shape[2], c=shape[3])
            W[stage, name] = ap
            return ap

        def bcast_row(ap, n=P):
            return ap.rearrange("(o n) -> o n", o=1).broadcast_to([n, ap.shape[0]])

        loads = {}

        def load(stage, dst, src):
            loads.setdefault(stage, []).append((dst, src))

        FFN = {1: (8, 64, "L0_ffn"), 3: (4, 128, "L1_ffn"), 5: (8, 256, "L2_ffn"), 7: (8, 64, "L3_ffn")}
        for s in range(8):
            wpos[s % 2] = 0
            if s == 0:
                for n in ("Wa", "Wb", "Wg", "Wo"):
                    load(s, wt(s, n, [C, C]), d["L0_conv_" + n])
                for n in ("ba", "bg"):
                    load(s, wt(s, n, [C, 1]), d["L0_conv_" + n].rearrange("(p o) -> p o", o=1))
                bo = wt(s, "bo", [P, 1])
                for h in range(2):
                    load(s, bo[h * C:(h + 1) * C], d["L0_conv_bo"].rearrange("(p o) -> p o", o=1))
                load(s, wt(s, "bb", [C, C]), bcast_row(d["L0_conv_bb"], C))
            if s in FFN:
                E, HD, nm = FFN[s]
                NH = E * HD // P
                w1 = wt(s, "w1", [C, E, HD])
                load(s, w1, d[nm + "_w1"].rearrange("e c h -> c e h"))
                load(s, wt(s, "b1", [P, NH]), d[nm + "_b1"])
                load(s, wt(s, "w2", [P, NH, C]), d[nm + "_w2"].rearrange("(k h) c -> h k c", h=P))
                b2 = wt(s, "b2", [3 * E, C])
                for i in range(3):
                    load(s, b2[i * E:(i + 1) * E], d[nm + "_b2"])
                wt(s, "expert_of", [3 * E, E], F32)
                wt(s, "spread", [3 * E, E * min(HD, P)], BF16)
                if s != 3:
                    load(s, wt(s, "router", [C, E]), d[nm + "_router"])
                if s == 5:
                    load(s, wt(s, "bg", [P, E]), bcast_row(d["L2_ffn_bg"]))
                if s == 3:
                    load(s, wt(s, "w_gat", [C, 16]), d["L1_ffn_W_gat"])
                    for n in ("att_src", "att_dst", "b_gat", "ln_gamma", "ln_beta"):
                        load(s, wt(s, n, [P, 16]), bcast_row(d["L1_ffn_" + n]))
            if s == 2:
                load(s, wt(s, "conv", [P, 4, 2 * C]), d["L1_conv_wk"])
                load(s, wt(s, "b", [P, C]), bcast_row(d["L1_conv_b"]))
            if s == 4:
                load(s, wt(s, "qkv", [C, 192]), d["L2_qkv_wT"])
                load(s, wt(s, "qkv_b", [P, 192]), bcast_row(d["L2_conv_qkv_b"]))
                load(s, wt(s, "norm_w", [P, C]), bcast_row(d["L2_conv_norm_w"]))
                load(s, wt(s, "proj_b", [P, C]), bcast_row(d["L2_conv_proj_b"]))
                pj = wt(s, "proj", [P, C])
                dw = wt(s, "dwc", [P, 9 * 2])
                load(s, dw, d["L2_dwc_taps"])
                for h in range(2):
                    load(s, pj[h * C:(h + 1) * C], d["L2_proj_wT"])
                load(s, wt(s, "dwc_b", [C, 1]), d["L2_conv_dwc_b"].rearrange("(p o) -> p o", o=1))
                wt(s, "conv", [P, 9 * 2, C])
            if s == 6:
                load(s, wt(s, "dw", [P, TAPS]), d["L3_dw_taps"])
                load(s, wt(s, "dk_w1", [C, 16]), d["L3_dk_w1T"])
                load(s, wt(s, "dk_w2", [16, 8 * TAPS]), d["L3_dk_w2T"])
                load(s, wt(s, "cg_w1", [C, 16]), d["L3_cg_w1T"])
                load(s, wt(s, "cg_w2", [16, C]), d["L3_cg_w2T"])
                for n in ("dk_b1", "cg_b1"):
                    load(s, wt(s, n, [16, 1]), d["L3_conv_" + n].rearrange("(p o) -> p o", o=1))
                load(s, wt(s, "dk_b2", [P, 8 * TAPS]), bcast_row(d["L3_dk_b2p"]))
                cb = wt(s, "cg_b2", [P, 1])
                for h in range(2):
                    load(s, cb[h * C:(h + 1) * C], d["L3_conv_cg_b2"].rearrange("(p o) -> p o", o=1))

        def region():
            return ExitStack()

        packed = sb("packed", [P, EPP], I32)
        pos_all = sb("pos_all", [P, EPP], I32)
        packed_ring = sb("packed_ring", [P, 2, GROUP], I32)
        pos_ring = sb("pos_ring", [P, 2, GROUP], I32)
        with region() as r:
            edge_i = sb("edge_i", [P, 2, EPP], I32, r)
            bits_i = sb("bits_i", [P, 2, EPP], I32, r)
            low_high = sb("low_high", [P, NG, 2, GROUP], BF16, r)
            ring = sb("ring", [P, 2, 2, GROUP], BF16, r)
            ring_low = sb("ring_low", [P, 2, GROUP], F32, r)
            onehot_lo = sb("onehot_lo", [P, 2, P, SUB], BF16, r)
            onehot_hi = sb("onehot_hi", [P, 2, NT, SUB], BF16, r)
            lo_on_part = sb("lo_on_part", [P, 2, SUB, P], F32, r)
            same_before = sb("same_before", [P, 2, SUB, P], BF16, r)
            lo_rows = sb("lo_rows", [GROUP, 2, P], BF16, r)
            sel = sb("sel", [GROUP, GROUP, P], BF16, r)
            tri = sb("tri", [P, P], BF16, r)
            tri_f = sb("tri_f", [P, P], F32, r)
            iota = sb("iota", [P, P, SUB], BF16, r)
            iota_p = sb("iota_p", [P, 1], F32, r)
            hist = sb("hist", [P, 2, NT], F32, r)
            cums = sb("cums", [P, NT], F32, r)
            junk = sb("junk", [P, SUB, NT], F32, r)
            rank = sb("rank", [P, 2, GROUP], F32, r)
            dropped = sb("dropped", [P, GROUP], F32, r)
            limits = sb("limits", [P, NW // 2], F32, r)
            split = sb("split", [P, 4, GROUP], F32, r)
            split_i = sb("split_i", [P, GROUP], I32, r)
        with region() as r:
            hsq = sb("hsq", [P, NT, C], F32, r)
        with region() as r:
            a_k = sb("a_k", [C, TOK], F32, r)
            g_l = sb("g_l", [C, TOK], F32, r)
            b_h = sb("b_h", [C, C, C], F32, r)
        with region() as r:
            hid = sb("hid", [P, 2, 16, 512], F32, r)
            gate_parts = sb("gate_parts", [P, NT * 24], F32, r)
            gt = [sb(f"gt{i}", [P, NT * 8], F32, r) for i in range(5)]
            gs = [sb(f"gs{i}", [P, NT], F32, r) for i in range(4)]
        with region() as r:
            image = sb("image", [P, B * 70 * 70], F32, r)
            diag = sb("diag", [P, B, TAPS, C], F32, r)
            pooled = sb("pooled", [C, B], F32, r)
            hid16 = sb("hid16", [16, 2, B], F32, r)
            hid_rep = sb("hid_rep", [16, B, P], F32, r)
            fused = sb("fused", [P, B, TAPS], F32, r)
            dyn = packed[:, 0:B * 4 * TAPS].bitcast(F32).rearrange("p (b n) -> p b n", b=B)
            gate3 = packed[:, B * 4 * TAPS:B * 4 * TAPS + B].bitcast(F32)
        with region() as r:
            sb("image_l2", [P, B * 68 * 68], F32, r)
            v_tok = sb("v_tok", [P, NT, C + 1], F32, r)
            k_tok = sb("k_tok", [P, NT, C], F32, r)
            sq_tok = sb("sq_tok", [P, NT, C], F32, r)
            kv = sb("kv", [C, B, C + 1], F32, r)
            zrec = sb("zrec", [P, NT], F32, r)
            ssq = sb("ssq", [P, 2, NT], F32, r)
        with region() as r:
            src_i = sb("src_i", [P, EPP + 2 * WIN], I32, r)
            same = pos_all[:, :].bitcast(F32)
            a_dst_e = sb("a_dst_e", [P, EPP, HEADS], F32, r)
            idx_ring = sb("idx_ring", [P, 2, WIN], I32, r)
            rows = sb("rows", [P, 2, WIN, ROW], F32, r)
            h_tok = sb("h_tok", [P, NT, ROW], F32, r)
            a_dst = sb("a_dst", [P, NT, HEADS], F32, r)
            has = sb("has", [P, NT], F32, r)
            start_f = sb("start_f", [P, NT], F32, r)
            start_i = sb("start_i", [P, NT], I32, r)
            end_i = sb("end_i", [P, NT], I32, r)
            part_i = sb("part_i", [P, NT], I32, r)
            part_f = sb("part_f", [P, NT], F32, r)
            cont = sb("cont", [P, NT], F32, r)
            first_i = sb("first_i", [P, 1], I32, r)
            first_f = sb("first_f", [P, 1], F32, r)
            last_dst = sb("last_dst", [P, 2], F32, r)
            prev_dst = sb("prev_dst", [P, 2], F32, r)
            tok_split = sb("tok_split", [P, 3, NT], F32, r)
            tok_part = sb("tok_part", [P, NT], F32, r)
            join = sb("join", [P, 2], F32, r)
            last = sb("last", [P, 3, ROW], F32, r)
            last_t = sb("last_t", [ROW, 8, P + 1], F32, r)
            carry = sb("carry", [P, ACC], F32, r)
            with region() as q:
                sorted_e = sb("sorted_e", [P, EPP], I32, q)
                dst_f = sb("dst_f", [P, EPP], F32, q)
                dst_i = packed[:, :]
            with region() as q:
                z = packed[:, HEADS * GE * WIN:HEADS * GE * WIN + WIN * HEADS].bitcast(F32).rearrange("p (w h) -> p w h", w=WIN)
                e4 = sb("e4", [P, HEADS, WIN], F32, q)
                restart = sb("restart", [P, WIN], F32, q)
                runmax = sb("runmax", [P, 2, HEADS, WIN + 1], F32, q)
                expo = sb("expo", [P, 2, HEADS, WIN], F32, q)
                scale = sb("scale", [P, 2, 2, HEADS, WIN], F32, q)
                msg = packed[:, 0:HEADS * GE * WIN].bitcast(F32).rearrange("p (h e w) -> p h e w", h=HEADS, e=GE)
                sums = sb("sums", [P, 2, WIN, ACC], F32, q)
        with region() as r:
            sb("below_tok_end", [P, EPP + 2 * WIN], F32, r)
            tok_end = sb("tok_end", [P, NT, ACC], F32, r)
            tok_carry = sb("tok_carry", [P, NT, ACC], F32, r)
            m_all = sb("m_all", [P, NT, HEADS], F32, r)
            e_self = sb("e_self", [P, NT, HEADS], F32, r)
            wgt = sb("wgt", [P, 3, NT, HEADS], F32, r)
            agg = sb("agg", [P, NT, ROW], F32, r)
            tmp = sb("tmp", [P, NT, ROW], F32, r)
            sc1 = sb("sc1", [P, NT], F32, r)
            sc2 = sb("sc2", [P, NT], F32, r)

        sems = {}

        def S(name):
            if name not in sems:
                sems[name] = sem(name)
            return sems[name]

        s_sc = [sem("s_scattered0"), sem("s_scattered1")]
        s_gath = [sem("s_gathered0"), sem("s_gathered1")]
        s_yout = [sem("s_sums_out0"), sem("s_sums_out1")]
        H = bank[0][:, 0:NT]
        sorted_d, start_d, row_d, adst_d, sums_d, carry_d = (scratch[n] for n in ("sorted", "start", "row", "adst", "sums", "carry"))
        n_w = n_chan[:, :].rearrange("w (t p c) -> w t p c", p=2, c=C)
        MIXERS = (0, 2, 4, 6)
        last_stage = max(stages)

        def steps(st, name):
            if name in ("normed", "centred", "squared", "var", "std"):
                return 4
            if name in ("chan", "chan_t"):
                return 16 if st else 0
            if name in ("y_ready", "y_back", "y_added"):
                return 16 if st else 0
            if name in ("conv", "img"):
                return 16 if st in (2, 4, 6) else 0
            if name == "conv_up":
                return 18 if st in (2, 4, 6) else 0
            if name == "conv_below":
                return B if st in (2, 4, 6) else 0
            if name == "img_zero":
                return int(st in (2, 4, 6))
            if st not in FFN:
                return 0
            if name in ("up", "hid"):
                return 16 * FFN[st][0] * FFN[st][1] // P
            if name in ("down", "gate_rows", "gate_rows_t"):
                return 16
            if name in ("spread", "scaled"):
                return 16 * min(FFN[st][0] * FFN[st][1] // P, FFN[st][0])
            if name == "router":
                return int(st != 3)
            return int(name in ("gate_parts", "ffn_spread", "gate_in", "gate_exp"))

        def at(st, name):
            return sum(steps(e, name) for e in stages if e < st)

        def weights_in(st):
            return S(f"weights_in{st % 2}"), 16 * sum(len(loads[e]) for e in stages if e <= st and e % 2 == st % 2)

        def done(st):
            return S("stage_done"), stages.index(st) + 1

        def ln_vector(v, link, st):
            eps = 1e-6 if st in MIXERS else 1e-5
            Q = 16
            for q in range(4):
                x, m = x_tok[:, q * Q:(q + 1) * Q, :], mean[:, q * Q:(q + 1) * Q]
                link(v.tensor_reduce(m, x, AX, ALU.add))
                link(v.tensor_scalar(m, m, 1.0 / C, None, ALU.mult))
                link(v.tensor_tensor(n_tok[:, q * Q:(q + 1) * Q, :], x, m.unsqueeze(2).broadcast_to([P, Q, C]), ALU.subtract))
                v.sem_inc(S("centred"), 1)
            for q in range(4):
                m = var[:, q * Q:(q + 1) * Q]
                v.wait_ge(S("squared"), at(st, "squared") + q + 1)
                link(v.tensor_reduce(m, hsq[:, q * Q:(q + 1) * Q, :], AX, ALU.add))
                link(v.tensor_scalar(m, m, 1.0 / C, eps, ALU.mult, ALU.add))
                v.sem_inc(S("var"), 1)
            for q in range(4):
                m = var[:, q * Q:(q + 1) * Q]
                n = n_tok[:, q * Q:(q + 1) * Q, :]
                v.wait_ge(S("std"), at(st, "std") + q + 1)
                link(v.reciprocal(m, m))
                v.tensor_tensor(n, n, m.unsqueeze(2).broadcast_to([P, Q, C]), ALU.mult).then_inc(S("normed"), 1)

        def ln_scalar(a, st):
            Q = 16
            for q in range(4):
                a.wait_ge(S("centred"), at(st, "centred") + q + 1)
                nc.scalar.activation(hsq[:, q * Q:(q + 1) * Q, :], n_tok[:, q * Q:(q + 1) * Q, :], ACT.Square).then_inc(S("squared"), 1)
            for q in range(4):
                a.wait_ge(S("var"), at(st, "var") + q + 1)
                m = var[:, q * Q:(q + 1) * Q]
                nc.scalar.activation(m, m, ACT.Sqrt).then_inc(S("std"), 1)

        def channels_tensor(pe, st, src=None, kind="chan"):
            src = n_tok if src is None else src
            for g in range(NT // 4):
                if g % 4 == 0 and kind == "chan":
                    pe.wait_ge(S("normed"), at(st, "normed") + g // 4 + 1)
                if g >= 2:
                    pe.wait_ge(S(kind), at(st, kind) + g - 1)
                for t in range(4):
                    m = nc.tensor.transpose(bank[6 + g % 2][0:C, t * P:(t + 1) * P], src[:, 4 * g + t, :], ident[:, :])
                m.then_inc(S(kind + "_t"), 1)

        def channels_scalar(a, st, kind="chan", bias=None):
            for g in range(NT // 4):
                a.wait_ge(S(kind + "_t"), at(st, kind + "_t") + g + 1)
                dst, src = n_chan[:, g * 512:(g + 1) * 512], bank[6 + g % 2][0:C, :]
                m = nc.scalar.copy(dst, src) if bias is None else nc.scalar.activation(dst, src, ACT.Identity, bias=bias)
                m.then_inc(S(kind), 1)

        rows_b = gt[4][:, :].bitcast(BF16).rearrange("p (s n) -> p s n", s=2)

        def rows_f(n, E):
            return gt[2 + n % 2][0:3 * E, :]

        def y_c(n):
            return gt[n % 2][0:C, :]

        def ffn_tensor(pe, st):
            E, HD, _ = FFN[st]
            NH = E * HD // P
            w1 = W[st, "w1"].rearrange("p e h -> p (e h)")
            pe.wait_ge(*weights_in(st))
            if st != 3:
                for t in range(NT):
                    if t % 4 == 0:
                        pe.wait_ge(S("chan"), at(st, "chan") + t // 4 + 1)
                    m = nc.tensor.matmul(bank[5][:, t * E:(t + 1) * E], n_chan[:, t * P:(t + 1) * P], W[st, "router"], start=True, stop=True)
                m.then_inc(S("router"), 1)

            def up(n):
                pe.wait_ge(S("chan"), at(st, "chan") + n + 1)
                for k in range(NH):
                    i = n * NH + k
                    if i >= 3:
                        pe.wait_ge(S("hid"), at(st, "hid") + i - 2)
                    nc.tensor.matmul(bank[i % 3][:, :], w1[:, k * P:(k + 1) * P], n_chan[:, n * 512:(n + 1) * 512],
                                     start=True, stop=True).then_inc(S("up"), 1)

            def gates_in(n):
                if n == 0:
                    pe.wait_ge(S("gate_parts"), at(st, "gate_parts") + 1)
                else:
                    pe.wait_ge(S("gate_rows"), at(st, "gate_rows") + n)
                parts = gate_parts[:, 0:NT * 3 * E].rearrange("p (t e) -> p t e", e=3 * E)
                for t in range(4):
                    m = nc.tensor.transpose(bank[5][0:3 * E, t * P:(t + 1) * P], parts[:, 4 * n + t, :], ident[:, :])
                m.then_inc(S("gate_rows_t"), 1)

            def spread(n, j):
                i = n * NS + j
                if i >= 2:
                    pe.wait_ge(S("scaled"), at(st, "scaled") + i - 1)
                nc.tensor.matmul(bank[3 + i % 2][:, :], W[st, "spread"][:, j * P:(j + 1) * P], rows_b[0:3 * E, n % 2, :], start=True, stop=True).then_inc(S("spread"), 1)

            def down(n):
                y = bank[6][0:C, :]
                pe.wait_ge(S("gate_rows"), at(st, "gate_rows") + n + 1)
                spread(n, 0)
                if n >= 1:
                    pe.wait_ge(S("y_ready"), at(st, "y_ready") + n)
                nc.tensor.matmul(y, W[st, "b2"], rows_f(n, E), start=True, stop=False)
                for j in range(NS):
                    if j + 1 < NS:
                        spread(n, j + 1)
                    pe.wait_ge(S("scaled"), at(st, "scaled") + n * NS + j + 1)
                    for k in range(j * NH // NS, (j + 1) * NH // NS):
                        m = nc.tensor.matmul(y, W[st, "w2"][:, k, :], hid[:, n % 2, k, :], start=False, stop=(k == NH - 1))
                m.then_inc(S("down"), 1)

            def back(n):
                pe.wait_ge(S("y_ready"), at(st, "y_ready") + n + 1)
                if n >= 1:
                    pe.wait_ge(S("y_added"), at(st, "y_added") + n)
                for t in range(4):
                    m = nc.tensor.transpose(bank[7][:, t * C:(t + 1) * C], y_c(n)[:, t * P:(t + 1) * P], ident[0:C, 0:C])
                m.then_inc(S("y_back"), 1)

            NS = min(NH, E)
            pe.wait_ge(S("ffn_spread"), at(st, "ffn_spread") + 1)
            for n in range(18):
                if n < 16:
                    up(n)
                    gates_in(n)
                if 1 <= n < 17:
                    if n == 1:
                        pe.wait_ge(S("chan"), at(st, "chan") + 16)
                    down(n - 1)
                if n >= 2:
                    back(n - 2)

        def ffn_scalar(a, st):
            E, HD, _ = FFN[st]
            NH = E * HD // P
            a.wait_ge(*weights_in(st))
            gate_scalar(a, st)
            for n in range(16):
                if n >= 2:
                    a.wait_ge(S("down"), at(st, "down") + n - 1)
                for k in range(NH):
                    i = n * NH + k
                    a.wait_ge(S("up"), at(st, "up") + i + 1)
                    nc.scalar.activation(hid[:, n % 2, k, :], bank[i % 3][:, :], ACT.Gelu,
                                         bias=W[st, "b1"][:, k:k + 1]).then_inc(S("hid"), 1)

        def top2(v, link, E, values, order, mask, m1, m2, eq, rest):
            def bc(m):
                return m.unsqueeze(2).broadcast_to([P, NT, E])
            cur = values
            for i, m in enumerate((m1, m2)):
                link(v.tensor_reduce(m, cur, AX, ALU.max))
                link(v.tensor_tensor(eq, cur, bc(m), ALU.is_equal))
                link(v.tensor_tensor(eq, eq, order, ALU.mult))
                link(v.tensor_reduce(gs[3][:, :], eq, AX, ALU.max))
                if i == 0:
                    link(v.tensor_tensor(mask, eq, bc(gs[3][:, :]), ALU.is_equal))
                    link(v.scalar_tensor_tensor(rest, mask, 2 * NEG, cur, ALU.mult, ALU.add))
                    cur = rest
                else:
                    link(v.tensor_tensor(eq, eq, bc(gs[3][:, :]), ALU.is_equal))
                    link(v.tensor_tensor(mask, mask, eq, ALU.add))

        def gate_vector(v, link, st):
            E = FFN[st][0]
            n = NT * E
            val, ex, eq, rest, mask = (g[:, 0:n].rearrange("p (t e) -> p t e", e=E) for g in gt[:5])
            G = gates[:, :, 0:E]
            order = (order8 if E == 8 else order4)[:, :].unsqueeze(1).broadcast_to([P, NT, E])

            def bc(m):
                return m.unsqueeze(2).broadcast_to([P, NT, E])
            m1, m2, m3 = gs[0][:, :], gs[1][:, :], gs[2][:, :]
            logits = bank[5][:, 0:n].rearrange("p (t e) -> p t e", e=E)
            if st in (1, 7):
                v.wait_ge(S("router"), at(st, "router") + 1)
                link(v.tensor_reduce(m1, logits, AX, ALU.max))
                link(v.tensor_tensor(ex, logits, bc(m1), ALU.subtract))
                v.sem_inc(S("gate_in"), 1)
                v.wait_ge(S("gate_exp"), at(st, "gate_exp") + 1)
                link(v.tensor_reduce(m1, ex, AX, ALU.add))
                link(v.reciprocal(m1, m1))
                link(v.tensor_tensor(val, ex, bc(m1), ALU.mult))
                top2(v, link, E, val, order, mask, m1, m2, eq, rest)
                link(v.tensor_tensor(m3, m1, m2, ALU.add))
                link(v.tensor_scalar(m3, m3, 1e-12, None, ALU.max))
                link(v.reciprocal(m3, m3))
                link(v.tensor_tensor(val, val, mask, ALU.mult))
                link(v.tensor_tensor(G, val, bc(m3), ALU.mult))
                return
            if st == 5:
                v.wait_ge(S("router"), at(st, "router") + 1)
                link(v.tensor_tensor(val, logits, W[st, "bg"].unsqueeze(1).broadcast_to([P, NT, E]), ALU.add))
            top2(v, link, E, val, order, mask, m1, m2, eq, rest)
            link(v.tensor_tensor(ex, val, bc(m1), ALU.subtract))
            v.sem_inc(S("gate_in"), 1)
            v.wait_ge(S("gate_exp"), at(st, "gate_exp") + 1)
            link(v.tensor_tensor(ex, ex, mask, ALU.mult))
            link(v.tensor_reduce(m3, ex, AX, ALU.add))
            link(v.reciprocal(m3, m3))
            link(v.tensor_tensor(G, ex, bc(m3), ALU.mult))

        def gate_scalar(a, st):
            E = FFN[st][0]
            ex = gt[1][:, 0:NT * E]
            a.wait_ge(S("gate_in"), at(st, "gate_in") + 1)
            nc.scalar.activation(ex, ex, ACT.Exp).then_inc(S("gate_exp"), 1)

        def ffn_spread(v, link, st):
            E, HD, _ = FFN[st]
            w = min(HD, P)
            expert_of = W[st, "expert_of"]
            r = slice(0, 3 * E)
            link(v.tensor_tensor(expert_of, ident[r, 0:E], ident[r, E:2 * E], ALU.add))
            link(v.tensor_tensor(expert_of, expert_of, ident[r, 2 * E:3 * E], ALU.add))
            v.wait_ge(*weights_in(st))
            link(v.tensor_copy(W[st, "spread"].rearrange("p (e w) -> p e w", w=w), expert_of.unsqueeze(2).broadcast_to([3 * E, E, w])))
            v.sem_inc(S("ffn_spread"), 1)

        def ffn_gate_parts(v, link, st):
            E = FFN[st][0]
            parts = gate_parts[:, 0:NT * 3 * E].rearrange("p (t i e) -> p t i e", i=3, e=E)
            short = gt[4][:, 0:NT * E // 2].bitcast(BF16).rearrange("p (t e) -> p t e", e=E)
            rest = gates[:, :, 0:E]
            for i in range(3):
                link(v.tensor_copy(short, rest))
                link(v.tensor_copy(parts[:, :, i, :], short))
                if i < 2:
                    link(v.tensor_tensor(rest, rest, parts[:, :, i, :], ALU.subtract))
            v.sem_inc(S("gate_parts"), 1)

        def ffn_vector(v, link, st):
            E, HD, _ = FFN[st]
            NH = E * HD // P
            NS = min(NH, E)
            ffn_spread(v, link, st)
            gate_vector(v, link, st)
            ffn_gate_parts(v, link, st)
            if st in (1, 7):
                link(v.tensor_tensor(x_tok[:, :, :], x_tok[:, :, :], n_tok[:, :, :], ALU.add))

            def gate_rows(n):
                v.wait_ge(S("gate_rows_t"), at(st, "gate_rows_t") + n + 1)
                if n >= 2:
                    v.wait_ge(S("down"), at(st, "down") + n - 1)
                v.tensor_copy(rows_f(n, E), bank[5][0:3 * E, :])
                v.tensor_copy(rows_b[0:3 * E, n % 2, :], bank[5][0:3 * E, :]).then_inc(S("gate_rows"), 1)

            def add(n):
                v.wait_ge(S("y_back"), at(st, "y_back") + n + 1)
                x = x_tok[:, 4 * n:4 * n + 4, :]
                v.tensor_tensor(x, x, bank[7][:, 0:4 * C].rearrange("p (t c) -> p t c", c=C), ALU.add).then_inc(S("y_added"), 1)

            gate_rows(0)
            for n in range(16):
                if n < 15:
                    gate_rows(n + 1)
                if n >= 1:
                    if n >= 3:
                        v.wait_ge(S("y_back"), at(st, "y_back") + n - 2)
                    v.wait_ge(S("down"), at(st, "down") + n)
                    v.tensor_copy(y_c(n - 1), bank[6][0:C, :]).then_inc(S("y_ready"), 1)
                for j in range(NS):
                    i = n * NS + j
                    v.wait_ge(S("spread"), at(st, "spread") + i + 1)
                    v.wait_ge(S("hid"), at(st, "hid") + n * NH + (j + 1) * NH // NS)
                    blocks = hid[:, n % 2, j * NH // NS:(j + 1) * NH // NS, :]
                    v.tensor_tensor(blocks, blocks, bank[3 + i % 2][:, :].unsqueeze(1).broadcast_to([P, NH // NS, 512]), ALU.mult).then_inc(S("scaled"), 1)
                if n >= 2:
                    add(n - 2)
            v.wait_ge(S("down"), at(st, "down") + 16)
            v.tensor_copy(y_c(15), bank[6][0:C, :]).then_inc(S("y_ready"), 1)
            add(14)
            add(15)
            v.wait_ge(S("y_added"), at(st, "y_added") + 16)
            v.sem_inc(done(st)[0], 1)

        def conv_pad(st):
            return {2: 1, 4: 2, 6: 3}[st]

        def img(st):
            side = IMG + 2 * conv_pad(st)
            return image[:, 0:B * side * side].rearrange("p (b r w) -> p b r w", b=B, w=side)

        def conv_memory(st):
            if st == 2:
                mem = diag[0:C, :, :, :].rearrange("p b n c -> p (b n c)")
                upper, y = mem[:, 0:2048], mem[:, 2048:3072]
            else:
                upper, y = packed[0:C, 0:2048].bitcast(F32), pos_all[0:C, 0:1024].bitcast(F32)
            return upper.rearrange("p (s n) -> p s n", s=4), y.rearrange("p (s n) -> p s n", s=2)

        def image_zero(v, link, st):
            p, im = conv_pad(st), img(st)
            link(v.memset(im[:, :, 0:p, :], 0.0))
            link(v.memset(im[:, :, p + IMG:, :], 0.0))
            link(v.memset(im[0:C, :, :, 0:p], 0.0))
            link(v.memset(im[0:C, :, :, p + IMG:], 0.0))
            if p > 1:
                link(v.memset(im[C:P, :, :, 0:p - 1], 0.0))
            link(v.memset(im[C:P, :, :, p - 1 + IMG:], 0.0))
            v.sem_inc(S("img_zero"), 1)

        def image_scalar(a, st, kind):
            p = conv_pad(st)
            a.wait_ge(S("img_zero"), at(st, "img_zero") + 1)
            for g in range(NT // 4):
                b, t = divmod(g, 8)
                a.wait_ge(S(kind + "_t"), at(st, kind + "_t") + g + 1)
                nc.scalar.copy(img(st)[0:C, b, p + 8 * t:p + 8 * t + 8, p:p + IMG],
                               bank[6 + g % 2][0:C, :].rearrange("c (r w) -> c r w", w=IMG)).then_inc(S(kind), 1)

        def image_vector(v, st, kind):
            p = conv_pad(st)
            for g in range(NT // 4):
                b, t = divmod(g, 8)
                v.wait_ge(S(kind), at(st, kind) + g + 1)
                rows8 = slice(p + 8 * t, p + 8 * t + 8)
                v.tensor_copy(img(st)[C:P, b, rows8, p - 1:p - 1 + IMG], img(st)[0:C, b, rows8, p:p + IMG]).then_inc(S("img"), 1)

        def conv_tensor(pe, st, weights):
            p = conv_pad(st)
            pairs = p + 1

            def window(b, r, n, px, py):
                return img(st)[:, b, r + 2 * py:r + 2 * py + n, 2 * px:2 * px + IMG]

            def back(g):
                pe.wait_ge(S("y_ready"), at(st, "y_ready") + g + 1)
                if g >= 2:
                    pe.wait_ge(S("y_added"), at(st, "y_added") + g - 1)
                for t in range(4):
                    m = nc.tensor.transpose(bank[3 + g % 2][:, t * C:(t + 1) * C], conv_memory(st)[1][:, g % 2, t * P:(t + 1) * P], ident[0:C, 0:C])
                m.then_inc(S("y_back"), 1)

            for g in range(NT // 4):
                b, t = divmod(g, 8)
                pe.wait_ge(S("img"), at(st, "img") + 8 * b + min(8, t + 2))
                if g >= 3:
                    pe.wait_ge(S("y_ready"), at(st, "y_ready") + g - 2)
                    pe.wait_ge(S("conv_up"), at(st, "conv_up") + 9 * ((g - 3) // 8) + (g - 3) % 8 + 1)
                for n in range(pairs * pairs):
                    px, py = divmod(n, pairs)
                    m = nc.tensor.matmul(bank[g % 3][:, :], weights(b, px, py), window(b, 8 * t, 8, px, py), start=(n == 0), stop=(n == pairs * pairs - 1))
                m.then_inc(S("conv"), 1)
                if t == 7:
                    for n in range(pairs * p):
                        px, py = divmod(n, p)
                        m = nc.tensor.matmul(bank[5][0:C, b * C:(b + 1) * C], weights(b, px, py)[:, C:P], window(b, IMG, 1, px, py),
                                             start=(n == 0), stop=(n == pairs * p - 1))
                    m.then_inc(S("conv_below"), 1)
                if g >= 2:
                    back(g - 2)
            back(NT // 4 - 2)
            back(NT // 4 - 1)

        def conv_scalar(a, st):
            upper = conv_memory(st)[0]
            for i in range(9 * B):
                b, t = divmod(i, 9)
                if st == 4:
                    features_scalar(a, i)
                if i >= 4:
                    pb, pt = divmod(i - 4, 9)
                    a.wait_ge(S("y_ready"), at(st, "y_ready") + 8 * pb + min(pt + 1, 8))
                if t < 8:
                    g = 8 * b + t
                    a.wait_ge(S("conv"), at(st, "conv") + g + 1)
                    nc.scalar.copy(upper[:, i % 4, :], bank[g % 3][C:P, :]).then_inc(S("conv_up"), 1)
                else:
                    a.wait_ge(S("conv_below"), at(st, "conv_below") + b + 1)
                    nc.scalar.copy(upper[:, i % 4, 0:IMG], bank[5][0:C, b * C:(b + 1) * C]).then_inc(S("conv_up"), 1)

        def conv_vector(v, link, st, kind="chan"):
            upper, y = conv_memory(st)
            image_vector(v, st, kind)

            def add(g):
                v.wait_ge(S("y_back"), at(st, "y_back") + g + 1)
                x = x_tok[:, 4 * g:4 * g + 4, :]
                v.tensor_tensor(x, x, bank[3 + g % 2][:, 0:4 * C].rearrange("p (t c) -> p t c", c=C), ALU.add).then_inc(S("y_added"), 1)

            for g in range(NT // 4):
                b, t = divmod(g, 8)
                i = 9 * b + t
                if st == 4:
                    features_vector(v, link, g)
                v.wait_ge(S("conv"), at(st, "conv") + g + 1)
                v.wait_ge(S("conv_up"), at(st, "conv_up") + i + 2)
                if g >= 2:
                    v.wait_ge(S("y_back"), at(st, "y_back") + g - 1)
                low = bank[g % 3][0:C, :]
                v.tensor_tensor(y[:, g % 2, 0:7 * IMG], low[:, 0:7 * IMG], upper[:, i % 4, IMG:8 * IMG], ALU.add)
                v.tensor_tensor(y[:, g % 2, 7 * IMG:8 * IMG], low[:, 7 * IMG:8 * IMG], upper[:, (i + 1) % 4, 0:IMG], ALU.add).then_inc(S("y_ready"), 1)
                if g >= 1:
                    add(g - 1)
            add(NT // 4 - 1)
            v.wait_ge(S("y_added"), at(st, "y_added") + NT // 4)
            if st != 4:
                v.sem_inc(done(st)[0], 1)

        def bias_vector(v, link, bias):
            link(v.tensor_tensor(x_tok[:, :, :], x_tok[:, :, :], bias.unsqueeze(1).broadcast_to([P, NT, C]), ALU.add))

        def l0_tensor(pe):
            pe.wait_ge(*weights_in(0))
            pe.wait_ge(S("s0_rows"), 32)
            rows_w = n_chan
            for j in range(16):
                if j >= 2:
                    pe.wait_ge(S("s0_a"), j - 1)
                    pe.wait_ge(S("s0_g"), j - 1)
                nc.tensor.matmul(bank[j % 2][0:C, :], W[0, "Wa"], rows_w[:, j * 512:(j + 1) * 512], start=True, stop=True).then_inc(S("s0_a_t"), 1)
                nc.tensor.matmul(bank[2 + j % 2][0:C, :], W[0, "Wg"], rows_w[:, j * 512:(j + 1) * 512], start=True, stop=True).then_inc(S("s0_g_t"), 1)
            ak = a_k[:, :].rearrange("k (b h c) -> k b h c", b=B, c=C)
            for b in range(B):
                for g in range(8 * b, 8 * b + 8):
                    c0 = (g % 8) * 8
                    if g >= 2:
                        pe.wait_ge(S("s0_b"), g - 1)
                    for i in range(8):
                        lhs = n_w[:, b * TPB:(b + 1) * TPB, :, c0 + i].rearrange("w t p -> w (t p)")
                        m = nc.tensor.matmul(bank[4 + g % 2][0:C, i * C:(i + 1) * C], lhs, W[0, "Wb"], start=True, stop=True)
                    m.then_inc(S("s0_b_t"), 1)
                pe.wait_ge(S("s0_a"), 16)
                for g in range(8 * b, 8 * b + 8):
                    c0 = (g % 8) * 8
                    pe.wait_ge(S("s0_b"), g + 1)
                    if g >= 2:
                        pe.wait_ge(S("s0_gab"), g - 1)
                    for i in range(8):
                        m = nc.tensor.matmul(bank[6 + g % 2][0:C, i * C:(i + 1) * C], b_h[:, c0 + i, :], ak[:, b, :, c0 + i], start=True, stop=True)
                    m.then_inc(S("s0_ab_t"), 1)
            gl = g_l[:, :].rearrange("l (t p c) -> l t p c", p=2, c=C)
            for m8 in range(8):
                pe.wait_ge(S("s0_gab"), 8 if m8 < 4 else 16)
                if m8 >= 2:
                    pe.wait_ge(S("s0_out"), m8 - 1)
                for par in range(2):
                    m = nc.tensor.matmul(bank[m8 % 2][par * C:(par + 1) * C, :], W[0, "Wo"], gl[:, m8 * 8:(m8 + 1) * 8, par, :], start=True, stop=True)
                m.then_inc(S("s0_out_t"), 1)

        def l0_scalar(a):
            a.wait_ge(*weights_in(0))
            for j in range(16):
                a.wait_ge(S("s0_g_t"), j + 1)
                nc.scalar.activation(g_l[:, j * 512:(j + 1) * 512], bank[2 + j % 2][0:C, :], ACT.Sigmoid, bias=W[0, "bg"]).then_inc(S("s0_g"), 1)

        def l0_vector(v, link):
            v.wait_ge(*weights_in(0))
            for j in range(16):
                v.wait_ge(S("s0_a_t"), j + 1)
                v.tensor_scalar(a_k[:, j * 512:(j + 1) * 512], bank[j % 2][0:C, :], W[0, "ba"], None, ALU.add).then_inc(S("s0_a"), 1)
            gl = g_l[:, :].rearrange("l (b h c) -> l b h c", b=B, c=C)
            for b in range(B):
                for g in range(8 * b, 8 * b + 8):
                    c0 = (g % 8) * 8
                    v.wait_ge(S("s0_b_t"), g + 1)
                    if b:
                        v.wait_ge(S("s0_ab_t"), g - 7)
                    v.tensor_tensor(b_h[:, c0:c0 + 8, :], bank[4 + g % 2][0:C, :].rearrange("p (i l) -> p i l", l=C),
                                    W[0, "bb"].unsqueeze(1).broadcast_to([C, 8, C]), ALU.add).then_inc(S("s0_b"), 1)
                v.wait_ge(S("s0_g"), 16)
                for g in range(8 * b, 8 * b + 8):
                    c0 = (g % 8) * 8
                    v.wait_ge(S("s0_ab_t"), g + 1)
                    dst = gl[:, b, :, c0:c0 + 8]
                    v.tensor_tensor(dst, dst, bank[6 + g % 2][0:C, :].rearrange("l (c j) -> l j c", j=C), ALU.mult).then_inc(S("s0_gab"), 1)
            for m8 in range(8):
                v.wait_ge(S("s0_out_t"), m8 + 1)
                x = x_tok[:, m8 * 8:(m8 + 1) * 8, :]
                v.scalar_tensor_tensor(x, bank[m8 % 2][:, :].rearrange("p (t c) -> p t c", c=C), W[0, "bo"], x, ALU.add, ALU.add).then_inc(S("s0_out"), 1)
            v.wait_ge(S("s0_out"), 8)
            v.sem_inc(done(0)[0], 1)

        def l2_tensor(pe):
            channels_tensor(pe, 4)
            pe.wait_ge(*weights_in(4))
            for g in range(NT // 2):
                pe.wait_ge(S("chan"), at(4, "chan") + g // 2 + 1)
                if g >= 2:
                    pe.wait_ge(S("s4_qkv"), g - 1)
                for t in range(2):
                    T = 2 * g + t
                    m = nc.tensor.matmul(bank[g % 2][:, t * 192:(t + 1) * 192], n_chan[:, T * P:(T + 1) * P], W[4, "qkv"], start=True, stop=True)
                m.then_inc(S("s4_qkv_t"), 1)
            pe.wait_ge(S("s4_qkv"), NT // 2)
            channels_tensor(pe, 4, src=v_tok[:, :, 0:C], kind="vchan")
            pe.wait_ge(S("s4_conv_w"), 1)
            conv_tensor(pe, 4, lambda b, px, py: W[4, "conv"][:, 2 * (3 * px + py):2 * (3 * px + py) + 2, :].rearrange("p h c -> p (h c)"))
            pe.wait_ge(S("s4_k"), 2)
            for b in range(B):
                for t in range(TPB):
                    T = b * TPB + t
                    m = nc.tensor.matmul(bank[2][0:C, b * 128:b * 128 + C + 1], k_tok[:, T, :], v_tok[:, T, :], start=(t == 0), stop=(t == TPB - 1))
            m.then_inc(S("s4_kv_t"), 1)
            pe.wait_ge(S("s4_q"), 2)
            channels_tensor(pe, 4, kind="qchan")
            pe.wait_ge(S("s4_kv"), 1)
            for g in range(NT // 4):
                pe.wait_ge(S("qchan"), g + 1)
                if g >= 2:
                    pe.wait_ge(S("s4_att"), g - 1)
                for t in range(4):
                    T = 4 * g + t
                    m = nc.tensor.matmul(bank[g % 2][:, t * 128:t * 128 + C + 1], n_chan[:, T * P:(T + 1) * P], kv[:, T // TPB, :], start=True, stop=True)
                m.then_inc(S("s4_att_t"), 1)
            pe.wait_ge(S("s4_att_done"), 1)
            channels_tensor(pe, 4, src=k_tok, kind="attchan")
            for g in range(NT // 8):
                pe.wait_ge(S("attchan"), 2 * g + 2)
                if g >= 2:
                    pe.wait_ge(S("s4_proj"), g - 1)
                for t in range(8):
                    T = 8 * g + t
                    m = nc.tensor.matmul(bank[3 + g % 2][:, t * C:(t + 1) * C], n_chan[:, T * P:(T + 1) * P], W[4, "proj"][0:C], start=True, stop=True)
                m.then_inc(S("s4_proj_t"), 1)

        FEATURES = [(kind, b) for kind in ("k", "q") for b in range(B)]

        def feature(j):
            kind, b = FEATURES[j]
            part = slice(b * TPB, (b + 1) * TPB)
            return kind, b, (k_tok if kind == "k" else n_tok)[:, part, :], sq_tok[:, part, :], ssq[:, int(kind == "q"), part]

        def features_scalar(a, i):
            if i < 4:
                kind, b, t, u, _ = feature(i)
                a.wait_ge(S(f"s4_{kind}_relu"), b + 1)
                nc.scalar.activation(t, t, ACT.Square).then_inc(S("s4_sq_a"), 1)
                a.wait_ge(S("s4_sq_a"), i + 1)
                if kind == "q":
                    a.wait_ge(S("s4_k_ssq"), b + 1)
                nc.scalar.activation(u, t, ACT.Square).then_inc(S(f"s4_{kind}_sq"), 1)
            if 3 <= i < 7:
                kind, b, _, _, w = feature(i - 3)
                a.wait_ge(S(f"s4_{kind}_ssq"), b + 1)
                nc.scalar.activation(w, w, ACT.Sqrt).then_inc(S(f"s4_{kind}_norm"), 1)

        def features_vector(v, link, g):
            if 1 <= g < 5:
                kind, b, _, u, w = feature(g - 1)
                v.wait_ge(S(f"s4_{kind}_sq"), b + 1)
                link(v.tensor_reduce(w, u, AX, ALU.add))
                v.sem_inc(S(f"s4_{kind}_ssq"), 1)
            if 4 <= g < 8:
                kind, b, t, _, w = feature(g - 4)
                v.wait_ge(S(f"s4_{kind}_norm"), b + 1)
                link(v.tensor_scalar(w, w, 1e-12, None, ALU.max))
                link(v.reciprocal(w, w))
                link(v.tensor_tensor(t, t, w.unsqueeze(2).broadcast_to([P, TPB, C]), ALU.mult))
                v.sem_inc(S(f"s4_{kind}"), 1)

        def l2_scalar(a):
            channels_scalar(a, 4)
            image_scalar(a, 4, "vchan")
            conv_scalar(a, 4)
            channels_scalar(a, 4, "qchan")
            a.wait_ge(S("s4_att"), 16)
            nc.scalar.activation(n_tok[:, :, :], k_tok[:, :, :], ACT.Square).then_inc(S("s4_att_sq"), 1)
            a.wait_ge(S("s4_att_ms"), 1)
            nc.scalar.activation(ssq[:, 1, :], ssq[:, 1, :], ACT.Sqrt).then_inc(S("s4_att_rms"), 1)
            a.wait_ge(*weights_in(4))
            channels_scalar(a, 4, "attchan", W[4, "dwc_b"])

        def l2_vector(v, link):
            bias = W[4, "qkv_b"].unsqueeze(1).broadcast_to([P, 2, 192])
            v.wait_ge(*weights_in(4))
            link(v.memset(v_tok[:, :, C:C + 1], 1.0))
            link(v.tensor_tensor(W[4, "conv"], W[4, "proj"].unsqueeze(1).broadcast_to([P, 18, C]),
                                 W[4, "dwc"].unsqueeze(2).broadcast_to([P, 18, C]), ALU.mult))
            v.sem_inc(S("s4_conv_w"), 1)
            image_zero(v, link, 4)
            for g in range(NT // 2):
                v.wait_ge(S("s4_qkv_t"), g + 1)
                src = bank[g % 2][:, 0:384].rearrange("p (t c) -> p t c", c=192)
                for i, x in enumerate((n_tok, k_tok, v_tok)):
                    m = v.tensor_tensor(x[:, 2 * g:2 * g + 2, 0:C], src[:, :, i * C:(i + 1) * C], bias[:, :, i * C:(i + 1) * C], ALU.add)
                m.then_inc(S("s4_qkv"), 1)
            v.wait_ge(S("s4_qkv"), NT // 2)
            for kind, b in FEATURES:
                t = (k_tok if kind == "k" else n_tok)[:, b * TPB:(b + 1) * TPB, :]
                v.tensor_scalar(t, t, 0.0, 1e-5, ALU.max, ALU.add).then_inc(S(f"s4_{kind}_relu"), 1)
            conv_vector(v, link, 4, "vchan")
            v.wait_ge(S("s4_kv_t"), 1)
            link(v.tensor_scalar(kv[:, :, :], bank[2][0:C, 0:256].rearrange("p (b c) -> p b c", b=B)[:, :, 0:C + 1], 1.0 / (IMG * IMG), None, ALU.mult))
            v.sem_inc(S("s4_kv"), 1)
            for g in range(NT // 4):
                v.wait_ge(S("s4_att_t"), g + 1)
                src = bank[g % 2][:, :].rearrange("p (t c) -> p t c", c=128)
                w = zrec[:, 4 * g:4 * g + 4]
                link(v.tensor_scalar(w, src[:, :, C], 1e-5, None, ALU.add))
                link(v.reciprocal(w, w))
                v.tensor_tensor(k_tok[:, 4 * g:4 * g + 4, :], src[:, :, 0:C], w.unsqueeze(2).broadcast_to([P, 4, C]), ALU.mult).then_inc(S("s4_att"), 1)
            w = ssq[:, 1, :]
            v.wait_ge(S("s4_att_sq"), 1)
            link(v.tensor_reduce(w, n_tok[:, :, :], AX, ALU.add))
            link(v.tensor_scalar(w, w, 1.0 / C, 1e-5, ALU.mult, ALU.add))
            v.sem_inc(S("s4_att_ms"), 1)
            v.wait_ge(S("s4_att_rms"), 1)
            link(v.reciprocal(w, w))
            link(v.tensor_tensor(k_tok[:, :, :], k_tok[:, :, :], w.unsqueeze(2).broadcast_to([P, NT, C]), ALU.mult))
            link(v.tensor_tensor(k_tok[:, :, :], k_tok[:, :, :], W[4, "norm_w"].unsqueeze(1).broadcast_to([P, NT, C]), ALU.mult))
            v.sem_inc(S("s4_att_done"), 1)
            bias_vector(v, link, W[4, "proj_b"])
            for g in range(NT // 8):
                v.wait_ge(S("s4_proj_t"), g + 1)
                x = x_tok[:, 8 * g:8 * g + 8, :]
                v.tensor_tensor(x, x, bank[3 + g % 2][:, :].rearrange("p (t c) -> p t c", c=C), ALU.add).then_inc(S("s4_proj"), 1)
            v.wait_ge(S("s4_proj"), 8)
            v.sem_inc(done(4)[0], 1)

        def l3_tensor(pe):
            pe.wait_ge(S("normed"), at(6, "normed") + 4)
            for b in range(B):
                for t in range(TPB):
                    m = nc.tensor.matmul(bank[2][0:C, b:b + 1], n_tok[:, b * TPB + t, :], ones_f[:, 0:1], start=(t == 0), stop=(t == TPB - 1))
            m.then_inc(S("s6_pool_t"), 1)
            pe.wait_ge(*weights_in(6))
            pe.wait_ge(S("s6_pool"), 1)
            nc.tensor.matmul(bank[3][0:16, 0:B], W[6, "dk_w1"], pooled[:, :], start=True, stop=True)
            nc.tensor.matmul(bank[3][0:16, B:2 * B], W[6, "cg_w1"], pooled[:, :], start=True, stop=True).then_inc(S("s6_hid_t"), 1)
            pe.wait_ge(S("s6_hidden"), 2)
            for h in range(2):
                m = nc.tensor.matmul(bank[4][h * C:(h + 1) * C, 0:B], W[6, "cg_w2"], hid16[:, 1, :], start=True, stop=True)
            m.then_inc(S("s6_gate_t"), 1)
            pe.wait_ge(S("s6_rep"), 1)
            for b in range(B):
                m = nc.tensor.matmul(bank[5][:, b * 8 * TAPS:(b + 1) * 8 * TAPS], hid_rep[:, b, :], W[6, "dk_w2"], start=True, stop=True)
            m.then_inc(S("s6_dyn_t"), 1)
            channels_tensor(pe, 6)
            pe.wait_ge(S("s6_diag"), 1)
            conv_tensor(pe, 6, lambda b, px, py: diag[:, b, 2 * (4 * px + py):2 * (4 * px + py) + 2, :].rearrange("p h c -> p (h c)"))

        def l3_scalar(a):
            a.wait_ge(*weights_in(6))
            a.wait_ge(S("s6_hid_t"), 1)
            for i, n in enumerate(("dk_b1", "cg_b1")):
                nc.scalar.activation(hid16[:, i, :], bank[3][0:16, i * B:(i + 1) * B], ACT.Gelu, bias=W[6, n]).then_inc(S("s6_hidden"), 1)
            a.wait_ge(S("s6_gate_t"), 1)
            nc.scalar.activation(gate3[:, :], bank[4][:, 0:B], ACT.Sigmoid, bias=W[6, "cg_b2"]).then_inc(S("s6_gate"), 1)
            image_scalar(a, 6, "chan")
            conv_scalar(a, 6)

        def l3_vector(v, link):
            v.wait_ge(S("s6_pool_t"), 1)
            link(v.tensor_scalar(pooled[:, :], bank[2][0:C, 0:B], 1.0 / (IMG * IMG), None, ALU.mult))
            v.sem_inc(S("s6_pool"), 1)
            image_zero(v, link, 6)
            v.wait_ge(S("s6_hidden"), 2)
            link(v.tensor_copy(hid_rep[:, :, :], hid16[:, 0, :].unsqueeze(2).broadcast_to([16, B, P])))
            v.sem_inc(S("s6_rep"), 1)
            v.wait_ge(*weights_in(6))
            v.wait_ge(S("s6_dyn_t"), 1)
            v.wait_ge(S("s6_gate"), 1)
            for h in range(2):
                p = slice(h * C, (h + 1) * C)
                src = bank[5][p, :].rearrange("p (b g h n) -> p b g h n", b=B, g=4, h=2)
                b2 = W[6, "dk_b2"][p].rearrange("p (g h n) -> p g h n", g=4, h=2)
                for b in range(B):
                    f = fused[p, b, :]
                    d4 = dyn[p, b, :].rearrange("p (g n) -> p g n", g=4)
                    link(v.tensor_tensor(d4, src[:, b, :, h, :], b2[:, :, h, :], ALU.add))
                    for g in range(4):
                        link(v.scalar_tensor_tensor(f, d4[:, g, :], gsel[p, g:g + 1], W[6, "dw"][p] if g == 0 else f, ALU.mult, ALU.add))
                    link(v.tensor_scalar(f, f, gate3[p, b:b + 1], None, ALU.mult))
            for b in range(B):
                link(v.tensor_tensor(diag[:, b, :, :], ident2[:, :].unsqueeze(1).broadcast_to([P, TAPS, C]),
                                     fused[:, b, :].unsqueeze(2).broadcast_to([P, TAPS, C]), ALU.mult))
            v.sem_inc(S("s6_diag"), 1)
            conv_vector(v, link, 6)

        SPLIT_STEPS = 10

        def split_position(v, step, pos, part, tmp, tmp_i):
            quot, rest, off = tmp
            step(v.tensor_scalar(quot, pos, span[:, 1:2], None, ALU.mult))
            step(v.tensor_copy(tmp_i, quot))
            step(v.tensor_copy(part, tmp_i))
            step(v.scalar_tensor_tensor(rest, part, span[:, 2:3], pos, ALU.mult, ALU.add))
            step(v.tensor_scalar(off, rest, 0.0, None, ALU.is_lt))
            step(v.tensor_tensor(part, part, off, ALU.subtract))
            step(v.scalar_tensor_tensor(rest, off, span[:, 0:1], rest, ALU.mult, ALU.add))
            step(v.tensor_scalar(off, rest, span[:, 0:1], None, ALU.is_ge))
            step(v.tensor_tensor(part, part, off, ALU.add))
            step(v.scalar_tensor_tensor(pos, part, span[:, 3:4], pos, ALU.mult, ALU.add))

        def pairs_in_use(eng):
            eng.wait_ge(S("sort_base"), 1)
            return eng.value_load(pairs_i[0:1, 0:1], min_val=1, max_val=NW // 2)

        def graph_tensor(pe):
            pe.wait_ge(*weights_in(3))
            for T in range(NT):
                pe.wait_ge(S("chan"), at(3, "chan") + T // 4 + 1)
                m = nc.tensor.matmul(bank[T // 32][:, (T % 32) * 16:(T % 32) * 16 + 16], n_chan[:, T * P:(T + 1) * P], W[3, "w_gat"], start=True, stop=True)
            m.then_inc(S("s3_h_t"), 1)
            pe.wait_ge(S("s3_last"), 1)
            for i in range(3):
                m = nc.tensor.transpose(bank[2][0:ROW, i * P:(i + 1) * P], last[:, i, :], ident[:, :])
            m.then_inc(S("s3_last_t"), 1)
            pe.wait_ge(S("s3_across"), 1)
            nc.tensor.transpose(bank[3][:, 0:ROW], last_t[0:ROW, 4, 1:P + 1], ident[0:ROW, 0:ROW])
            nc.tensor.transpose(bank[3][:, 32:32 + ROW], last_t[0:ROW, 0, 1:P + 1], ident[0:ROW, 0:ROW]).then_inc(S("s3_carry_t"), 1)

        def graph_scalar(a):
            def window(i, b):
                a.wait_ge(S("s3_expo"), 2 * i + b + 1)
                nc.scalar.activation(scale[:, b, :, :, :], expo[:, :, :, :], ACT.Exp).then_inc(S("s3_scale"), 1)
            pairs = pairs_in_use(a)
            with a.Fori(0, NW // 2) as i:
                with a.If(i < pairs):
                    for b in range(2):
                        window(i, b)
            a.wait_ge(S("s3_across_in"), 1)
            nc.scalar.activation(last_t[0:ROW, 2, 1:P + 1], last_t[0:ROW, 1, 1:P + 1], ACT.Exp).then_inc(S("s3_across_exp"), 1)
            nc.scalar.activation(last_t[0:ROW, 3, 1:P + 1], last_t[0:ROW, 5, 1:P + 1], ACT.Exp).then_inc(S("s3_across_exp"), 1)
            a.wait_ge(S("s3_merge_in"), 1)
            nc.scalar.activation(wgt[:, :, :, :], wgt[:, :, :, :], ACT.Exp).then_inc(S("s3_merge_exp"), 1)
            a.wait_ge(S("s3_score_var"), 1)
            nc.scalar.activation(sc2[:, :], sc2[:, :], ACT.Sqrt).then_inc(S("s3_score_std"), 1)

        def graph_vector(v, link):
            H16 = HEADS * GE

            def rep(ap, n):
                return ap.unsqueeze(1).broadcast_to([P, NT, n])
            v.wait_ge(*weights_in(3))
            v.wait_ge(S("s3_h_t"), 1)
            for i in range(2):
                link(v.tensor_copy(h_tok[:, 32 * i:32 * i + 32, 0:H16], bank[i][:, :].rearrange("p (t f) -> p t f", f=H16)))
            prod16 = src_i[:, 0:NT * H16].bitcast(F32).rearrange("p (t f) -> p t f", f=H16)
            for att, dst in (("att_src", h_tok[:, :, H16:ROW]), ("att_dst", a_dst[:, :, :])):
                link(v.tensor_tensor(prod16, h_tok[:, :, 0:H16], rep(W[3, att], H16), ALU.mult))
                link(v.tensor_reduce(dst, prod16.rearrange("p t (h g) -> p t h g", g=GE), AX, ALU.add))
            link(v.tensor_scalar(has[:, :], seg_size[:, :], 0.0, None, ALU.is_gt))
            link(v.tensor_scalar(start_f[:, :], has[:, :], -1.0, -1.0e9, ALU.add, ALU.mult))
            tmp3 = tuple(tok_split[:, i, :] for i in range(3))
            link(v.tensor_copy(part_f[:, :], seg_base[:, :]))
            split_position(v, link, part_f[:, :], tok_part[:, :], tmp3, part_i[:, :])
            link(v.tensor_tensor(start_f[:, :], start_f[:, :], part_f[:, :], ALU.add))
            link(v.tensor_copy(start_i[:, :], start_f[:, :]))
            link(v.tensor_tensor(start_f[:, :], seg_base[:, :], seg_size[:, :], ALU.add))
            link(v.tensor_scalar(start_f[:, :], start_f[:, :], -1.0, 0.0, ALU.add, ALU.max))
            split_position(v, link, start_f[:, :], part_f[:, :], tmp3, part_i[:, :])
            link(v.tensor_copy(end_i[:, :], start_f[:, :]))
            link(v.tensor_scalar(cont[:, :], part_f[:, :], span[:, 0:1], None, ALU.mult))
            link(v.tensor_tensor(cont[:, :], seg_base[:, :], cont[:, :], ALU.is_lt))
            link(v.tensor_tensor(cont[:, :], cont[:, :], has[:, :], ALU.mult))
            link(v.tensor_scalar(part_f[:, :], part_f[:, :], -1.0, 0.0, ALU.add, ALU.max))
            link(v.tensor_copy(part_i[:, :], part_f[:, :]))
            v.sem_inc(S("s3_tok"), 1)
            link(v.memset(prev_dst[:, :], -1.0))
            v.wait_ge(S("s3_sorted"), 16)
            link(v.memset(src_i[:, EPP:EPP + 2 * WIN], 0))
            link(v.tensor_scalar(src_i[:, 0:EPP], sorted_e[:, :], TOK - 1, None, ALU.bitwise_and))
            link(v.tensor_scalar(dst_i[:, :], sorted_e[:, :], 13, None, ALU.logical_shift_right))
            link(v.tensor_copy(dst_f[:, :], dst_i[:, :]))
            link(v.scalar_tensor_tensor(same[:, :], dst_f[:, :], float(TOK), dst_f[:, :], ALU.is_lt, ALU.mult))
            link(v.tensor_reduce(last_dst[:, 0:1], same[:, :], AX, ALU.max))
            link(v.tensor_copy(last_dst[:, 1:2], last_dst[:, 0:1]))
            v.sem_inc(S("s3_last_dst"), 1)
            link(v.tensor_tensor(same[:, 1:EPP], dst_f[:, 1:EPP], dst_f[:, 0:EPP - 1], ALU.is_equal))
            link(v.tensor_scalar(first_f[:, :], dst_f[:, 0:1], float(TOK - 1), None, ALU.min))
            link(v.tensor_copy(first_i[:, :], first_f[:, :]))
            link(v.tensor_tensor(join[:, 1:2], dst_f[:, 0:1], last_dst[:, 0:1], ALU.is_equal))
            v.wait_ge(S("s3_prev_dst"), 16)
            link(v.tensor_tensor(join[:, 0:1], dst_f[:, 0:1], prev_dst[:, 0:1], ALU.is_equal))
            link(v.memset(same[:, 0:1], 0.0))
            v.sem_inc(S("s3_idx_all"), 1)
            for b in range(2):
                link(v.tensor_copy(idx_ring[:, b, :], src_i[:, b * WIN:(b + 1) * WIN]))
                v.sem_inc(S("s3_idx"), 1)
            v.wait_ge(S("s3_adst"), 16)
            for h in range(HEADS):
                link(v.tensor_tensor_scan(a_dst_e[:, :, h], same[:, :], a_dst_e[:, :, h], 0.0, ALU.mult, ALU.add))
            link(v.memset(runmax[:, 1, :, WIN:WIN + 1], NEG))
            link(v.memset(sums[:, 1, WIN - 1, :], 0.0))

            STEPS = 34

            def window(i, b, first=False):
                g = 2 * i + b
                k = [0]

                def step(ins):
                    k[0] += 1
                    ins.then_inc(S("s3_window"), 1)
                    v.wait_ge(S("s3_window"), g * STEPS + k[0])
                prev = 1 - b
                v.wait_ge(s_gath[b], (i + 1) * (16 * WIN))
                at = bass.ds(g * WIN, WIN)
                step(v.tensor_tensor(z[:, :, :], rows[:, b, :, H16:ROW], a_dst_e[:, at, :], ALU.add))
                zt = z[:, :, :].rearrange("p c h -> p h c")
                step(v.scalar_tensor_tensor(e4[:, :, :], zt, 0.2, zt, ALU.mult, ALU.max))
                step(v.tensor_scalar(restart[:, :], same[:, at], -1.0, -NEG, ALU.add, ALU.mult))
                step(v.tensor_copy(runmax[:, b, :, 0:1], runmax[:, prev, :, WIN:WIN + 1]))
                for h in range(HEADS):
                    step(v.tensor_tensor_scan(runmax[:, b, h, 1:WIN + 1], restart[:, :], e4[:, h, :], runmax[:, prev, h, WIN:WIN + 1], ALU.add, ALU.max))
                step(v.tensor_tensor(expo[:, 0, :, :], runmax[:, b, :, 0:WIN], restart[:, :].unsqueeze(1).broadcast_to([P, HEADS, WIN]), ALU.add))
                step(v.tensor_tensor(expo[:, 0, :, :], expo[:, 0, :, :], runmax[:, b, :, 1:WIN + 1], ALU.subtract))
                step(v.tensor_tensor(expo[:, 1, :, :], e4[:, :, :], runmax[:, b, :, 1:WIN + 1], ALU.subtract))
                v.sem_inc(S("s3_expo"), 1)
                v.wait_ge(S("s3_scale"), g + 1)
                step(v.tensor_tensor(msg[:, :, :, :], rows[:, b, :, 0:H16].rearrange("p c (h t) -> p h t c", t=GE),
                                     scale[:, b, 1, :, :].unsqueeze(2).broadcast_to([P, HEADS, GE, WIN]), ALU.mult))
                if not first:
                    v.wait_ge(s_yout[b], i * 16)
                for f in range(ROW):
                    h = f // GE if f < H16 else f - H16
                    val = msg[:, h, f % GE, :] if f < H16 else scale[:, b, 1, h, :]
                    step(v.tensor_tensor_scan(sums[:, b, :, f], scale[:, b, 0, h, :], val, sums[:, prev, WIN - 1, f:f + 1], ALU.mult, ALU.add))
                step(v.tensor_copy(sums[:, b, :, ROW:ACC].rearrange("p c h -> p h c"), runmax[:, b, :, 1:WIN + 1]))
                step(v.tensor_copy(idx_ring[:, b, :], src_i[:, bass.ds((g + 2) * WIN, WIN)]))
                v.sem_inc(S("s3_sums"), 1)
                v.sem_inc(S("s3_idx"), 1)
                assert k[0] == STEPS, k[0]

            for b in range(2):
                window(0, b, True)
            pairs = pairs_in_use(v)
            with v.Fori(1, NW // 2) as i:
                with v.If(i < pairs):
                    for b in range(2):
                        window(i, b)

            end = sums[:, 1, WIN - 1, :]
            link(v.tensor_copy(last[:, 0, :], end[:, 0:ROW]))
            link(v.tensor_copy(last[:, 1, 0:H16].rearrange("p (h t) -> p h t", t=GE), end[:, ROW:ACC].unsqueeze(2).broadcast_to([P, HEADS, GE])))
            link(v.tensor_copy(last[:, 1, H16:ROW], end[:, ROW:ACC]))
            link(v.tensor_tensor(join[:, 0:1], join[:, 0:1], join[:, 1:2], ALU.mult))
            link(v.tensor_scalar(join[:, 0:1], join[:, 0:1], -1.0, -NEG, ALU.add, ALU.mult))
            link(v.tensor_copy(last[:, 2, :], join[:, 0:1].broadcast_to([P, ROW])))
            v.sem_inc(S("s3_last"), 1)
            v.wait_ge(S("s3_last_t"), 1)
            R = last_t[0:ROW, :, :]
            src = bank[2][0:ROW, :]
            one = slice(1, P + 1)
            link(v.tensor_copy(R[:, 6, one], src[:, 2 * P:3 * P]))
            link(v.tensor_copy(R[:, 7, one], src[:, P:2 * P]))
            link(v.memset(R[:, 0, 0:1], NEG))
            link(v.tensor_tensor_scan(R[:, 0, one], R[:, 6, one], R[:, 7, one], NEG, ALU.add, ALU.max))
            link(v.tensor_tensor(R[:, 1, one], R[:, 0, 0:P], R[:, 6, one], ALU.add))
            link(v.tensor_tensor(R[:, 1, one], R[:, 1, one], R[:, 0, one], ALU.subtract))
            link(v.tensor_tensor(R[:, 5, one], R[:, 7, one], R[:, 0, one], ALU.subtract))
            v.sem_inc(S("s3_across_in"), 1)
            v.wait_ge(S("s3_across_exp"), 2)
            link(v.tensor_tensor(R[:, 3, one], R[:, 3, one], src[:, 0:P], ALU.mult))
            link(v.tensor_tensor_scan(R[:, 4, one], R[:, 2, one], R[:, 3, one], 0.0, ALU.mult, ALU.add))
            v.sem_inc(S("s3_across"), 1)
            v.wait_ge(S("s3_carry_t"), 1)
            link(v.tensor_copy(carry[:, 0:ROW], bank[3][:, 0:ROW]))
            link(v.tensor_copy(carry[:, ROW:ACC], bank[3][:, 32 + H16:32 + ROW]))
            v.sem_inc(S("s3_carry"), 1)

            link(v.tensor_tensor(e_self[:, :, :], h_tok[:, :, H16:ROW], a_dst[:, :, :], ALU.add))
            link(v.scalar_tensor_tensor(e_self[:, :, :], e_self[:, :, :], 0.2, e_self[:, :, :], ALU.mult, ALU.max))
            link(v.tensor_scalar(has[:, :], has[:, :], -1.0, -NEG, ALU.add, ALU.mult))
            link(v.tensor_scalar(cont[:, :], cont[:, :], -1.0, -NEG, ALU.add, ALU.mult))
            v.wait_ge(S("s3_tok_end"), 16 * NT)
            v.wait_ge(S("s3_tok_carry"), 16 * NT)

            def bc4(ap):
                return ap.unsqueeze(2).broadcast_to([P, NT, HEADS])
            link(v.tensor_tensor(wgt[:, 0, :, :], tok_end[:, :, ROW:ACC], bc4(has[:, :]), ALU.add))
            link(v.tensor_tensor(wgt[:, 1, :, :], tok_carry[:, :, ROW:ACC], bc4(cont[:, :]), ALU.add))
            link(v.tensor_tensor(m_all[:, :, :], wgt[:, 0, :, :], wgt[:, 1, :, :], ALU.max))
            link(v.tensor_tensor(m_all[:, :, :], m_all[:, :, :], e_self[:, :, :], ALU.max))
            link(v.tensor_tensor(wgt[:, 0, :, :], wgt[:, 0, :, :], m_all[:, :, :], ALU.subtract))
            link(v.tensor_tensor(wgt[:, 1, :, :], wgt[:, 1, :, :], m_all[:, :, :], ALU.subtract))
            link(v.tensor_tensor(wgt[:, 2, :, :], e_self[:, :, :], m_all[:, :, :], ALU.subtract))
            v.sem_inc(S("s3_merge_in"), 1)
            v.wait_ge(S("s3_merge_exp"), 1)

            def weigh(out, src, w, ones_too=True):
                link(v.tensor_tensor(out[:, :, 0:H16].rearrange("p t (h g) -> p t h g", g=GE), src[:, :, 0:H16].rearrange("p t (h g) -> p t h g", g=GE),
                                     w.unsqueeze(3).broadcast_to([P, NT, HEADS, GE]), ALU.mult))
                if ones_too:
                    link(v.tensor_tensor(out[:, :, H16:ROW], src[:, :, H16:ROW], w, ALU.mult))
                else:
                    link(v.tensor_copy(out[:, :, H16:ROW], w))
            weigh(agg, tok_end, wgt[:, 0, :, :])
            weigh(tmp, tok_carry, wgt[:, 1, :, :])
            link(v.tensor_tensor(agg[:, :, :], agg[:, :, :], tmp[:, :, :], ALU.add))
            weigh(tmp, h_tok, wgt[:, 2, :, :], False)
            link(v.tensor_tensor(agg[:, :, :], agg[:, :, :], tmp[:, :, :], ALU.add))
            den = agg[:, :, H16:ROW]
            link(v.tensor_scalar(den, den, 1e-16, None, ALU.add))
            link(v.reciprocal(den, den))
            A = agg[:, :, 0:H16]
            A4 = A.rearrange("p t (h g) -> p t h g", g=GE)
            link(v.tensor_tensor(A4, A4, den.unsqueeze(3).broadcast_to([P, NT, HEADS, GE]), ALU.mult))
            link(v.tensor_tensor(A, A, rep(W[3, "b_gat"], H16), ALU.add))
            link(v.tensor_reduce(sc1[:, :], A, AX, ALU.add))
            link(v.tensor_scalar(sc1[:, :], sc1[:, :], 1.0 / H16, None, ALU.mult))
            link(v.tensor_tensor(A, A, sc1[:, :].unsqueeze(2).broadcast_to([P, NT, H16]), ALU.subtract))
            T16 = tmp[:, :, 0:H16]
            link(v.tensor_tensor(T16, A, A, ALU.mult))
            link(v.tensor_reduce(sc2[:, :], T16, AX, ALU.add))
            link(v.tensor_scalar(sc2[:, :], sc2[:, :], 1.0 / H16, 1e-5, ALU.mult, ALU.add))
            v.sem_inc(S("s3_score_var"), 1)
            v.wait_ge(S("s3_score_std"), 1)
            link(v.reciprocal(sc2[:, :], sc2[:, :]))
            link(v.tensor_tensor(A, A, sc2[:, :].unsqueeze(2).broadcast_to([P, NT, H16]), ALU.mult))
            link(v.tensor_tensor(A, A, rep(W[3, "ln_gamma"], H16), ALU.mult))
            link(v.tensor_tensor(A, A, rep(W[3, "ln_beta"], H16), ALU.add))
            link(v.tensor_reduce(gates[:, :, 4:8], A.rearrange("p t (h g) -> p t g h", g=GE), AX, ALU.add))
            val = gt[0][:, 0:NT * 4].rearrange("p (t e) -> p t e", e=4)
            link(v.tensor_scalar(val, gates[:, :, 4:8], 1.0 / HEADS, None, ALU.mult))

        def blank_sync(sp):
            pairs = pairs_in_use(sp)
            out_v = sums_d.rearrange("(p j) f -> p j f", p=P)
            blank = packed[:, 0:WIN * ACC].bitcast(F32).rearrange("p (w f) -> p w f", f=ACC)
            with sp.Fori(0, NW // 2) as i:
                with sp.If(i >= pairs - 1):
                    for b in range(2):
                        sp.dma_start(out_v[:, bass.ds((2 * i + b) * WIN, WIN), :], blank).then_inc(S("blank_out"), 16)
            return pairs

        def graph_sync(sp, pairs):
            rows_v = row_d.rearrange("(t p) f -> p t f", p=P)
            sp.wait_ge(S("s3_tok"), 1)
            sp.dma_start(rows_v, h_tok[:, :, :]).then_inc(S("s3_tables"), 16)
            sp.dma_start(adst_d.rearrange("(t p) f -> p t f", p=P), a_dst[:, :, :]).then_inc(S("s3_tables"), 16)
            blanked = sp.value_load(pairs_i[0:1, 1:2], min_val=1, max_val=NW // 2)
            sp.wait_ge(S("blank_out"), blanked * (2 * 16))
            for b in range(2):
                sp.wait_ge(s_sc[b], 8 * EPP)
            lists = sorted_d.rearrange("(p j) t -> p (j t)", p=P)
            sp.dma_start(sorted_e[:, :], lists).then_inc(S("s3_sorted"), 16)
            sp.wait_ge(S("s3_last_dst"), 1)
            sp.dma_start(prev_dst[1:P, :], last_dst[0:P - 1, :]).then_inc(S("s3_prev_dst"), 16)
            sp.wait_ge(S("s3_starts"), 16 * NT)
            sp.dma_start(a_dst_e[:, :, :].rearrange("p j h -> p (j h)"), start_d.rearrange("(p j) h -> p (j h)", p=P)).then_inc(S("s3_starts_in"), 16)
            out_v = sums_d.rearrange("(p j) f -> p j f", p=P)

            with sp.Fori(0, NW // 2) as i:
                with sp.If(i < pairs):
                    for b in range(2):
                        sp.wait_ge(S("s3_sums"), 2 * i + b + 1)
                        sp.dma_start(out_v[:, bass.ds((2 * i + b) * WIN, WIN), :], sums[:, b, :, :]).then_inc(s_yout[b], 16)
            sp.wait_ge(S("s3_carry"), 1)
            sp.dma_start(carry_d, carry[:, :]).then_inc(S("s3_carry_ready"), 16)

        def graph_pool(g):
            def at(ap):
                return bass.IndirectOffsetOnAxis(ap=ap, axis=0)
            g.wait_ge(S("s3_tok"), 1)
            for T in range(NT):
                g.indirect_dma_start(out=start_d[:, :], out_offset=at(start_i[:, T:T + 1]), in_=a_dst[:, T, :], in_offset=None,
                                     bounds_check=EDGES - 1, oob_is_err=False).then_inc(S("s3_starts"), 16)
            g.wait_ge(S("s3_tables"), 32)
            g.wait_ge(S("s3_idx_all"), 1)
            g.wait_ge(S("s3_starts_in"), 16)
            g.indirect_dma_start(out=a_dst_e[:, 0, :], out_offset=None, in_=adst_d[:, :], in_offset=at(first_i[:, 0:1])).then_inc(S("s3_adst"), 16)
            pairs = pairs_in_use(g)
            with g.Fori(0, NW // 2) as i:
                with g.If(i < pairs):
                    for b in range(2):
                        g.wait_ge(S("s3_idx"), 2 * i + b + 1)
                        g.sem_inc(S("s3_pool_go"), 1)
                        for c in range(WIN):
                            g.indirect_dma_start(out=rows[:, b, c, :], out_offset=None, in_=row_d[:, :], in_offset=at(idx_ring[:, b, c:c + 1])).then_inc(s_gath[b], 16)
            for b in range(2):
                g.wait_ge(s_yout[b], pairs * 16)
                g.sem_inc(S("s3_pool_go"), 1)
            for T in range(NT):
                g.indirect_dma_start(out=tok_end[:, T, :], out_offset=None, in_=sums_d[:, :], in_offset=at(end_i[:, T:T + 1])).then_inc(S("s3_tok_end"), 16)
            g.wait_ge(S("s3_carry_ready"), 16)
            for T in range(NT):
                g.indirect_dma_start(out=tok_carry[:, T, :], out_offset=None, in_=carry_d[:, :], in_offset=at(part_i[:, T:T + 1])).then_inc(S("s3_tok_carry"), 16)

        NQ = GROUP // SUB

        def sort_sync(sp):
            sp.dma_start(edge_i[:, :, :], d["L1_ffn_edge_index"].rearrange("t (p j) -> p t j", p=P)).then_inc(S("sort_edges"), 16)
            sp.wait_ge(S("sort_fill"), 1)
            sp.dma_start(sorted_d.rearrange("(p j) t -> p (j t)", p=P), n_tok[:, 0:NT // 2, :].bitcast(I32).rearrange("p t c -> p (t c)")).then_inc(S("sort_filled"), 16)
            sv = start_d.rearrange("(h p j) f -> h p (j f)", p=P, h=2)
            for h in range(2):
                sp.dma_start(sv[h], x_tok[:, :, :].rearrange("p t c -> p (t c)")).then_inc(S("sort_zeroed"), 16)

        def sort_pool(g):
            g.iota(iota[:, :, :], pattern=[[1, P], [0, SUB]], base=0, channel_multiplier=0, allow_small_or_imprecise_dtypes=True).then_inc(S("c_made"), 1)
            g.iota(iota_p[:, :], pattern=[[0, 1]], base=0, channel_multiplier=1, allow_small_or_imprecise_dtypes=True).then_inc(S("c_made"), 1)
            g.iota(order8[:, :], pattern=[[-1, 8]], base=8, channel_multiplier=0, allow_small_or_imprecise_dtypes=True).then_inc(S("c_made"), 1)
            g.iota(order4[:, :], pattern=[[-1, 4]], base=4, channel_multiplier=0, allow_small_or_imprecise_dtypes=True).then_inc(S("c_made"), 1)
            for t, x in ((ident, 0.0), (ident2, 0.0), (tri, 1.0), (tri_f, 1.0), (ones_f, 1.0), (ones_b, 1.0), (gsel, 1.0)):
                g.memset(t[:, :], x).then_inc(S("c_made"), 1)
            g.memset(sel[:, :, :], 1.0).then_inc(S("c_made"), 1)
            g.wait_ge(S("c_made"), 12)

            def pick(t, op, fill, base, pattern, cm):
                return g.affine_select(out=t, in_=t, compare_op=op, fill=fill, base=base, pattern=pattern, channel_multiplier=cm)
            pick(ident[:, :], ALU.not_equal, 1.0, 0, [[-1, P]], 1).then_inc(S("c_ready"), 1)
            pick(tri[:, :], ALU.is_gt, 0.0, 0, [[1, P]], -1).then_inc(S("c_ready"), 1)
            pick(tri_f[:, :], ALU.is_gt, 0.0, 0, [[1, P]], -1).then_inc(S("c_ready"), 1)
            pick(sel[:, :, :], ALU.is_equal, 0.0, 0, [[1, GROUP], [0, P]], -1).then_inc(S("c_ready"), 1)
            for h in range(2):
                p = slice(h * C, (h + 1) * C)
                pick(ident2[p, :], ALU.not_equal, 1.0, 0, [[-1, C]], 1).then_inc(S("c_ready"), 1)
                pick(gsel[p, :], ALU.is_ge, 0.0, 0, [[-16, 4]], 1).then_inc(S("c_gsel"), 1)
                g.wait_ge(S("c_gsel"), h + 1)
                pick(gsel[p, :], ALU.is_ge, 0.0, 15, [[16, 4]], -1).then_inc(S("c_ready"), 1)
            g.wait_ge(S("sort_filled"), 16)

            def scatter_pair(i, first):
                for b in range(2):
                    at_group = bass.ds((i * 2 + b) * GROUP, GROUP)
                    g.wait_ge(S("sort_pos"), i * 2 + b + 1)
                    g.sem_inc(S("sort_pool_go"), 1)
                    if not first:
                        g.wait_ge(s_sc[b], i * (16 * GROUP))
                        g.sem_inc(S("sort_pool_go"), 1)
                    g.tensor_copy(pos_ring[:, b, :], pos_all[:, at_group]).then_inc(S("sort_rings"), 1)
                    g.tensor_copy(packed_ring[:, b, :], packed[:, at_group]).then_inc(S("sort_rings"), 1)
                    g.wait_ge(S("sort_rings"), (i * 2 + b) * 2 + 2)
                    g.sem_inc(S("sort_pool_go"), 1)
                    for c in range(GROUP):
                        g.indirect_dma_start(out=sorted_d[:, :], out_offset=bass.IndirectOffsetOnAxis(ap=pos_ring[:, b, c:c + 1], axis=0),
                                             in_=packed_ring[:, b, c:c + 1], in_offset=None, bounds_check=EDGES - 1, oob_is_err=False).then_inc(s_sc[b], 16)

            scatter_pair(0, True)
            with g.Fori(1, NG // 2) as i:
                scatter_pair(i, False)

        def sort_scalar(a):
            a.wait_ge(S("sort_base_in"), 1)
            nc.scalar.copy(hist[:, 0, :], H).then_inc(S("sort_hist"), 1)
            with a.Fori(0, EPP // 2) as i:
                for b in range(2):
                    c = i * 2 + b
                    a.wait_ge(S("sort_counted"), c + 1)
                    a.wait_ge(S("sort_ranked_t"), c + 1)
                    nc.scalar.copy(hist[:, (b + 1) % 2, :], H).then_inc(S("sort_hist"), 1)

        def sort_tensor(pe):
            pe.wait_ge(S("c_made"), 12)
            pe.wait_ge(S("sort_fill"), 1)
            nc.tensor.matmul(H, ones_f[:, :], x_tok[:, 0, :], start=True, stop=False, skip_group_check=True)
            with pe.Fori(0, NSUB // 2) as i:
                for b in range(2):
                    pe.wait_ge(S("sort_one1"), i * 2 + b + 1)
                    for c in range(SUB):
                        m = nc.tensor.matmul(H, onehot_lo[:, b, :, c], onehot_hi[:, b, :, c], start=False, stop=False, skip_group_check=True)
                    m.then_inc(S("sort_total_t"), 1)
            pe.wait_ge(S("c_ready"), 8)
            pe.wait_ge(S("sort_total"), 1)
            nc.tensor.matmul(bank[1][:, 0:NT], tri_f[:, :], seg_size[:, :], start=True, stop=True)
            nc.tensor.matmul(bank[1][:, NT:2 * NT], ones_f[:, :], seg_size[:, :], start=True, stop=True).then_inc(S("sort_cums_t"), 1)
            pe.wait_ge(S("sort_base"), 1)
            nc.tensor.matmul(H, ident[:, :], seg_base[:, :], start=True, stop=False, skip_group_check=True).then_inc(S("sort_base_in"), 1)

            def rows_of(gi, b):
                pe.wait_ge(S("sort_ring"), gi + 1)
                nc.tensor.transpose(bank[1][0:GROUP, 0:P], ring_low[:, b, :], ident[:, :]).then_inc(S("sort_rows_t"), 1)
                pe.wait_ge(S("sort_rows"), gi + 1)

            def spread(sub, b, q):
                pe.wait_ge(S("sort_one"), sub)
                for k in range(SUB):
                    m = nc.tensor.matmul(bank[2 + k // 4][:, (k % 4) * P:(k % 4 + 1) * P], sel[:, q * SUB + k, :], lo_rows[:, b, :], start=True, stop=True)
                m.then_inc(S("sort_bc_t"), 1)

            def ranks(sub, q):
                sbuf = q % 2
                pe.wait_ge(S("sort_one"), sub + 1)
                for k in range(SUB):
                    ch = sub * SUB + k
                    R = bank[4 + k // 2][:, (k % 2) * NT:(k % 2 + 1) * NT]
                    if k % 2 == 0:
                        pe.wait_ge(S("sort_rank"), ch + 2)
                    nc.tensor.matmul(R, same_before[:, sbuf, k, :], onehot_hi[:, sbuf, :, k], start=True, stop=False)
                    pe.wait_ge(S("sort_hist"), ch + 1)
                    nc.tensor.matmul(H, onehot_lo[:, sbuf, :, k], onehot_hi[:, sbuf, :, k], start=False, stop=False, skip_group_check=True).then_inc(S("sort_counted"), 1)
                    nc.tensor.matmul(R, lo_on_part[:, sbuf, k, :], hist[:, k % 2, :], start=False, stop=True).then_inc(S("sort_ranked_t"), 1)

            def rank_pair(i, more):
                for b in range(2):
                    gi = i * 2 + b
                    for q in range(NQ):
                        sub = gi * NQ + q
                        if q < NQ - 1:
                            spread(sub + 1, b, q + 1)
                        elif b == 0 or more:
                            rows_of(gi + 1, 1 - b)
                            spread(sub + 1, 1 - b, 0)
                        ranks(sub, q)

            pe.sem_inc(S("sort_ranked_t"), 1)
            rows_of(0, 0)
            spread(0, 0, 0)
            with pe.Fori(0, NG // 2 - 1) as i:
                rank_pair(i, True)
            rank_pair(NG // 2 - 1, False)

        def sort_vector(v, link):
            link(v.memset(n_tok[:, 0:NT // 2, :].bitcast(I32), (2 * TOK) << 13))
            link(v.memset(x_tok[:, :, :], 0.0))
            v.sem_inc(S("sort_fill"), 1)
            v.wait_ge(S("c_made"), 12)
            v.wait_ge(S("sort_edges"), 16)
            link(v.tensor_scalar(bits_i[:, 0, :], edge_i[:, 1, :], P - 1, None, ALU.bitwise_and))
            link(v.tensor_scalar(bits_i[:, 1, :], edge_i[:, 1, :], 7, None, ALU.logical_shift_right))

            def groups(ap):
                return ap.rearrange("p (g c) -> p g c", c=GROUP)
            link(v.tensor_copy(low_high[:, :, 0, :], groups(bits_i[:, 0, :])))
            link(v.tensor_copy(low_high[:, :, 1, :], groups(bits_i[:, 1, :])))
            link(v.tensor_scalar(edge_i[:, 0, :], edge_i[:, 0, :], float(TOK - 1), None, ALU.min))
            link(v.tensor_scalar(bits_i[:, 0, :], edge_i[:, 1, :], 13, None, ALU.logical_shift_left))
            link(v.tensor_tensor(packed[:, :], bits_i[:, 0, :], edge_i[:, 0, :], ALU.bitwise_or))

            def onehots(sbuf, rb, q):
                at_sub = slice(q * SUB, (q + 1) * SUB)
                v.tensor_tensor(onehot_lo[:, sbuf, :, :], iota[:, :, :], ring[:, rb, 0, at_sub].unsqueeze(1).broadcast_to([P, P, SUB]), ALU.is_equal)
                return v.tensor_tensor(onehot_hi[:, sbuf, :, :], iota[:, 0:NT, :], ring[:, rb, 1, at_sub].unsqueeze(1).broadcast_to([P, NT, SUB]), ALU.is_equal)
            v.sem_inc(S("sort_total_t"), 2)
            v.sem_inc(S("sort_rank"), SUB)
            with v.Fori(0, NG // 2) as i:
                for b in range(2):
                    gi = i * 2 + b
                    v.tensor_copy(ring[:, b, :, :], low_high[:, bass.ds(gi, 1), :, :].rearrange("p o k c -> p (o k) c")).then_inc(S("sort_ring1"), 1)
                    v.wait_ge(S("sort_ring1"), gi + 1)
                    for q in range(NQ):
                        v.wait_ge(S("sort_total_t"), gi * NQ + q + 1)
                        onehots(q % 2, b, q).then_inc(S("sort_one1"), 1)
            v.wait_ge(S("sort_total_t"), NSUB + 2)
            link(v.tensor_copy(seg_size[:, :], H))
            v.sem_inc(S("sort_total"), 1)
            v.wait_ge(S("sort_cums_t"), 1)
            link(v.tensor_tensor_scan(cums[:, :], ones_f[:, 0:NT], bank[1][:, NT:2 * NT], 0.0, ALU.mult, ALU.add))
            link(v.tensor_scalar(limits[:, :], iota[:, 0:NW // 2, 0], float(2 * WIN * P), None, ALU.mult))
            link(v.memset(limits[:, 0:1], -1.0))
            link(v.tensor_scalar(limits[:, :], limits[:, :], cums[:, NT - 1:NT], None, ALU.is_lt))
            link(v.tensor_reduce(span[:, 1:2], limits[:, :], AX, ALU.add))
            link(v.tensor_copy(pairs_i[:, 0:1], span[:, 1:2]))
            link(v.tensor_scalar(span[:, 0:1], span[:, 1:2], -1.0, float(NW // 2 + 1), ALU.mult, ALU.add))
            link(v.tensor_copy(pairs_i[:, 1:2], span[:, 0:1]))
            link(v.tensor_scalar(span[:, 0:1], span[:, 1:2], float(2 * WIN), None, ALU.mult))
            link(v.reciprocal(span[:, 1:2], span[:, 0:1]))
            link(v.tensor_scalar(span[:, 2:3], span[:, 0:1], -1.0, None, ALU.mult))
            link(v.tensor_scalar(span[:, 3:4], span[:, 0:1], -1.0, float(EPP), ALU.mult, ALU.add))
            link(v.tensor_tensor(cums[:, :], cums[:, :], bank[1][:, NT:2 * NT], ALU.subtract))
            link(v.tensor_tensor(seg_base[:, :], cums[:, :], bank[1][:, 0:NT], ALU.add))
            v.sem_inc(S("sort_base"), 1)
            v.wait_ge(S("c_ready"), 8)

            def ring_of(gi, b):
                v.tensor_copy(ring[:, b, :, :], low_high[:, bass.ds(gi, 1), :, :].rearrange("p o k c -> p (o k) c")).then_inc(S("sort_ring_b"), 1)
                v.wait_ge(S("sort_ring_b"), gi + 1)
                v.tensor_copy(ring_low[:, b, :], ring[:, b, 0, :]).then_inc(S("sort_ring"), 1)
                v.wait_ge(S("sort_rows_t"), gi + 1)
                v.tensor_copy(lo_rows[:, b, :], bank[1][0:GROUP, 0:P]).then_inc(S("sort_rows"), 1)

            def make(sub, b, q):
                sbuf = q % 2
                onehots(sbuf, b, q)
                v.wait_ge(S("sort_bc_t"), sub + 1)
                for t in range(2):
                    low = bank[2 + t][:, :].rearrange("p (a b) -> p a b", b=P)
                    j = q * SUB + 4 * t
                    v.tensor_tensor(same_before[:, sbuf, 4 * t:4 * t + 4, :], low, ring_low[:, b, j:j + 4].unsqueeze(2).broadcast_to([P, 4, P]), ALU.is_equal).then_inc(S("sort_same"), 1)
                for t in range(2):
                    v.wait_ge(S("sort_same"), sub * 2 + t + 1)
                    m = same_before[:, sbuf, 4 * t:4 * t + 4, :]
                    v.tensor_tensor(m, m, tri[:, :].unsqueeze(1).broadcast_to([P, 4, P]), ALU.mult)
                for t in range(2):
                    m = v.tensor_scalar(lo_on_part[:, sbuf, 4 * t:4 * t + 4, :], bank[2 + t][:, :].rearrange("p (a b) -> p a b", b=P), iota_p[:, 0:1], None, ALU.is_equal)
                m.then_inc(S("sort_one"), 1)

            def read_ranks(sub, b, q):
                for k in range(SUB):
                    j = q * SUB + k
                    if k % 2 == 0:
                        v.wait_ge(S("sort_ranked_t"), sub * SUB + k + 3)
                    v.tensor_tensor_reduce(junk[:, k, :], bank[4 + k // 2][:, (k % 2) * NT:(k % 2 + 1) * NT], onehot_hi[:, q % 2, :, k], 1.0, 0.0,
                                           ALU.mult, ALU.add, rank[:, b, j:j + 1]).then_inc(S("sort_rank"), 1)

            def rank_pair(i, more):
                for b in range(2):
                    gi = i * 2 + b
                    for q in range(NQ):
                        sub = gi * NQ + q
                        v.wait_ge(S("sort_rank"), sub * SUB + SUB)
                        if q < NQ - 1:
                            make(sub + 1, b, q + 1)
                        elif b == 0 or more:
                            ring_of(gi + 1, 1 - b)
                            make(sub + 1, 1 - b, 0)
                        read_ranks(sub, b, q)
                    k = [0]

                    def step(ins):
                        k[0] += 1
                        ins.then_inc(S("sort_step"), 1)
                        v.wait_ge(S("sort_step"), gi * (SPLIT_STEPS + 1) + k[0])
                    step(v.tensor_scalar(dropped[:, :], ring[:, b, 1, :], float(NT), 1.0e9, ALU.is_ge, ALU.mult))
                    v.wait_ge(S("sort_rank"), (gi + 1) * GROUP + SUB)
                    split_position(v, step, rank[:, b, :], split[:, 0, :], (split[:, 1, :], split[:, 2, :], split[:, 3, :]), split_i[:, :])
                    assert k[0] == SPLIT_STEPS + 1
                    v.tensor_tensor(pos_all[:, bass.ds(gi * GROUP, GROUP)], rank[:, b, :], dropped[:, :], ALU.add).then_inc(S("sort_pos"), 1)

            ring_of(0, 0)
            make(0, 0, 0)
            with v.Fori(0, NG // 2 - 1) as i:
                rank_pair(i, True)
            rank_pair(NG // 2 - 1, False)

        def x_tensor(pe):
            pe.wait_ge(S("x_in"), 16)
            pe.wait_ge(S("sort_rank"), EPP + SUB)
            pe.wait_ge(S("c_ready"), 8)
            for g in range(8):
                if g >= 2:
                    pe.wait_ge(S("x_copied"), g - 1)
                for t in range(8):
                    T = 8 * g + t
                    m = nc.tensor.transpose(bank[6 + g % 2][:, t * C:(t + 1) * C], n_chan[:, T * P:(T + 1) * P], ident[0:C, 0:C])
                m.then_inc(S("x_t"), 1)

        def x_vector(v):
            v.wait_ge(S("sort_zeroed"), 32)
            for g in range(8):
                v.wait_ge(S("x_t"), g + 1)
                v.tensor_copy(x_tok[:, 8 * g:8 * g + 8, :], bank[6 + g % 2][:, :].rearrange("p (t c) -> p t c", c=C)).then_inc(S("x_copied"), 1)
            v.wait_ge(S("x_copied"), 8)

        SORT = 3 in stages
        block = ctx.enter_context(nc.Block())

        @block.sync
        def _(sp):
            def weights(st):
                if st not in stages:
                    return
                if st - 2 in stages:
                    sp.wait_ge(*done(st - 2))
                for dst, src in loads[st]:
                    sp.dma_start(dst, src).then_inc(S(f"weights_in{st % 2}"), 16)

            sp.dma_start(n_chan[:, :].rearrange("c (b n) -> c b n", b=B), d["x"].rearrange("b c h w -> c b (h w)")).then_inc(S("x_in"), 16)
            sort_sync(sp)
            weights(0)
            weights(1)
            if 3 in stages:
                pairs = blank_sync(sp)
            if 0 in stages:
                sp.wait_ge(S("normed"), at(0, "normed") + 4)
                sp.wait_ge(S("x_copied"), 8)
                for par in range(2):
                    sp.dma_start(n_w[:, :, par, :], n_tok[par * C:(par + 1) * C, :, :]).then_inc(S("s0_rows"), 16)
            weights(2)
            weights(3)
            weights(4)
            if 3 in stages:
                graph_sync(sp, pairs)
            for st in (5, 6, 7):
                weights(st)
            for b in range(B):
                sp.wait_ge(S("out"), 8 * (b + 1))
                sp.dma_start(out.rearrange("b c h w -> c b (h w)")[:, b], n_chan[:, b * TOK // 2:(b + 1) * TOK // 2]).then_inc(S("stored"), 16)
            sp.wait_ge(S("stored"), 32)
            sp.wait_ge(S("sort_zeroed"), 32)

        @block.gpsimd
        def _(g):
            sort_pool(g)
            if 3 in stages:
                graph_pool(g)
            for b in range(2):
                g.wait_ge(s_sc[b], 8 * EPP)

        @block.tensor
        def _(pe):
            sort_tensor(pe)
            x_tensor(pe)
            for st in stages:
                if st == 0:
                    l0_tensor(pe)
                if st in FFN:
                    channels_tensor(pe, st)
                    if st == 3:
                        graph_tensor(pe)
                    ffn_tensor(pe, st)
                if st == 2:
                    channels_tensor(pe, 2)
                    pe.wait_ge(*weights_in(2))
                    conv_tensor(pe, 2, lambda b, px, py: W[2, "conv"][:, 2 * px + py, :])
                if st == 4:
                    l2_tensor(pe)
                if st == 6:
                    l3_tensor(pe)
            pe.wait_ge(*done(last_stage))
            channels_tensor(pe, 9, src=x_tok, kind="out")

        @block.scalar
        def _(a):
            sort_scalar(a)
            for st in stages:
                ln_scalar(a, st)
                if st == 0:
                    l0_scalar(a)
                if st in FFN:
                    channels_scalar(a, st)
                    if st == 3:
                        graph_scalar(a)
                    ffn_scalar(a, st)
                if st == 2:
                    image_scalar(a, 2, "chan")
                    conv_scalar(a, 2)
                if st == 4:
                    l2_scalar(a)
                if st == 6:
                    l3_scalar(a)
            channels_scalar(a, 9, "out")

        @block.vector
        def _(v):
            chain = [0]

            def link(ins):
                chain[0] += 1
                ins.then_inc(S("vector_chain"), 1)
                v.wait_ge(S("vector_chain"), chain[0])

            sort_vector(v, link)
            x_vector(v)
            for st in stages:
                ln_vector(v, link, st)
                if st == 0:
                    l0_vector(v, link)
                if st in FFN:
                    if st == 3:
                        graph_vector(v, link)
                    ffn_vector(v, link, st)
                if st == 2:
                    v.wait_ge(S("normed"), at(2, "normed") + 4)
                    image_zero(v, link, 2)
                    v.wait_ge(*weights_in(2))
                    bias_vector(v, link, W[2, "b"])
                    conv_vector(v, link, 2)
                if st == 4:
                    l2_vector(v, link)
                if st == 6:
                    l3_vector(v, link)


def layouts(inputs):
    import numpy as np
    c = np.ascontiguousarray
    d = {}
    for n, a in inputs.items():
        d[n] = np.asarray(a)
    for n in ("L0_ffn", "L1_ffn", "L2_ffn", "L3_ffn"):
        b1, b2, w2 = (d[f"{n}_{x}"] if f"{n}_{x}" in d else d[f"{n}_{x.upper()}"] for x in ("b1", "b2", "w2"))
        if n + "_W1" in d:
            d[n + "_w1"] = d.pop(n + "_W1")
            w2 = d.pop(n + "_W2")
        d[n + "_b1"] = c(b1.reshape(-1, P).T)
        d[n + "_b2"] = c(b2)
        d[n + "_w2"] = c(w2.reshape(-1, 64))
    for n in ("L0_ffn", "L3_ffn"):
        d[n + "_router"] = c(d.pop(n + "_router_w").T)
    d["L2_ffn_router"] = c(d.pop("L2_ffn_Wg"))
    for n in ("att_src", "att_dst"):
        d["L1_ffn_" + n] = c(d["L1_ffn_" + n].reshape(-1))

    def kernel_pairs(taps):
        k = taps.shape[0]
        pairs = (k + 1) // 2
        both = np.zeros((2, taps.shape[2], pairs, pairs, 2) + taps.shape[3:], taps.dtype)
        for y in range(k):
            for x in range(k):
                both[x % 2, :, x // 2, y // 2, y % 2] = taps[y, x]
        return both.reshape((2 * taps.shape[2], pairs * pairs, -1))
    w = d.pop("L1_conv_w").reshape(8, 3, 3, 8, 8)
    full = np.zeros((3, 3, 8, 8, 8, 8), w.dtype)
    for n in range(8):
        for m in range(8):
            full[:, :, :, n, :, m] = w[..., (m - n) % 8].transpose(1, 2, 3, 0)
    d["L1_conv_wk"] = kernel_pairs(full.reshape(3, 3, 64, 64))
    d["L2_qkv_wT"] = c(d.pop("L2_conv_qkv_w").T)
    d["L2_proj_wT"] = c(d.pop("L2_conv_proj_w").T)
    d["L2_dwc_taps"] = kernel_pairs(d.pop("L2_conv_dwc_w")[:, 0].transpose(1, 2, 0)).reshape(P, -1)
    d["L3_dw_taps"] = kernel_pairs(d.pop("L3_conv_dw_weight")[:, 0].transpose(1, 2, 0)).reshape(P, -1)
    d["L3_dk_w1T"] = c(d.pop("L3_conv_dk_w1").T)
    d["L3_cg_w1T"] = c(d.pop("L3_conv_cg_w1").T)
    d["L3_cg_w2T"] = c(d.pop("L3_conv_cg_w2").T)

    def dyn_pairs(a):
        a = a.reshape(4, 7, 7, -1)
        both = np.zeros((4, 2, 4, 4, 2, a.shape[-1]), a.dtype)
        for y in range(7):
            for x in range(7):
                both[:, x % 2, x // 2, y // 2, y % 2] = a[:, y, x]
        return c(both.reshape(8 * TAPS, -1).T)
    d["L3_dk_w2T"] = dyn_pairs(d.pop("L3_conv_dk_w2"))
    d["L3_dk_b2p"] = dyn_pairs(d.pop("L3_conv_dk_b2"))[0]
    return {n: c(a) for n, a in d.items()}


STAGES = (0, 1, 2, 3, 4, 5, 6, 7)


def kernel(**inputs):
    import numpy as np
    import concourse.bacc as bacc
    from concourse.bass_utils import run_bass_kernel_spmd

    nc = bacc.Bacc("TRN2", target_bir_lowering=False, num_devices=1)
    arrays = {"in_" + n: a for n, a in layouts(inputs).items()}
    d = {n[3:]: nc.dram_tensor(n, a.shape, mybir.dt.from_np(a.dtype), kind="ExternalInput").ap() for n, a in arrays.items()}
    out = nc.dram_tensor("out", (B, C, IMG, IMG), F32, kind="ExternalOutput").ap()
    scratch = {n: nc.dram_tensor("scratch_" + n, s, F32, kind="Internal").ap() for n, s in (
        ("start", (EDGES, HEADS)), ("row", (TOK, ROW)), ("adst", (TOK, HEADS)),
        ("sums", (EDGES, ACC)), ("carry", (P, ACC)))}
    scratch["sorted"] = nc.dram_tensor("scratch_sorted", (EDGES, 1), I32, kind="Internal").ap()
    program(nc, d, out, scratch, STAGES)
    r = run_bass_kernel_spmd(nc, [arrays], core_ids=[0])
    return r.results[0]["out"]
```
